# Optimizing a Trainium2 kernel written in Bass

```python
import numpy as np
import jax
import jax.numpy as jnp

def _softmax(x, axis=-1):
    return jax.nn.softmax(x, axis=axis)

def _gelu(x):
    return jax.nn.gelu(x, approximate=True)

def _silu(x):
    return jax.nn.silu(x)

def _sigmoid(x):
    return jax.nn.sigmoid(x)

def _layernorm(x, axis=-1, eps=1e-05):
    m = jnp.mean(x, axis=axis, keepdims=True)
    v = jnp.var(x, axis=axis, keepdims=True)
    return (x - m) / jnp.sqrt(v + eps)

def _scatter_add(tgt, idx, src, axis=0):
    return tgt.at[idx].add(src)

def _segment_sum(src, seg, n):
    return jax.ops.segment_sum(src, seg, n)
kernel_name = 'mk_adj_ffn_d2_adj_r2_88fa57'

def setup_inputs(seed: int=0):
    np.random.seed(seed)
    _w = jnp.asarray

    def _rec_inputs():
        import jax
        import jax.numpy as jnp
        _gk = jax.random.key(seed)
        x = 7.22e-05 + 1 * jax.random.normal(jax.random.fold_in(_gk, 1), (64, 128, 128), jnp.float32)
        _a = jax.random.bernoulli(jax.random.fold_in(_gk, 2), 0.015625, (128, 128))
        _a = jnp.logical_or(_a, jnp.eye(128, dtype=bool))
        adj = _a.astype(jnp.int32)
        return (x, adj)
    x, adj = _rec_inputs()

    def _L0_gnn_setup():
        import jax, jax.numpy as jnp
        import numpy as np
        B, N, D_IN, D_OUT, H = (64, 256, 128, 128, 4)
        HD = D_OUT // H
        key = jax.random.key(seed)
        ks = jax.random.split(key, 10)
        x = jax.random.normal(ks[0], (B, N, D_IN), dtype=jnp.float32)
        adj = jax.random.randint(ks[1], (N, N), 0, 2, dtype=jnp.int32)
        adj = adj.at[jnp.arange(N), jnp.arange(N)].set(1)
        s_in = 1.0 / np.sqrt(D_IN)
        s_out = 1.0 / np.sqrt(D_OUT)
        wq = jax.random.uniform(ks[2], (D_OUT, D_IN), jnp.float32, -s_in, s_in)
        bq = jax.random.uniform(ks[3], (D_OUT,), jnp.float32, -s_in, s_in)
        wk = jax.random.uniform(ks[4], (D_OUT, D_IN), jnp.float32, -s_in, s_in)
        bk = jax.random.uniform(ks[5], (D_OUT,), jnp.float32, -s_in, s_in)
        wv = jax.random.uniform(ks[6], (D_OUT, D_IN), jnp.float32, -s_in, s_in)
        bv = jax.random.uniform(ks[7], (D_OUT,), jnp.float32, -s_in, s_in)
        wo = jax.random.uniform(ks[8], (D_OUT, D_OUT), jnp.float32, -s_out, s_out)
        bo = jax.random.uniform(ks[9], (D_OUT,), jnp.float32, -s_out, s_out)
        return {'x': x, 'adj': adj, 'wq': wq, 'bq': bq, 'wk': wk, 'bk': bk, 'wv': wv, 'bv': bv, 'wo': wo, 'bo': bo}
    _L0_gnn_all = _L0_gnn_setup()
    _L0_gnn_in = {k: v for k, v in _L0_gnn_all.items() if k in ('wq', 'bq', 'wk', 'bk', 'wv', 'bv', 'wo', 'bo')}
    del _L0_gnn_all

    def _L0_ffn_setup():
        import jax, jax.numpy as jnp
        import numpy as np
        B, S, D, F, E, K = (8, 1024, 128, 512, 8, 2)
        key = jax.random.key(seed)
        ks = jax.random.split(key, 10)
        s = 0.02
        return {'x': jax.random.normal(ks[0], (B, S, D), dtype=jnp.float32), 'Wr': jax.random.normal(ks[1], (D, E), dtype=jnp.float32) * s, 'W1s': jax.random.normal(ks[2], (D, F), dtype=jnp.float32) * s, 'b1s': jnp.zeros((F,), dtype=jnp.float32), 'W2s': jax.random.normal(ks[3], (F, D), dtype=jnp.float32) * s, 'b2s': jnp.zeros((D,), dtype=jnp.float32), 'W1p': jax.random.normal(ks[4], (E, D, F), dtype=jnp.float32) * s, 'b1p': jnp.zeros((E, F), dtype=jnp.float32), 'W2p': jax.random.normal(ks[5], (E, F, D), dtype=jnp.float32) * s, 'b2p': jnp.zeros((E, D), dtype=jnp.float32)}
    _L0_ffn_all = _L0_ffn_setup()
    _L0_ffn_in = {k: v for k, v in _L0_ffn_all.items() if k in ('Wr', 'W1s', 'b1s', 'W2s', 'b2s', 'W1p', 'b1p', 'W2p', 'b2p')}
    del _L0_ffn_all

    def _L1_gnn_setup():
        import jax, jax.numpy as jnp
        import numpy as np
        EPS = 1e-05

        def _layernorm(x, g, b):
            mu = jnp.mean(x, axis=-1, keepdims=True)
            var = jnp.mean(jnp.square(x - mu), axis=-1, keepdims=True)
            return (x - mu) * jax.lax.rsqrt(var + EPS) * g + b
        key = jax.random.key(seed)
        ks = jax.random.split(key, 8)
        F, N, C, H = (2048, 64, 128, 8)
        x = jax.random.normal(ks[0], (F, N, C), dtype=jnp.float32)
        adj = jax.random.randint(ks[1], (N, N), 0, 2, dtype=jnp.int32)
        adj = jnp.maximum(adj, jnp.eye(N, dtype=jnp.int32))
        s = 1.0 / np.sqrt(C)
        w_qkv = jax.random.normal(ks[2], (C, 3 * C), dtype=jnp.float32) * s
        w1 = jax.random.normal(ks[3], (C, C), dtype=jnp.float32) * s
        b1 = jnp.zeros((C,), dtype=jnp.float32)
        w2 = jax.random.normal(ks[4], (C, C), dtype=jnp.float32) * s
        b2 = jnp.zeros((C,), dtype=jnp.float32)
        ln1_g = jnp.ones((C,), jnp.float32)
        ln1_b = jnp.zeros((C,), jnp.float32)
        ln2_g = jnp.ones((C,), jnp.float32)
        ln2_b = jnp.zeros((C,), jnp.float32)
        return {'x': x, 'adj': adj, 'w_qkv': w_qkv, 'ln1_g': ln1_g, 'ln1_b': ln1_b, 'ln2_g': ln2_g, 'ln2_b': ln2_b, 'w1': w1, 'b1': b1, 'w2': w2, 'b2': b2}
    _L1_gnn_all = _L1_gnn_setup()
    _L1_gnn_in = {k: v for k, v in _L1_gnn_all.items() if k in ('w_qkv', 'ln1_g', 'ln1_b', 'ln2_g', 'ln2_b', 'w1', 'b1', 'w2', 'b2')}
    del _L1_gnn_all

    def _L1_ffn_setup():
        import jax, jax.numpy as jnp
        import numpy as np
        B, S, D = (8, 2048, 128)
        H = 4 * D
        CAPACITY = 0.5
        key = jax.random.key(seed)
        ks = jax.random.split(key, 6)
        x = jax.random.normal(ks[0], (B, S, D), dtype=jnp.float32)
        attention_mask = jnp.zeros((B, 1, 1, S), dtype=jnp.float32)
        wr = jax.random.normal(ks[1], (D, 1), dtype=jnp.float32) * 0.02
        br = jnp.zeros((1,), dtype=jnp.float32)
        w1 = jax.random.normal(ks[2], (D, H), dtype=jnp.float32) * 0.02
        b1 = jnp.zeros((H,), dtype=jnp.float32)
        w2 = jax.random.normal(ks[3], (H, D), dtype=jnp.float32) * 0.02
        b2 = jnp.zeros((D,), dtype=jnp.float32)
        return {'x': x, 'attention_mask': attention_mask, 'wr': wr, 'br': br, 'w1': w1, 'b1': b1, 'w2': w2, 'b2': b2}
    _L1_ffn_all = _L1_ffn_setup()
    _L1_ffn_in = {k: v for k, v in _L1_ffn_all.items() if k in ('attention_mask', 'wr', 'br', 'w1', 'b1', 'w2', 'b2')}
    del _L1_ffn_all
    return {'x': x, 'adj': adj, 'L0_gnn_wq': _L0_gnn_in['wq'], 'L0_gnn_bq': _L0_gnn_in['bq'], 'L0_gnn_wk': _L0_gnn_in['wk'], 'L0_gnn_bk': _L0_gnn_in['bk'], 'L0_gnn_wv': _L0_gnn_in['wv'], 'L0_gnn_bv': _L0_gnn_in['bv'], 'L0_gnn_wo': _L0_gnn_in['wo'], 'L0_gnn_bo': _L0_gnn_in['bo'], 'L0_ffn_Wr': _L0_ffn_in['Wr'], 'L0_ffn_W1s': _L0_ffn_in['W1s'], 'L0_ffn_b1s': _L0_ffn_in['b1s'], 'L0_ffn_W2s': _L0_ffn_in['W2s'], 'L0_ffn_b2s': _L0_ffn_in['b2s'], 'L0_ffn_W1p': _L0_ffn_in['W1p'], 'L0_ffn_b1p': _L0_ffn_in['b1p'], 'L0_ffn_W2p': _L0_ffn_in['W2p'], 'L0_ffn_b2p': _L0_ffn_in['b2p'], 'L1_gnn_w_qkv': _L1_gnn_in['w_qkv'], 'L1_gnn_ln1_g': _L1_gnn_in['ln1_g'], 'L1_gnn_ln1_b': _L1_gnn_in['ln1_b'], 'L1_gnn_ln2_g': _L1_gnn_in['ln2_g'], 'L1_gnn_ln2_b': _L1_gnn_in['ln2_b'], 'L1_gnn_w1': _L1_gnn_in['w1'], 'L1_gnn_b1': _L1_gnn_in['b1'], 'L1_gnn_w2': _L1_gnn_in['w2'], 'L1_gnn_b2': _L1_gnn_in['b2'], 'L1_ffn_attention_mask': _L1_ffn_in['attention_mask'], 'L1_ffn_wr': _L1_ffn_in['wr'], 'L1_ffn_br': _L1_ffn_in['br'], 'L1_ffn_w1': _L1_ffn_in['w1'], 'L1_ffn_b1': _L1_ffn_in['b1'], 'L1_ffn_w2': _L1_ffn_in['w2'], 'L1_ffn_b2': _L1_ffn_in['b2']}

def reference(x, adj, L0_gnn_wq, L0_gnn_bq, L0_gnn_wk, L0_gnn_bk, L0_gnn_wv, L0_gnn_bv, L0_gnn_wo, L0_gnn_bo, L0_ffn_Wr, L0_ffn_W1s, L0_ffn_b1s, L0_ffn_W2s, L0_ffn_b2s, L0_ffn_W1p, L0_ffn_b1p, L0_ffn_W2p, L0_ffn_b2p, L1_gnn_w_qkv, L1_gnn_ln1_g, L1_gnn_ln1_b, L1_gnn_ln2_g, L1_gnn_ln2_b, L1_gnn_w1, L1_gnn_b1, L1_gnn_w2, L1_gnn_b2, L1_ffn_attention_mask, L1_ffn_wr, L1_ffn_br, L1_ffn_w1, L1_ffn_b1, L1_ffn_w2, L1_ffn_b2):
    import jax
    import jax.numpy as jnp

    def _L0_gnn_ref(x, adj, wq, bq, wk, bk, wv, bv, wo, bo):
        import jax, jax.numpy as jnp
        import numpy as np
        B, N, D_IN, D_OUT, H = (64, 256, 128, 128, 4)
        HD = D_OUT // H
        b, n, _ = x.shape
        q = (x @ wq.T + bq).reshape(b, n, H, HD).transpose(0, 2, 1, 3)
        k = (x @ wk.T + bk).reshape(b, n, H, HD).transpose(0, 2, 1, 3)
        v = (x @ wv.T + bv).reshape(b, n, H, HD).transpose(0, 2, 1, 3)
        scores = jnp.einsum('bhnd,bhmd->bhnm', q, k) / jnp.sqrt(jnp.float32(HD))
        scores = jnp.where(adj[None, None] == 0, -jnp.inf, scores)
        attn = jnp.nan_to_num(jax.nn.softmax(scores, axis=-1), nan=0.0)
        out = jnp.einsum('bhnm,bhmd->bhnd', attn, v)
        out = out.transpose(0, 2, 1, 3).reshape(b, n, D_OUT)
        return out @ wo.T + bo

    def _L0_ffn_ref(x, Wr, W1s, b1s, W2s, b2s, W1p, b1p, W2p, b2p):
        import jax, jax.numpy as jnp
        import numpy as np
        B, S, D, F, E, K = (8, 1024, 128, 512, 8, 2)
        gelu = lambda t: jax.nn.gelu(t, approximate=False)
        shared = gelu(x @ W1s + b1s) @ W2s + b2s
        rw = jax.nn.softmax(x @ Wr, axis=-1)
        topw, topi = jax.lax.top_k(rw, K)
        topw = topw / jnp.sum(topw, axis=-1, keepdims=True)
        mask = jnp.sum(jax.nn.one_hot(topi, E, dtype=topw.dtype) * topw[..., None], axis=-2)
        h = gelu(jnp.einsum('bsd,edf->bsef', x, W1p) + b1p)
        priv = jnp.einsum('bsef,efd->bsed', h, W2p) + b2p
        routed = jnp.einsum('bsed,bse->bsd', priv, mask)
        return shared + routed

    def _L1_gnn_ref(x, adj, w_qkv, ln1_g, ln1_b, ln2_g, ln2_b, w1, b1, w2, b2):
        import jax, jax.numpy as jnp
        import numpy as np
        EPS = 1e-05

        def _layernorm(x, g, b):
            mu = jnp.mean(x, axis=-1, keepdims=True)
            var = jnp.mean(jnp.square(x - mu), axis=-1, keepdims=True)
            return (x - mu) * jax.lax.rsqrt(var + EPS) * g + b
        F, N, C = x.shape
        H = 8
        D = C // H
        qkv = jnp.einsum('fnc,ck->fnk', x, w_qkv)
        q, k, v = jnp.split(qkv, 3, axis=-1)
        q = q.reshape(F, N, H, D)
        k = k.reshape(F, N, H, D)
        v = v.reshape(F, N, H, D)
        scores = jnp.einsum('fnhd,fmhd->fhnm', q, k) / jnp.sqrt(jnp.asarray(D, x.dtype))
        mask = (adj > 0)[None, None, :, :]
        scores = jnp.where(mask, scores, jnp.asarray(-1000000000.0, x.dtype))
        attn = jax.nn.softmax(scores, axis=-1)
        t = jnp.einsum('fhnm,fmhd->fnhd', attn, v).reshape(F, N, C)
        x = _layernorm(x + t, ln1_g, ln1_b)
        h = jax.nn.relu(jnp.einsum('fnc,cd->fnd', x, w1) + b1)
        f_out = jnp.einsum('fnd,dc->fnc', h, w2) + b2
        x = _layernorm(x + f_out, ln2_g, ln2_b)
        return x

    def _L1_ffn_ref(x, attention_mask, wr, br, w1, b1, w2, b2):
        import jax, jax.numpy as jnp
        import numpy as np
        B, S, D = (8, 2048, 128)
        H = 4 * D
        CAPACITY = 0.5
        b, s, d = x.shape
        weights = (jnp.einsum('bsd,do->bso', x, wr) + br)[..., 0]
        k = max(1, int(CAPACITY * s))
        kk = k - 1 if k > 1 else 1
        _, idx = jax.lax.top_k(weights, k)
        sel_idx = idx[:, :kk]
        sel = jnp.take_along_axis(x, sel_idx[:, :, None], axis=1)
        h = jax.nn.gelu(jnp.einsum('bkd,dh->bkh', sel, w1) + b1)
        y = jnp.einsum('bkh,hd->bkd', h, w2) + b2
        w_sel = jnp.take_along_axis(weights, sel_idx, axis=1)
        y = y * w_sel[..., None]
        batch_idx = jnp.arange(b)[:, None]
        processed = jnp.zeros_like(x).at[batch_idx, sel_idx].set(y)
        return processed + x
    x = x + _L0_gnn_ref(_layernorm(x, axis=-1), adj, L0_gnn_wq, L0_gnn_bq, L0_gnn_wk, L0_gnn_bk, L0_gnn_wv, L0_gnn_bv, L0_gnn_wo, L0_gnn_bo)
    x = x + _L0_ffn_ref(_layernorm(x, axis=-1), L0_ffn_Wr, L0_ffn_W1s, L0_ffn_b1s, L0_ffn_W2s, L0_ffn_b2s, L0_ffn_W1p, L0_ffn_b1p, L0_ffn_W2p, L0_ffn_b2p)
    x = x + _L1_gnn_ref(_layernorm(x, axis=-1), adj, L1_gnn_w_qkv, L1_gnn_ln1_g, L1_gnn_ln1_b, L1_gnn_ln2_g, L1_gnn_ln2_b, L1_gnn_w1, L1_gnn_b1, L1_gnn_w2, L1_gnn_b2)
    x = x + _L1_ffn_ref(_layernorm(x, axis=-1), L1_ffn_attention_mask, L1_ffn_wr, L1_ffn_br, L1_ffn_w1, L1_ffn_b1, L1_ffn_w2, L1_ffn_b2)
    return x

_drawn_inputs = setup_inputs


def setup_inputs(seed=0):
    import zlib

    import numpy as np

    out = dict(_drawn_inputs(seed))
    spreads = {'L0_ffn_b1s': (0.0, 0.334),
     'L0_ffn_b2s': (0.0, 0.1),
     'L0_ffn_b1p': (0.0, 0.457),
     'L0_ffn_b2p': (0.0, 0.1),
     'L1_gnn_ln1_g': (1.0, 0.2),
     'L1_gnn_ln1_b': (0.0, 0.1),
     'L1_gnn_ln2_g': (1.0, 0.2),
     'L1_gnn_ln2_b': (0.0, 0.1),
     'L1_gnn_b1': (0.0, 0.273),
     'L1_gnn_b2': (0.0, 0.1),
     'L1_ffn_b1': (0.0, 0.8),
     'L1_ffn_b2': (0.0, 0.8)}
    factors = {'L0_gnn_bq': 8.0, 'L0_gnn_bk': 8.0, 'L1_ffn_wr': 8.0, 'L1_ffn_w1': 8.0, 'L1_ffn_w2': 8.0}
    for name, (base, spread) in spreads.items():
        noise = np.random.default_rng([zlib.crc32(name.encode()), seed]).standard_normal(out[name].shape)
        drawn = base * np.exp(spread * noise) if base else spread * noise
        out[name] = jnp.asarray(drawn.astype(out[name].dtype))
    for name, factor in factors.items():
        out[name] = (out[name] * factor).astype(out[name].dtype)
    return out
```

```python
from contextlib import ExitStack

import numpy as np

import concourse.bass as bass
from concourse import mybir

P = 128
GRAPHS, PAIRS = 64, 32
HIDDEN = 512
CHUNKS = HIDDEN // P
EXPERTS = 8
SHARED, MOD = 8, 9
NETS = 10
TILE = 2 * P
SHARED_TILES = GRAPHS * P // TILE
ROUTED_TILES = 2 * SHARED_TILES + EXPERTS
ALL_TILES = SHARED_TILES + ROUTED_TILES
ROUTED_ROWS = ROUTED_TILES * TILE
HEADS_A, HEADS_C = 4, 8
WIDTH_A, WIDTH_C = P // HEADS_A, P // HEADS_C
KEPT = 63
SLOTS = 64
MOD_TILES = GRAPHS // 4
EPS = 1e-5
MASKED = -1e30
TAKEN = -3e38
WSCALE = 64.0
FIRST = 6

COL_BQ, COL_BK, COL_B1C = NETS * CHUNKS, NETS * CHUNKS + 1, NETS * CHUNKS + 2
COLS = NETS * CHUNKS + 3
(ROW_BV, ROW_BO, ROW_G1, ROW_B1, ROW_G2, ROW_B2, ROW_FB, ROW_WR, ROW_BR) = range(9)
ROW_NETS = 9
ROWS = ROW_NETS + NETS
MAT_Q, MAT_K, MAT_V, MAT_O, MAT_QKV, MAT_F1, MAT_F2, MAT_R = 0, 128, 256, 384, 512, 896, 1024, 1152
MATS = 1160
C_ID, C_TRI, C_ONE, C_IOTA = 0, 128, 256, 384
C_H4, C_H8, C_REV, C_THR, C_TIX = 512, 516, 524, 532, 596
CONSTS = 596 + ROUTED_TILES


def constants():
    c = np.zeros((P, CONSTS), np.float32)
    k = np.arange(P)
    c[:, C_ID:C_ID + P] = np.eye(P)
    c[:, C_TRI:C_TRI + P] = k[:, None] < k[None, :]
    c[:, C_ONE:C_ONE + P] = 1.0
    c[:, C_IOTA:C_IOTA + P] = k
    c[:, C_H4:C_H4 + 4] = k[:, None] // WIDTH_A == np.arange(4)
    c[:, C_H8:C_H8 + 8] = k[:, None] // WIDTH_C == np.arange(8)
    c[:, C_REV:C_REV + 8] = np.arange(8, 0, -1)
    c[:, C_THR:C_THR + 64] = TILE * np.arange(64)
    c[:, C_TIX:C_TIX + ROUTED_TILES] = np.arange(ROUTED_TILES)
    return c


def build(nc, x, adj, mats, cols, rows, w1, w2, consts, out):
    F32, F16, BF16, I32 = mybir.dt.float32, mybir.dt.float16, mybir.dt.bfloat16, mybir.dt.int32
    ACT, ALU, AX = mybir.ActivationFunctionType, mybir.AluOpType, mybir.AxisListType
    ctx = ExitStack()
    with ctx:
        def sb(name, shape, dt=F32):
            return ctx.enter_context(nc.sbuf_tensor(name, shape, dt))

        sems = {}

        def sem(name):
            if name not in sems:
                sems[name] = ctx.enter_context(nc.semaphore(name))
            return sems[name]

        def two(name, shape, dt=F32):
            return [sb(f"{name}{j}", shape, dt) for j in range(2)]

        def after(eng, s, n):
            if isinstance(n, int) and n <= 0:
                return
            eng.wait_ge(s, n)

        sorted_rows = nc.dram_tensor("sorted_rows", [ROUTED_ROWS, 2 * P], F16, kind="Internal").ap()
        results = nc.dram_tensor("results", [SHARED_TILES * TILE + ROUTED_ROWS, P], F32, kind="Internal").ap()

        X = sb("X", [P, PAIRS, 2, P])
        HL = sb("HL", [P, PAIRS, 2, 2, P], F16)
        WH = sb("WH", [P, NETS, 2, HIDDEN], F16)
        WL = sb("WL", [P, NETS, 2, HIDDEN], F16)
        MT = sb("MT", [P, MATS])
        CL = sb("CL", [P, COLS])
        RW = sb("RW", [P, ROWS, P])
        CN = sb("CN", [P, CONSTS])
        ADJ = sb("ADJ", [P, P], I32)
        ident16 = sb("ident16", [P, P], F16)
        identb = sb("identb", [P, P], BF16)
        mask0 = sb("mask0", [P, 4, P], BF16)
        mask1 = sb("mask1", [P, 4, P], BF16)
        has = sb("has", [P, 1])
        wscale = sb("wscale", [P, 1])
        zeros = sb("zeros", [P, 512])
        ADJF = sb("ADJF", [P, P])
        ADJN = sb("ADJN", [P, P])
        SHIFT = sb("SHIFT", [P, 2 * GRAPHS], I32)

        XN = two("XN", [P, 2, P])
        XNT = sb("XNT", [P, 2, P])
        QT = sb("QT", [P, 2, P])
        KT = sb("KT", [P, 2, P])
        KB = two("KB", [P, 1024])
        VA = two("VA", [P, 2, HEADS_A, WIDTH_A + 1])
        VC = two("VC", [P, 2, HEADS_C, WIDTH_C + 1])
        MX = sb("MX", [P, 8])
        PR = two("PR", [P, 8, P])
        PT = sb("PT", [P, 8, P])
        RS = sb("RS", [P, 8])
        ON = sb("ON", [P, 2, P])
        OT = sb("OT", [P, 2, P])
        HF = two("HF", [P, 2, P])
        HT = sb("HT", [P, 2, P])
        GROUPS = ("an", "c1", "c2")
        STATS = {t: sb("STATS_" + t, [P, 4, 6]) for t in GROUPS}
        MV = {t: sb("MV_" + t, [P, 4, 2]) for t in GROUPS}
        ROOT = {t: sb("ROOT_" + t, [P, 4]) for t in GROUPS}
        epsc = sb("epsc", [P, 1])
        LG = sb("LG", [P, GRAPHS, EXPERTS])
        WT = sb("WT", [P, 2, GRAPHS])
        SL = sb("SL", [P, GRAPHS, 2], I32)
        EID = sb("EID", [P, ROUTED_TILES], I32)
        WTOK = sb("WTOK", [P, GRAPHS])
        POS = sb("POS", [P, GRAPHS])

        XS = two("XS", [P, 2, 2, P], F16)
        XTS = two("XTS", [P, 2, TILE], F16)
        RAW = two("RAW", [P, CHUNKS, TILE])
        HH = two("HH", [P, CHUNKS, TILE], F16)
        HLO = two("HLO", [P, CHUNKS, TILE], F16)
        YS = two("YS", [P, 2, P])
        SG = [t[:, :, :, :].rearrange("p g a d -> p g (a d)") for t in XS]
        ISG = two("ISG", [P, 4], I32)
        PS = ctx.enter_context(nc.psum_tensor("PS", [P, 8, 512], F32))

        PRF = [t[:, :, :].rearrange("p b m -> p (b m)") for t in PR]
        OH1 = PRF[0][:, 0:512].rearrange("p (a e) -> p a e", e=EXPERTS)
        TMP = PRF[0][:, 512:1024].rearrange("p (a e) -> p a e", e=EXPERTS)
        OH2 = PRF[1][:, 0:512].rearrange("p (a e) -> p a e", e=EXPERTS)
        OH12 = PRF[1][:, 512:1024]
        WIDE = KB[0][:, 0:ROUTED_TILES * EXPERTS]
        KEY = sb("KEY", [P, GRAPHS])
        BEST = sb("BEST", [P, 2, GRAPHS])
        CNT = sb("CNT", [P, 4, EXPERTS])
        EIDF = sb("EIDF", [P, ROUTED_TILES])

        ident = CN[:, C_ID:C_ID + P]

        def bcast(ap, axis, n):
            a = ap.unsqueeze(axis)
            shape = list(a.shape)
            shape[axis] = n
            return a.broadcast_to(shape)

        def row(r):
            return RW[:, r, :]

        x_ld = [sem("x_ld0"), sem("x_ld1")]
        const_ld, cols_ld, rows_ld, mats_ld, adj_ld = (sem(n) for n in
            ("const_ld", "cols_ld", "rows_ld", "mats_ld", "adj_ld"))
        raw_ld = [sem("raw_ld0"), sem("raw_ld1")]
        zero_st = sem("zero_st")
        setup = sem("setup")
        spare_p = sem("spare_p")
        spare = sem("spare")
        out_st = [sem("out_st0"), sem("out_st1")]
        FIRST_X = 4
        SETUP = 8
        ZERO_ROWS = 4
        ZERO_STORES = ROUTED_ROWS // P // ZERO_ROWS
        CHUNK_STEPS = 2 * NETS

        def norm_stats(v, tag, n, sites):
            st, mv = STATS[tag], MV[tag]
            for place, src in sites:
                for g in range(2):
                    ins = v.bn_stats(st[:, 2 * place + g, :], src(g))
            ins.then_inc(sem(tag + "_stats"), 1)
            v.wait_ge(sem(tag + "_stats"), n).then_inc(spare, 1)
            for place, src in sites:
                for g in range(2):
                    ins = v.bn_aggr(mv[:, 2 * place + g, :], st[:, 2 * place + g, :])
            ins.then_inc(sem(tag + "_aggr"), 1)

        def norm_root(act, tag, n):
            act.wait_ge(sem(tag + "_aggr"), n)
            act.activation(ROOT[tag][:, :], MV[tag][:, :, 1], ACT.Ln, bias=epsc[:, 0:1]).then_inc(sem(tag + "_ln"), 1)
            act.wait_ge(sem(tag + "_ln"), n)
            act.activation(ROOT[tag][:, :], ROOT[tag][:, :], ACT.Exp, scale=-0.5).then_inc(sem(tag + "_root"), 1)

        def norm_apply(v, tag, n, place, src, dst, done, free=()):
            v.wait_ge(sem(tag + "_root"), n)
            for s, m in free:
                after(v, s, m)
            for g in range(2):
                q = 2 * place + g
                ins = v.tensor_scalar(dst(g), src(g), MV[tag][:, q, 0:1], ROOT[tag][:, q:q + 1],
                                      ALU.subtract, ALU.mult)
            ins.then_inc(done, 1)

        a_xnT, a_T, a_qk, a_v, a_S, a_PT, a_O, a_OT, a_wo, a_h0T, a_lg = (sem("a_" + n) for n in
            "xnT T qk v S PT O OT wo h0T lg".split())
        a_q, a_k, a_exp, a_pt, a_OTs, a_h0Ts = (sem("a_" + n) for n in "q k exp pt OTs h0Ts".split())
        a_xn, a_vs, a_max, a_sub, a_r, a_On, a_x1, a_h0, a_lgs = (sem("a_" + n) for n in
            "xn vs max sub r On x1 h0 lgs".split())
        a_kb, a_xb, a_hi, a_lo, prep_t, prep_hi, prep = (sem(n) for n in
            "a_kb a_xb a_hi a_lo prep_t prep_hi prep".split())
        LAST_A = PAIRS + 2

        def live(k, n=PAIRS):
            return not isinstance(k, int) or 0 <= k < n

        def pe_a(pe, i, j):
            if live(i):
                pe.wait_ge(a_xn, i + 1)
                after(pe, a_h0Ts, i - 3)
                for g in range(2):
                    ins = pe.transpose(PS[:, 0, g * P:(g + 1) * P], XN[j][:, g, :], ident)
                ins.then_inc(a_T, 1)
            k = i - 2
            if live(k):
                pe.wait_ge(a_On, k + 1)
                for g in range(2):
                    ins = pe.transpose(PS[:, 7, g * P:(g + 1) * P], ON[:, g, :], ident)
                ins.then_inc(a_OT, 1)
            if live(i):
                pe.wait_ge(a_xnT, i + 1)
                after(pe, a_k, i)
                xt = XNT[:, :, :].rearrange("p g n -> p (g n)")
                pe.matmul(PS[:, 1, 0:256], MT[:, MAT_Q:MAT_Q + P], xt, start=True, stop=True)
                pe.matmul(PS[:, 1, 256:512], MT[:, MAT_K:MAT_K + P], xt, start=True, stop=True).then_inc(a_qk, 1)
                after(pe, a_lgs, i - 3)
                for g in range(2):
                    ins = pe.matmul(PS[:, 2, g * P:(g + 1) * P], XNT[:, g, :], MT[:, MAT_V:MAT_V + P],
                                    start=True, stop=True)
                ins.then_inc(a_v, 1)
            if live(k):
                pe.wait_ge(a_OTs, k + 1)
                for g in range(2):
                    ins = pe.matmul(PS[:, 7, g * P:(g + 1) * P], OT[:, g, :], MT[:, MAT_O:MAT_O + P],
                                    start=True, stop=True)
                ins.then_inc(a_wo, 1)
            if live(i):
                pe.wait_ge(a_q, i + 1)
                pe.wait_ge(a_kb, i + 1)
                after(pe, a_sub, i)
                for g in range(2):
                    pe.matmul(PS[:, 3 + g, :], QT[:, g, :], KB[j][:, g * 512:(g + 1) * 512], start=True, stop=False)
                    ins = pe.matmul(PS[:, 3 + g, :], identb[:, :], mask0[:, :, :].rearrange("p h m -> p (h m)"),
                                    start=False, stop=True)
                ins.then_inc(a_S, 1)
            k = i - 3
            if live(k):
                pe.wait_ge(a_h0, k + 1)
                if live(i):
                    pe.wait_ge(a_xnT, i + 1)
                else:
                    after(pe, a_h0Ts, k)
                for g in range(2):
                    ins = pe.transpose(PS[:, 0, g * P:(g + 1) * P], HF[(j + 1) % 2][:, g, :], ident)
                ins.then_inc(a_h0T, 1)
            k = i - 1
            if live(k):
                pe.wait_ge(a_exp, k + 1)
                after(pe, a_pt, k)
                for b in range(8):
                    ins = pe.transpose(PS[:, 5 + b // 4, (b % 4) * P:(b % 4 + 1) * P], PR[(j + 1) % 2][:, b, :], ident)
                ins.then_inc(a_PT, 1)
            k = i - 3
            if live(k):
                pe.wait_ge(a_h0Ts, k + 1)
                after(pe, a_vs, i + 1 if live(i) else PAIRS)
                if not live(i):
                    after(pe, a_lgs, k)
                for g in range(2):
                    ins = pe.matmul(PS[:, 2, 256 + 8 * g:264 + 8 * g], HT[:, g, :], MT[:, MAT_R:MAT_R + 8],
                                    start=True, stop=True)
                ins.then_inc(a_lg, 1)
            k = i - 1
            if live(k):
                pe.wait_ge(a_pt, k + 1)
                pe.wait_ge(a_vs, k + 1)
                after(pe, a_x1, k)
                for b in range(8):
                    ins = pe.matmul(PS[:, 7, 33 * b:33 * b + 33], PT[:, b, :],
                                    VA[(j + 1) % 2][:, b // 4, b % 4, :], start=True, stop=True)
                ins.then_inc(a_O, 1)

        def act_a(act, i, j):
            if live(i):
                act.wait_ge(a_T, i + 1)
                act.activation(XNT[:, :, :].rearrange("p g n -> p (g n)"), PS[:, 0, 0:256], ACT.Copy).then_inc(a_xnT, 1)
            k = i - 2
            if live(k):
                act.wait_ge(a_OT, k + 1)
                act.activation(OT[:, :, :].rearrange("p g n -> p (g n)"), PS[:, 7, 0:256], ACT.Copy).then_inc(a_OTs, 1)
            if live(i):
                act.wait_ge(a_qk, i + 1)
                act.activation(QT[:, :, :].rearrange("p g n -> p (g n)"), PS[:, 1, 0:256], ACT.Identity,
                               bias=CL[:, COL_BQ:COL_BQ + 1]).then_inc(a_q, 1)
                after(act, a_kb, i)
                act.activation(KT[:, :, :].rearrange("p g n -> p (g n)"), PS[:, 1, 256:512], ACT.Identity,
                               bias=CL[:, COL_BK:COL_BK + 1]).then_inc(a_k, 1)
            k = i - 3
            if live(k):
                act.wait_ge(a_h0T, k + 1)
                act.activation(HT[:, :, :].rearrange("p g n -> p (g n)"), PS[:, 0, 0:256], ACT.Copy).then_inc(a_h0Ts, 1)
            if live(i - 2) or live(i + 1):
                norm_root(act, "an", i + 2)
            k = i - 1
            if live(k):
                act.wait_ge(a_PT, k + 1)
                act.activation(PT[:, :, :].rearrange("p b n -> p (b n)"),
                               PS[:, 5:7, :].rearrange("p b n -> p (b n)"), ACT.Copy).then_inc(a_pt, 1)
            if live(i):
                act.wait_ge(a_sub, i + 1)
                pr = PR[j][:, :, :].rearrange("p b n -> p (b n)")
                act.activation(pr, pr, ACT.Exp, scale=float(WIDTH_A) ** -0.5).then_inc(a_exp, 1)

        def x_site(i):
            return (0, lambda g: X[:, i, g, :])

        def h_site(k):
            return (1, lambda g: X[:, k, g, :])

        def normed_x(v, i, j):
            norm_apply(v, "an", i + 1, *x_site(i), lambda g: XN[j][:, g, :], a_xn, [(a_T, i - 1)])

        def dve_a(v, i, j):
            k = i - 2
            if live(k):
                v.wait_ge(a_O, k + 1)
                v.reciprocal(RS[:, :], PS[:, 7, 0:264].rearrange("p (b w) -> p b w", w=33)[:, :, 32]).then_inc(a_r, 1)
                v.wait_ge(a_r, k + 1)
                v.scalar_tensor_tensor(ON[:, :, :].rearrange("p g (h w) -> p (g h) w", w=32),
                                       PS[:, 7, 0:264].rearrange("p (b w) -> p b w", w=33)[:, :, 0:32],
                                       has[:, 0:1], bcast(RS[:, :], 2, 32), ALU.mult, ALU.mult).then_inc(a_On, 1)
            if live(i):
                v.wait_ge(a_v, i + 1)
                after(v, a_O, i - 1)
                v.tensor_tensor(VA[j][:, :, :, 0:32], PS[:, 2, 0:256].rearrange("p (g h w) -> p g h w", g=2, w=32),
                                bcast(row(ROW_BV).rearrange("p (h w) -> p h w", w=32), 1, 2), ALU.add).then_inc(a_vs, 1)
            if live(k):
                v.wait_ge(a_wo, k + 1)
                v.wait_ge(a_xb, k + 1)
                v.tensor_tensor(X[:, k, :, :], PS[:, 7, 0:256].rearrange("p (g d) -> p g d", g=2), X[:, k, :, :],
                                ALU.add).then_inc(a_x1, 1)
                v.wait_ge(a_x1, k + 1).then_inc(spare, 1)
            sites = [x_site(i + 1)] * live(i + 1) + [h_site(k)] * live(k)
            if sites:
                norm_stats(v, "an", i + 2, sites)
            if live(i):
                v.wait_ge(a_S, i + 1)
                v.tensor_reduce(MX[:, :], PS[:, 3:5, :].rearrange("p g (h m) -> p (g h) m", h=4), AX.X,
                                ALU.max).then_inc(a_max, 1)
                v.wait_ge(a_max, i + 1)
                after(v, a_PT, i - 1)
                v.tensor_tensor(PR[j][:, :, :], PS[:, 3:5, :].rearrange("p g (h m) -> p (g h) m", h=4),
                                bcast(MX[:, :], 2, P), ALU.subtract).then_inc(a_sub, 1)
            if live(i + 1):
                normed_x(v, i + 1, (j + 1) % 2)
            if live(k):
                norm_apply(v, "an", i + 2, *h_site(k), lambda g: HF[j][:, g, :], a_h0, [(a_h0T, k - 1), (a_lo, k - 1)])
            k = i - 3
            if live(k):
                v.wait_ge(a_lg, k + 1)
                v.tensor_copy(LG[:, :, :].rearrange("p (q g) e -> p q (g e)", g=2)[:, k, :],
                              PS[:, 2, 256:272]).then_inc(a_lgs, 1)

        def pool_a(pool, i, j, chunk):
            if live(i):
                pool.wait_ge(a_k, i + 1)
                after(pool, a_S, i - 1)
                for g in range(2):
                    ins = pool.tensor_tensor(KB[j][:, g * 512:(g + 1) * 512].rearrange("p (h m) -> p h m", h=4),
                                             bcast(KT[:, g, :], 1, 4), bcast(CN[:, C_H4:C_H4 + 4], 2, P), ALU.mult)
                ins.then_inc(a_kb, 1)
                pool.wait_ge(a_xn, i + 1)
                pool.tensor_tensor(X[:, i, :, :], X[:, i, :, :], bcast(row(ROW_BO), 1, 2), ALU.add).then_inc(a_xb, 1)
            if chunk:
                e = i // 2 if isinstance(i, int) else chunk_net[0]
                raw = RAW[j][:, :, :].rearrange("p c t -> p (c t)")[:, 0:HIDDEN]
                tmp = RAW[j][:, :, :].rearrange("p c t -> p (c t)")[:, HIDDEN:2 * HIDDEN]
                pool.wait_ge(raw_ld[j], 16 * (e + 1))
                pool.tensor_tensor(tmp, raw, wscale[:, 0:1].broadcast_to([P, HIDDEN]), ALU.mult).then_inc(prep_t, 1)
                pool.wait_ge(prep_t, i + 1).then_inc(spare_p, 1)
                pool.tensor_copy(WH[:, e, j, :], tmp).then_inc(prep_hi, 1)
                pool.wait_ge(prep_hi, i + 1)
                pool.tensor_tensor(WL[:, e, j, :], tmp, WH[:, e, j, :], ALU.subtract).then_inc(prep, 1)
            k = i - 3
            if live(k):
                jk = (j + 1) % 2
                pool.wait_ge(a_h0, k + 1).then_inc(spare_p, 1)
                pool.tensor_copy(HL[:, k, :, 0, :], HF[jk][:, :, :]).then_inc(a_hi, 1)
                pool.wait_ge(a_hi, k + 1)
                pool.tensor_tensor(HL[:, k, :, 1, :], HF[jk][:, :, :], HL[:, k, :, 0, :], ALU.subtract).then_inc(a_lo, 1)

        chunk_net = [None]

        class Net:
            def __init__(self, tag):
                (self.T, self.xT, self.h, self.g, self.hi, self.lo, self.y, self.ys) = (
                    sem(tag + n) for n in ("_T", "_xT", "_h", "_g", "_hi", "_lo", "_y", "_ys"))

        b, d = Net("b"), Net("d")

        def first_layer(pe, s, k, j, e):
            pe.wait_ge(s.xT, k + 1)
            for half in range(2):
                after(pe, s.g, 2 * k + half - 3)
                for c in (2 * half, 2 * half + 1):
                    dst = PS[:, 2 + 2 * j + half, (c % 2) * TILE:(c % 2 + 1) * TILE]
                    wh, wl = (w[:, e, 0, c * P:(c + 1) * P] for w in (WH, WL))
                    pe.matmul(dst, wh, XTS[j][:, 0, :], start=True, stop=False)
                    pe.matmul(dst, wh, XTS[j][:, 1, :], start=False, stop=False)
                    ins = pe.matmul(dst, wl, XTS[j][:, 0, :], start=False, stop=True)
                ins.then_inc(s.h, 1)

        def gelu(act, s, k, j, e, func):
            for half in range(2):
                act.wait_ge(s.h, 2 * k + half + 1)
                after(act, s.lo, 2 * k + half - 3)
                for c in (2 * half, 2 * half + 1):
                    ins = act.activation(RAW[j][:, c, :], PS[:, 2 + 2 * j + half, (c % 2) * TILE:(c % 2 + 1) * TILE],
                                         func, bias=CL[:, 0:NETS * CHUNKS].rearrange("p (e c) -> p e c", e=NETS)[:, e, c:c + 1],
                                         scale=1.0 / WSCALE)
                ins.then_inc(s.g, 1)

        def split(v, s, k, j):
            for half in range(2):
                cs = slice(2 * half, 2 * half + 2)
                v.wait_ge(s.g, 2 * k + half + 1)
                if half == 0:
                    after(v, s.y, k - 1)
                v.tensor_copy(HH[j][:, cs, :], RAW[j][:, cs, :]).then_inc(s.hi, 1)
                v.wait_ge(s.hi, 2 * k + half + 1)
                v.tensor_tensor(HLO[j][:, cs, :], RAW[j][:, cs, :], HH[j][:, cs, :], ALU.subtract).then_inc(s.lo, 1)

        def second_layer(pe, s, k, j, e, bank_free):
            pe.wait_ge(s.lo, 2 * k + 2)
            after(pe, *bank_free)
            for t in range(2):
                for c in range(CHUNKS):
                    hh, hl = (h[j][:, c, t * P:(t + 1) * P] for h in (HH, HLO))
                    wh, wl = (w[:, e, 1, c * P:(c + 1) * P] for w in (WH, WL))
                    dst = PS[:, 6 + j, t * P:(t + 1) * P]
                    pe.matmul(dst, hh, wh, start=c == 0, stop=False)
                    pe.matmul(dst, hh, wl, start=False, stop=False)
                    ins = pe.matmul(dst, hl, wh, start=False, stop=c == CHUNKS - 1)
            ins.then_inc(s.y, 1)

        xs_ld = [sem("xs_ld0"), sem("xs_ld1")]
        y_st = [sem("y_st0"), sem("y_st1")]
        sc_copy, sc_idx = sem("sc_copy"), sem("sc_idx")
        sc_done = [sem("sc_done0"), sem("sc_done1")]
        route = sem("route")
        r_slots, r_eid, r_cnt, r_diff, r_exp = (sem("r_" + n) for n in "slots eid cnt diff exp".split())
        r_oh = sem("r_oh")
        LAST_B = ALL_TILES + 1
        SPLIT_B = SHARED_TILES + 4

        def in_b(k):
            return not isinstance(k, int) or 0 <= k < ALL_TILES

        def is_shared(k, shared_loop):
            return k < SHARED_TILES if isinstance(k, int) else shared_loop

        def net_of(eng, k, shared_loop):
            if is_shared(k, shared_loop):
                return SHARED
            eng.wait_ge(r_eid, 1)
            return eng.value_load(EID[0:1, bass.ds(k - SHARED_TILES, 1)], min_val=0, max_val=EXPERTS - 1)

        def half_of(k, p, c):
            return k // 2 if isinstance(k, int) else p + c // 2

        def pe_b(pe, t, j, p, shared):
            if in_b(t):
                after(pe, b.xT, t - 1)
                if is_shared(t, shared):
                    src = HL[:, t, :, :, :]
                else:
                    src = XS[j]
                    pe.wait_ge(xs_ld[j], 16 * (half_of(t, p, j) + 1 - SHARED_TILES // 2))
                dst = PS[:, j, :].bitcast(F16)
                for hl in range(2):
                    for g in range(2):
                        ins = pe.transpose(dst[:, hl * TILE + g * P:hl * TILE + (g + 1) * P], src[:, g, hl, :], ident16[:, :])
                ins.then_inc(b.T, 1)
            k = t - 1
            if in_b(k):
                first_layer(pe, b, k, (j + 1) % 2, net_of(pe, k, shared))
            k = t - 2
            if in_b(k):
                second_layer(pe, b, k, j, net_of(pe, k, shared), (b.ys, k - 1))

        def act_b(act, t, j, p, shared):
            if in_b(t):
                act.wait_ge(b.T, t + 1)
                after(act, b.h, 2 * t - 2)
                act.activation(XTS[j][:, :, :].rearrange("p a b -> p (a b)"), PS[:, j, :].bitcast(F16)[:, 0:2 * TILE],
                               ACT.Copy).then_inc(b.xT, 1)
            k = t - 1
            if in_b(k):
                gelu(act, b, k, (j + 1) % 2, net_of(act, k, shared), ACT.Gelu)

        def dve_b(v, t, j, p, shared):
            k = t - 1
            if in_b(k):
                split(v, b, k, (j + 1) % 2)
            k = t - 2
            if in_b(k):
                e = net_of(v, k, shared)
                v.wait_ge(b.y, k + 1)
                after(v, y_st[j], 16 * half_of(k - 2, p, j - 4) + 16)
                v.scalar_tensor_tensor(YS[j][:, :, :], PS[:, 6 + j, 0:256].rearrange("p (g d) -> p g d", g=2),
                                       1.0 / WSCALE, bcast(RW[:, ROW_NETS + e, :], 1, 2) if isinstance(e, int) else
                                       bcast(RW[:, ROW_NETS:ROWS, :][:, e, :], 1, 2), ALU.mult, ALU.add).then_inc(b.ys, 1)

        def sp_b(sp, t, j, p, shared):
            k = t + 1
            if in_b(k) and not is_shared(k, shared):
                jk = (j + 1) % 2
                if isinstance(k, int) and k == SHARED_TILES:
                    for s in sc_done:
                        sp.wait_ge(s, 64 * PAIRS // 2)
                if not isinstance(k, int) or k - 2 >= SHARED_TILES:
                    sp.wait_ge(b.T, k - 1)
                r = (k - SHARED_TILES) * TILE
                sp.dma_start(XS[jk][:, :, :, :].rearrange("p g a d -> p g (a d)"),
                             sorted_rows[bass.ds(r, TILE), :].rearrange("(g p) d -> p g d", p=P)).then_inc(xs_ld[jk], 16)
            k = t - 2
            if in_b(k):
                sp.wait_ge(b.ys, k + 1)
                sp.dma_start(results[bass.ds(k * TILE, TILE), :].rearrange("(g p) d -> p g d", p=P),
                             YS[j][:, :, :]).then_inc(y_st[j], 16)

        def run_b(eng, fn):
            for t in range(FIRST):
                fn(eng, t, t % 2, None, True)
            with eng.Fori(FIRST // 2, SHARED_TILES // 2 - 1) as p:
                for j in range(2):
                    fn(eng, p * 2 + j, j, p, True)
            for t in range(SHARED_TILES - 2, SPLIT_B):
                fn(eng, t, t % 2, None, True)
            with eng.Fori(SPLIT_B // 2, ALL_TILES // 2 - 1) as p:
                for j in range(2):
                    fn(eng, p * 2 + j, j, p, False)
            for t in range(ALL_TILES - 2, LAST_B + 1):
                fn(eng, t, t % 2, None, False)

        c_T, c_aT, c_qk, c_v, c_w1, c_F, c_S, c_PT, c_O = (sem("c_" + n) for n in "T aT qk v w1 F S PT O".split())
        c_zT, c_aTs, c_q, c_k, c_relu, c_pt, c_exp = (sem("c_" + n) for n in "zT aTs q k relu pt exp".split())
        c_x2a, c_x2b, c_x2, c_z, c_vs, c_max, c_sub, c_r, c_On, c_s1, c_n1, c_s2, c_n2, c_x3, c_u, c_uw, c_xu = (
            sem("c_" + n) for n in "x2a x2b x2 z vs max sub r On s1 n1 s2 n2 x3 u uw xu".split())
        c_kb, c_ag, c_a, c_ab, c_cg, c_c, c_hi, c_lo, c_um = (sem("c_" + n) for n in "kb ag a ab cg c hi lo um".split())
        g_idx = sem("g_idx")
        g_ld = [sem("g_ld0"), sem("g_ld1")]
        ysh_ld = [sem("ysh_ld0"), sem("ysh_ld1")]
        LAST_C = PAIRS + 4
        GY = two("GY", [P, 4, P])
        YSH = YS
        S1 = sb("S1", [P, 2, P])
        A1 = two("A1", [P, 2, P])
        AB = two("AB", [P, 2, P])
        S2 = sb("S2", [P, 2, P])
        C2 = two("C2", [P, 2, P])
        HR = sb("HR", [P, 2 * P])
        UM = sb("UM", [P, 2, P])
        AT = HT

        def flat(t):
            return t.rearrange("p a b -> p (a b)")

        def scores_c(pe, i, j, u, g):
            if g == 0:
                pe.wait_ge(c_q, i + 1)
            pe.wait_ge(c_kb, u + 1)
            after(pe, c_sub, u)
            for h in range(2):
                pe.matmul(PS[:, 3 + h, :], QT[:, g, :], KB[g][:, h * 512:(h + 1) * 512], start=True, stop=False)
                ins = pe.matmul(PS[:, 3 + h, :], identb[:, :], mask1[:, :, :].rearrange("p h m -> p (h m)"),
                                start=False, stop=True)
            ins.then_inc(c_S, 1)

        def transposed_c(pe, u, g):
            pe.wait_ge(c_exp, u + 1)
            after(pe, c_pt, u)
            for h in range(8):
                ins = pe.transpose(PS[:, 5 + h // 4, (h % 4) * P:(h % 4 + 1) * P], PR[g][:, h, :], ident)
            ins.then_inc(c_PT, 1)

        def pv_c(pe, u, g, jv):
            pe.wait_ge(c_pt, u + 1)
            after(pe, c_On, u)
            for h in range(8):
                ins = pe.matmul(PS[:, 7, 17 * h:17 * h + 17], PT[:, h, :], VC[jv][:, g, h, :], start=True, stop=True)
            ins.then_inc(c_O, 1)

        def pe_c(pe, i, j):
            jj = (j + 1) % 2
            if live(i):
                pe.wait_ge(c_z, i + 1)
                after(pe, c_relu, i - 2)
                for g in range(2):
                    ins = pe.transpose(PS[:, 0, g * P:(g + 1) * P], XN[j][:, g, :], ident)
                ins.then_inc(c_T, 1)
                pe.wait_ge(c_zT, i + 1)
                after(pe, c_k, i)
                pe.matmul(PS[:, 1, 0:256], MT[:, MAT_QKV:MAT_QKV + P], flat(XNT[:, :, :]), start=True, stop=True)
                pe.matmul(PS[:, 1, 256:512], MT[:, MAT_QKV + P:MAT_QKV + 2 * P], flat(XNT[:, :, :]),
                          start=True, stop=True).then_inc(c_qk, 1)
                after(pe, c_s2, i - 2)
                for g in range(2):
                    ins = pe.matmul(PS[:, 2, g * P:(g + 1) * P], XNT[:, g, :], MT[:, MAT_QKV + 2 * P:MAT_QKV + 3 * P],
                                    start=True, stop=True)
                ins.then_inc(c_v, 1)
            k = i - 2
            if live(k):
                pe.wait_ge(c_a, k + 1)
                if not live(i):
                    after(pe, c_relu, k)
                for g in range(2):
                    ins = pe.transpose(PS[:, 0, g * P:(g + 1) * P], A1[j][:, g, :], ident)
                ins.then_inc(c_aT, 1)
            if live(i):
                scores_c(pe, i, j, 2 * i, 0)
            if live(k):
                pe.wait_ge(c_aTs, k + 1)
                pe.matmul(PS[:, 0, 0:256], MT[:, MAT_F1:MAT_F1 + P], flat(AT[:, :, :]), start=True, stop=True).then_inc(c_w1, 1)
            if live(i - 1):
                transposed_c(pe, 2 * i - 1, 1)
                pv_c(pe, 2 * i - 1, 1, jj)
            if live(k):
                pe.wait_ge(c_relu, k + 1)
                after(pe, c_vs, i + 1 if live(i) else PAIRS)
                if not live(i):
                    after(pe, c_s2, k)
                for g in range(2):
                    ins = pe.matmul(PS[:, 2, g * P:(g + 1) * P], HR[:, g * P:(g + 1) * P], MT[:, MAT_F2:MAT_F2 + P],
                                    start=True, stop=True)
                ins.then_inc(c_F, 1)
            if live(i):
                scores_c(pe, i, j, 2 * i + 1, 1)
                transposed_c(pe, 2 * i, 0)
                pe.wait_ge(c_vs, i + 1)
                pv_c(pe, 2 * i, 0, j)

        def pt_evac_c(act, u):
            act.wait_ge(c_PT, u + 1)
            act.activation(flat(PT[:, :, :]), flat(PS[:, 5:7, :]), ACT.Copy).then_inc(c_pt, 1)

        def exp_c(act, u, g):
            act.wait_ge(c_sub, u + 1)
            act.activation(flat(PR[g][:, :, :]), flat(PR[g][:, :, :]), ACT.Exp, scale=float(WIDTH_C) ** -0.5).then_inc(c_exp, 1)

        def act_c(act, i, j):
            if live(i):
                act.wait_ge(c_T, i + 1)
                act.activation(flat(XNT[:, :, :]), PS[:, 0, 0:256], ACT.Copy).then_inc(c_zT, 1)
                act.wait_ge(c_qk, i + 1)
                act.activation(flat(QT[:, :, :]), PS[:, 1, 0:256], ACT.Copy).then_inc(c_q, 1)
                after(act, c_kb, 2 * i)
                act.activation(flat(KT[:, :, :]), PS[:, 1, 256:512], ACT.Copy).then_inc(c_k, 1)
            if live(i + 1) or live(i - 4):
                norm_root(act, "c1", i + 2)
            k = i - 2
            if live(k):
                act.wait_ge(c_aT, k + 1)
                act.activation(flat(AT[:, :, :]), PS[:, 0, 0:256], ACT.Copy).then_inc(c_aTs, 1)
                act.wait_ge(c_w1, k + 1)
                act.activation(HR[:, :], PS[:, 0, 0:256], ACT.Relu, bias=CL[:, COL_B1C:COL_B1C + 1]).then_inc(c_relu, 1)
            if live(i - 1):
                pt_evac_c(act, 2 * i - 1)
            if live(i):
                exp_c(act, 2 * i, 0)
            if live(i - 1) or live(i - 2):
                norm_root(act, "c2", i)
            if live(i):
                pt_evac_c(act, 2 * i)
                exp_c(act, 2 * i + 1, 1)

        def softmax_c(v, u, g):
            ss = PS[:, 3:5, :].rearrange("p g (h m) -> p (g h) m", h=4)
            v.wait_ge(c_S, u + 1)
            v.tensor_reduce(MX[:, :], ss, AX.X, ALU.max).then_inc(c_max, 1)
            v.wait_ge(c_max, u + 1)
            after(v, c_PT, u - 1)
            v.tensor_tensor(PR[g][:, :, :], ss, bcast(MX[:, :], 2, P), ALU.subtract).then_inc(c_sub, 1)

        def normalise_c(v, u, g):
            o = PS[:, 7, 0:136].rearrange("p (h w) -> p h w", w=17)
            v.wait_ge(c_O, u + 1)
            v.reciprocal(RS[:, :], o[:, :, 16]).then_inc(c_r, 1)
            v.wait_ge(c_r, u + 1)
            v.tensor_tensor(ON[:, g, :].rearrange("p (h w) -> p h w", w=16), o[:, :, 0:16],
                            bcast(RS[:, :], 2, 16), ALU.mult).then_inc(c_On, 1)

        def combined_x(v, i, j, p, c):
            v.wait_ge(ysh_ld[j], 16 * (half_of(i, p, c) + 1))
            v.tensor_tensor(X[:, i, :, :], X[:, i, :, :], YSH[j][:, :, :], ALU.add).then_inc(c_x2a, 1)
            v.wait_ge(g_ld[j], 64 * (half_of(i, p, c) + 1))
            for choice, before, done in ((0, c_x2a, c_x2b), (1, c_x2b, c_x2)):
                v.wait_ge(before, i + 1)
                for g in range(2):
                    w = WT[:, choice, :].rearrange("p (q g) -> p q g", g=2)[:, i, g:g + 1]
                    ins = v.scalar_tensor_tensor(X[:, i, g, :], GY[j][:, 2 * g + choice, :], w, X[:, i, g, :],
                                                 ALU.mult, ALU.add)
                ins.then_inc(done, 1)
            v.wait_ge(c_x2, i + 1).then_inc(spare, 1)

        def normed_z(v, i, j):
            norm_apply(v, "c1", i + 1, *x_site(i), lambda g: XN[j][:, g, :], c_z, [(c_T, i - 1), (c_s1, i - 1)])

        s1_site = (0, lambda g: S1[:, g, :])
        s2_site = (1, lambda g: S2[:, g, :])

        def dve_c(v, i, j, p=None):
            jj = (j + 1) % 2
            if live(i - 1):
                normalise_c(v, 2 * i - 2, 0)
            if live(i):
                v.wait_ge(c_v, i + 1)
                after(v, c_O, 2 * i - 2)
                v.tensor_copy(VC[j][:, :, :, 0:16], PS[:, 2, 0:256].rearrange("p (g h w) -> p g h w", g=2, w=16)).then_inc(c_vs, 1)
            if live(i + 1):
                combined_x(v, i + 1, jj, p, j + 1)
            ku = i - 4
            if live(ku):
                v.wait_ge(c_c, ku + 1)
                v.tensor_tensor(X[:, ku, :, :], X[:, ku, :, :], C2[j][:, :, :], ALU.add).then_inc(c_x3, 1)
                v.wait_ge(c_x3, ku + 1).then_inc(spare, 1)
            sites = [x_site(i + 1)] * live(i + 1) + [h_site(ku)] * live(ku)
            if sites:
                norm_stats(v, "c1", i + 2, sites)
            if live(i):
                softmax_c(v, 2 * i, 0)
            if live(ku):
                norm_apply(v, "c1", i + 2, *h_site(ku), lambda g: HF[j][:, g, :], c_u, [(c_lo, ku - 1), (c_um, ku - 1)])
                v.wait_ge(c_u, ku + 1)
                v.tensor_tensor(X[:, ku, :, :], X[:, ku, :, :], HF[j][:, :, :], ALU.add).then_inc(c_xu, 1)
            k1, k2 = i - 1, i - 2
            if live(k1):
                normalise_c(v, 2 * i - 1, 1)
                v.wait_ge(c_On, 2 * k1 + 2)
                v.tensor_tensor(S1[:, :, :], XN[jj][:, :, :], ON[:, :, :], ALU.add).then_inc(c_s1, 1)
            if live(i + 1):
                normed_z(v, i + 1, jj)
            if live(k2):
                v.wait_ge(c_F, k2 + 1)
                v.wait_ge(c_ab, k2 + 1)
                v.tensor_tensor(S2[:, :, :], PS[:, 2, 0:256].rearrange("p (g d) -> p g d", g=2), AB[j][:, :, :],
                                ALU.add).then_inc(c_s2, 1)
            if live(k1):
                v.wait_ge(c_s1, k1 + 1).then_inc(spare, 1)
            if live(k2):
                v.wait_ge(c_s2, k2 + 1).then_inc(spare, 1)
            sites = [s1_site] * live(k1) + [s2_site] * live(k2)
            if sites:
                norm_stats(v, "c2", i, sites)
            if live(i):
                softmax_c(v, 2 * i + 1, 1)
            if live(k1):
                norm_apply(v, "c2", i, *s1_site, lambda g: A1[jj][:, g, :], c_n1, [(c_aT, k1 - 1), (c_ab, k1 - 1)])
            if live(k2):
                norm_apply(v, "c2", i, *s2_site, lambda g: C2[j][:, g, :], c_n2, [(c_x3, k2 - 1)])
            k = i - 5
            if live(k):
                v.wait_ge(c_um, k + 1)
                v.tensor_reduce(WTOK[:, :].rearrange("p (q g) -> p q g", g=2)[:, k, :], UM[:, :, :], AX.X,
                                ALU.add).then_inc(c_uw, 1)

        def gather_c(pool, i, j, p, c):
            if not isinstance(i, int) or i > 1:
                pool.wait_ge(c_x2, i - 1).then_inc(spare_p, 1)
            pool.tensor_copy(ISG[j][:, :], SL[:, :, :].rearrange("p (q g) k -> p q (g k)", g=2)[:, i, :]).then_inc(g_idx, 1)
            for q in range(4):
                if q == 0:
                    pool.wait_ge(g_idx, i + 1).then_inc(spare_p, 1)
                pool.indirect_dma_start(out=GY[j][:, q, :], out_offset=None, in_=results[:, :],
                                        in_offset=bass.IndirectOffsetOnAxis(ap=ISG[j][:, q:q + 1], axis=0)).then_inc(g_ld[j], 16)

        def pool_c(pool, i, j, p=None):
            jj = (j + 1) % 2
            k = i - 2
            if live(k):
                pool.wait_ge(c_n1, k + 1)
                pool.tensor_tensor(A1[j][:, :, :], A1[j][:, :, :], bcast(row(ROW_G1), 1, 2), ALU.mult).then_inc(c_ag, 1)
                pool.wait_ge(c_ag, k + 1)
                pool.tensor_tensor(A1[j][:, :, :], A1[j][:, :, :], bcast(row(ROW_B1), 1, 2), ALU.add).then_inc(c_a, 1)
                pool.wait_ge(c_a, k + 1)
                after(pool, c_s2, k - 1)
                pool.tensor_tensor(AB[j][:, :, :], A1[j][:, :, :], bcast(row(ROW_FB), 1, 2), ALU.add).then_inc(c_ab, 1)
            if live(i):
                for g in range(2):
                    if g == 0:
                        pool.wait_ge(c_k, i + 1)
                    after(pool, c_S, 2 * i + g - 1)
                    pool.tensor_tensor(KB[g][:, :].rearrange("p (h m) -> p h m", h=8), bcast(KT[:, g, :], 1, 8),
                                       bcast(CN[:, C_H8:C_H8 + 8], 2, P), ALU.mult).then_inc(c_kb, 1)
            k = i - 3
            if live(k):
                pool.wait_ge(c_n2, k + 1)
                pool.tensor_tensor(C2[jj][:, :, :], C2[jj][:, :, :], bcast(row(ROW_G2), 1, 2), ALU.mult).then_inc(c_cg, 1)
                pool.wait_ge(c_cg, k + 1)
                pool.tensor_tensor(C2[jj][:, :, :], C2[jj][:, :, :], bcast(row(ROW_B2), 1, 2), ALU.add).then_inc(c_c, 1)
            if live(i + 2):
                gather_c(pool, i + 2, j, p, j + 2)
            k = i - 4
            if live(k):
                pool.wait_ge(c_u, k + 1)
                after(pool, c_uw, k)
                pool.tensor_tensor(UM[:, :, :], HF[j][:, :, :], bcast(row(ROW_WR), 1, 2), ALU.mult).then_inc(c_um, 1)
                pool.tensor_copy(HL[:, k, :, 0, :], HF[j][:, :, :]).then_inc(c_hi, 1)
                pool.wait_ge(c_hi, k + 1)
                pool.tensor_tensor(HL[:, k, :, 1, :], HF[j][:, :, :], HL[:, k, :, 0, :], ALU.subtract).then_inc(c_lo, 1)

        def sp_c(sp, i, j, p=None):
            if live(i):
                after(sp, c_x2a, i - 1)
                sp.dma_start(YSH[j][:, :, :], results[bass.ds(i * TILE, TILE), :].rearrange("(g p) d -> p g d", p=P)
                             ).then_inc(ysh_ld[j], 16)

        d_rank, d_oh, d_OT, d_OTs, d_yh, d_yf, d_yl, d_Z, d_o, d_wt, d_wg, d_pt = (
            sem("d_" + n) for n in "rank oh OT OTs yh yf yl Z o wt wg pt".split())
        LAST_D = MOD_TILES + 2
        PR16 = [t.bitcast(F16) for t in PRF]
        OH = [t[:, 0:512].rearrange("p (g s) -> p g s", g=4) for t in PR16]
        OHT = [t[:, 512:1024].rearrange("p (g s) -> p g s", g=4) for t in PR16]
        YH = [t[:, 1024:1280].rearrange("p (g d) -> p g d", g=2) for t in PR16]
        YL = [t[:, 1280:1536].rearrange("p (g d) -> p g d", g=2) for t in PR16]
        OUT = GY
        YF = A1
        IOTAM = sb("IOTAM", [P, P])
        WG, WK, SEL, CAND, PLACE = (KB[0][0:GRAPHS, n * P:(n + 1) * P] for n in range(5))
        TOP = sb("TOP", [GRAPHS, 8])
        KMAX = sb("KMAX", [GRAPHS, 1])

        def in_d(k):
            return not isinstance(k, int) or 0 <= k < MOD_TILES

        def u_parts(t, g, hl):
            return HL[:, :, :, :, :].rearrange("p (t q) g a d -> p t (q g) a d", q=2)[:, t, g, hl, :]

        def pe_d(pe, t, j):
            if in_d(t):
                if isinstance(t, int) and t == 0:
                    pe.wait_ge(c_lo, PAIRS)
                pe.wait_ge(d_oh, t + 1)
                after(pe, d_OTs, t - 1)
                for hl in range(2):
                    for g in range(4):
                        o = g % 2 * SLOTS
                        ins = pe.matmul(PS[:, j, hl * TILE + g * SLOTS:hl * TILE + (g + 1) * SLOTS], u_parts(t, g, hl),
                                        OH[j][:, g, o:o + SLOTS], start=True, stop=True)
                ins.then_inc(d.T, 1)
            k, jj = t - 1, (j + 1) % 2
            if in_d(k):
                first_layer(pe, d, k, jj, MOD)
                dst = PS[:, jj, :].bitcast(F16)
                for g in range(4):
                    ins = pe.transpose(dst[:, g * P:(g + 1) * P], OH[jj][:, g, :], ident16[:, :])
                ins.then_inc(d_OT, 1)
            k = t - 2
            if in_d(k):
                second_layer(pe, d, k, j, MOD, (d_o, k - 1))
            k = t - 3
            if in_d(k):
                pe.wait_ge(d_yl, k + 1)
                pe.wait_ge(d_OTs, k + 1)
                for g in range(4):
                    dst = PS[:, 6 + jj, g * P:(g + 1) * P]
                    pe.matmul(dst, OHT[jj][:, g, :], YH[jj][:, g // 2, :], start=True, stop=False)
                    ins = pe.matmul(dst, OHT[jj][:, g, :], YL[jj][:, g // 2, :], start=False, stop=True)
                ins.then_inc(d_Z, 1)

        def act_d(act, t, j):
            jj = (j + 1) % 2
            if in_d(t):
                act.wait_ge(d.T, t + 1)
                after(act, d.h, 2 * t - 2)
                act.activation(flat(XTS[j][:, :, :]), PS[:, j, :], ACT.Copy).then_inc(d.xT, 1)
            k = t - 1
            if in_d(k):
                gelu(act, d, k, jj, MOD, ACT.Gelu_apprx_tanh)
                act.wait_ge(d_OT, k + 1)
                after(act, d_Z, k - 1)
                act.activation(flat(OHT[jj][:, :, :]), PS[:, jj, :].bitcast(F16)[:, 0:512], ACT.Copy).then_inc(d_OTs, 1)

        def one_hots(v, t, j):
            after(v, d_OT, t - 1)
            for g in range(4):
                col = POS[:, :].rearrange("p (t g) -> p t g", g=4)[:, t, g:g + 1]
                table = IOTAM[:, :] if g % 2 else CN[:, C_IOTA:C_IOTA + P]
                ins = v.tensor_scalar(OH[j][:, g, :], table, col, None, ALU.is_equal)
            ins.then_inc(d_oh, 1)

        def dve_d(v, t, j, p=None):
            jj = (j + 1) % 2
            if in_d(t + 1):
                one_hots(v, t + 1, jj)
            k = t - 1
            if in_d(k):
                split(v, d, k, jj)
            k = t - 2
            if in_d(k):
                v.wait_ge(d.y, k + 1)
                v.scalar_tensor_tensor(YF[j][:, :, :], PS[:, 6 + j, 0:256].rearrange("p (g d) -> p g d", g=2),
                                       1.0 / WSCALE, bcast(row(ROW_NETS + MOD), 1, 2), ALU.mult, ALU.add).then_inc(d_yf, 1)
                v.wait_ge(d_yf, k + 1)
                after(v, d_Z, k - 1)
                v.tensor_copy(YH[j][:, :, :], YF[j][:, :, :]).then_inc(d_yh, 1)
                v.wait_ge(d_yh, k + 1)
                v.tensor_tensor(YL[j][:, :, :], YF[j][:, :, :], YH[j][:, :, :], ALU.subtract).then_inc(d_yl, 1)
            k = t - 3
            if in_d(k):
                v.wait_ge(d_Z, k + 1)
                after(v, out_st[jj], 16 * half_of(k - 2, p, j - 5) + 16)
                for g in range(4):
                    w = WTOK[:, :].rearrange("p (t g) -> p t g", g=4)[:, k, g:g + 1]
                    xk = X[:, :, :, :].rearrange("p (t q) g d -> p t (q g) d", q=2)[:, k, g, :]
                    ins = v.scalar_tensor_tensor(OUT[jj][:, g, :], PS[:, 6 + jj, g * P:(g + 1) * P], w, xk,
                                                 ALU.mult, ALU.add)
                ins.then_inc(d_o, 1)

        def sp_d(sp, t, j, p=None):
            k, jj = t - 3, (j + 1) % 2
            if in_d(k):
                sp.wait_ge(d_o, k + 1)
                sp.dma_start(out[bass.ds(4 * k, 4), :, :].rearrange("g p d -> p g d"), OUT[jj][:, :, :]).then_inc(out_st[jj], 16)

        def run(eng, fn, last, end, start=FIRST):
            for i in range(start):
                fn(eng, i, i % 2)
            with eng.Fori(start // 2, end // 2) as p:
                for j in range(2):
                    fn(eng, p * 2 + j, j)
            for i in range(end, last + 1):
                fn(eng, i, i % 2)

        def run_p(eng, fn, last, end, start=FIRST):
            for i in range(start):
                fn(eng, i, i % 2, None)
            with eng.Fori(start // 2, end // 2) as p:
                for j in range(2):
                    fn(eng, p * 2 + j, j, p)
            for i in range(end, last + 1):
                fn(eng, i, i % 2, None)

        block = ctx.enter_context(nc.Block())

        @block.sync
        def _(sp):
            sp.dma_start(CN[:, :], consts).then_inc(const_ld, 16)
            xv = x.rearrange("(q g) p d -> p q g d", g=2)
            sp.dma_start(X[:, 0:FIRST_X, :, :], xv[:, 0:FIRST_X, :, :]).then_inc(x_ld[0], 16)
            sp.dma_start(MT[:, :], mats).then_inc(mats_ld, 16)
            sp.dma_start(CL[:, :], cols).then_inc(cols_ld, 16)
            sp.dma_start(ADJ[:, :], adj).then_inc(adj_ld, 16)
            sp.dma_start(RW[:, :, :].rearrange("p r d -> p (r d)"),
                         rows.rearrange("(a r) d -> a (r d)", a=1).broadcast_to([P, ROWS * P])).then_inc(rows_ld, 16)
            sp.dma_start(X[:, FIRST_X:PAIRS, :, :], xv[:, FIRST_X:PAIRS, :, :]).then_inc(x_ld[1], 16)

            def raw_load(i, e, k):
                after(sp, prep, i - 1)
                dst = RAW[k][:, :, :].rearrange("p c t -> p (c t)")[:, 0:HIDDEN]
                if k == 0:
                    sp.dma_start(dst, w1[e, :, :]).then_inc(raw_ld[k], 16)
                else:
                    sp.dma_start(dst.rearrange("p (c d) -> p c d", c=CHUNKS),
                                 w2[e, :, :].rearrange("(c p) d -> p c d", p=P)).then_inc(raw_ld[k], 16)

            raw_load(0, 0, 0)
            raw_load(1, 0, 1)
            with sp.Fori(1, NETS) as e:
                for k in range(2):
                    raw_load(e * 2 + k, e, k)
            sp.wait_ge(setup, 1)
            with sp.Fori(0, ZERO_STORES) as q:
                sp.dma_start(sorted_rows[bass.ds(q * (ZERO_ROWS * P), ZERO_ROWS * P), :].rearrange("(p a) d -> p (a d)", p=P),
                             zeros[:, :].bitcast(F16)).then_inc(zero_st, 16)
            run_b(sp, sp_b)
            for j in range(2):
                sp.wait_ge(y_st[j], 16 * ALL_TILES // 2)
            run_p(sp, sp_c, PAIRS - 1, PAIRS)
            run_p(sp, sp_d, LAST_D, MOD_TILES)
            for j in range(2):
                sp.wait_ge(out_st[j], 16 * MOD_TILES // 2)

        @block.gpsimd
        def _(pool):
            pool.memset(wscale[:, :], WSCALE)
            pool.memset(epsc[:, :], EPS)
            for t in GROUPS:
                pool.memset(MV[t][:, :, :], 1.0)
            for j in range(2):
                pool.memset(VA[j][:, :, :, WIDTH_A:WIDTH_A + 1], 1.0)
                ins = pool.memset(VC[j][:, :, :, WIDTH_C:WIDTH_C + 1], 1.0)
            ins.then_inc(sem("pool_setup"), 1)
            pool.wait_ge(sem("pool_setup"), 1)
            pool.wait_ge(const_ld, 16)
            pool.wait_ge(rows_ld, 16)
            for i in range(FIRST):
                pool_a(pool, i, i % 2, True)
            with pool.Fori(FIRST // 2, NETS) as p:
                for j in range(2):
                    chunk_net[0] = p
                    pool_a(pool, p * 2 + j, j, True)
            with pool.Fori(NETS, PAIRS // 2) as p:
                for j in range(2):
                    pool_a(pool, p * 2 + j, j, False)
            for i in range(PAIRS, LAST_A + 1):
                pool_a(pool, i, i % 2, False)

            pool.wait_ge(r_slots, 2)
            pool.wait_ge(zero_st, 16 * ZERO_STORES)
            pool.wait_ge(a_lo, PAIRS)

            def scatter(q, j, p):
                if p is not None:
                    pool.wait_ge(sc_done[j], 64 * p).then_inc(spare_p, 1)
                pool.tensor_copy(SG[j][:, :, :].bitcast(I32), HL[:, q, :, :, :].rearrange("p g a d -> p g (a d)").bitcast(I32)
                                 ).then_inc(sc_copy, 1)
                pool.tensor_copy(ISG[j][:, :], SL[:, :, :].rearrange("p (q g) k -> p q (g k)", g=2)[:, q, :]).then_inc(sc_idx, 1)
                pool.wait_ge(sc_copy, q + 1).then_inc(spare_p, 1)
                pool.wait_ge(sc_idx, q + 1).then_inc(spare_p, 1)
                for n in range(4):
                    pool.indirect_dma_start(out=sorted_rows[:, :],
                                            out_offset=bass.IndirectOffsetOnAxis(ap=ISG[j][:, n:n + 1], axis=0),
                                            in_=SG[j][:, n // 2, :], in_offset=None).then_inc(sc_done[j], 16)

            for q in range(2):
                scatter(q, q, None)
            with pool.Fori(1, PAIRS // 2) as p:
                for j in range(2):
                    scatter(p * 2 + j, j, p)

            for j in range(2):
                pool.wait_ge(sc_done[j], 64 * PAIRS // 2)
            pool.tensor_tensor(flat(SL[:, :, :]), flat(SL[:, :, :]), SHIFT[:, :], ALU.add).then_inc(sem("shifted"), 1)
            pool.wait_ge(sem("shifted"), 1)
            for j in range(2):
                pool.wait_ge(y_st[j], 16 * ALL_TILES // 2)
            pool.wait_ge(b.T, ALL_TILES)
            gather_c(pool, 0, 0, None, 0)
            gather_c(pool, 1, 1, None, 0)
            run_p(pool, pool_c, LAST_C, PAIRS - 2)

        @block.scalar
        def _(act):
            act.wait_ge(cols_ld, 16)
            act.wait_ge(sem("pool_setup"), 1)
            norm_root(act, "an", 1)
            run(act, act_a, LAST_A, PAIRS)
            act.wait_ge(r_diff, 1)
            act.activation(WT[:, 1, :], WT[:, 0, :], ACT.Exp).then_inc(r_exp, 1)
            run_b(act, act_b)
            norm_root(act, "c1", 1)
            run(act, act_c, LAST_C, PAIRS - 2)
            act.wait_ge(d_wt, 1)
            act.activation(WG, PS[0:GRAPHS, 0, 0:P], ACT.Copy).then_inc(d_wg, 1)
            run(act, act_d, LAST_D, MOD_TILES)

        @block.tensor
        def _(pe):
            pe.wait_ge(const_ld, 16)
            pe.wait_ge(mats_ld, 16)
            pe.wait_ge(setup, SETUP)
            run(pe, pe_a, LAST_A, PAIRS)
            pe.wait_ge(r_oh, 1)
            oh = OH12[:, :]
            pe.matmul(PS[:, 3, :], CN[:, C_TRI:C_TRI + P], oh, start=True, stop=True)
            pe.matmul(PS[:, 4, :], CN[:, C_ONE:C_ONE + P], oh, start=True, stop=True).then_inc(r_cnt, 1)
            pe.wait_ge(prep, CHUNK_STEPS)
            pe.wait_ge(a_lo, PAIRS)
            pe.wait_ge(a_h0Ts, PAIRS)
            pe.wait_ge(a_lgs, PAIRS)
            pe.wait_ge(a_x1, PAIRS)
            pe.wait_ge(r_slots, 1)
            run_b(pe, pe_b)
            pe.wait_ge(b.ys, ALL_TILES)
            run(pe, pe_c, LAST_C, PAIRS)
            pe.wait_ge(c_uw, PAIRS + 1)
            pe.wait_ge(c_s2, PAIRS)
            pe.transpose(PS[0:GRAPHS, 0, 0:P], WTOK[:, :], ident).then_inc(d_wt, 1)
            pe.wait_ge(d_rank, 1)
            pe.transpose(PS[:, 1, 0:GRAPHS], PLACE, CN[0:GRAPHS, C_ID:C_ID + GRAPHS]).then_inc(d_pt, 1)
            run(pe, pe_d, LAST_D, MOD_TILES)

        @block.vector
        def _(v):
            one = [0]

            def then(ins):
                one[0] += 1
                ins.then_inc(route, 1)
                v.wait_ge(route, one[0])

            v.memset(zeros[:, :], 0.0).then_inc(setup, 1)
            v.wait_ge(const_ld, 16)
            v.wait_ge(adj_ld, 16)
            v.tensor_copy(ident16[:, :], ident).then_inc(setup, 1)
            v.tensor_copy(identb[:, :], ident).then_inc(setup, 1)
            then(v.tensor_copy(ADJF[:, :], ADJ[:, :]))
            v.tensor_scalar(mask0[:, :, :], bcast(ADJF[:, :], 1, 4), 0.0, MASKED, ALU.is_equal, ALU.mult).then_inc(setup, 1)
            v.tensor_scalar(mask1[:, :, :], bcast(ADJF[:, :], 1, 4), 0.0, MASKED, ALU.is_le, ALU.mult).then_inc(setup, 1)
            v.tensor_scalar(IOTAM[:, :], CN[:, C_IOTA:C_IOTA + P], float(SLOTS), None, ALU.subtract).then_inc(setup, 1)
            then(v.tensor_scalar(ADJN[:, :], ADJF[:, :], 0.0, None, ALU.not_equal))
            v.tensor_reduce(has[:, :], ADJN[:, :], AX.X, ALU.max).then_inc(setup, 1)
            v.memset(SHIFT[:, :], SHARED_TILES * TILE).then_inc(setup, 1)
            v.wait_ge(x_ld[0], 16)
            v.wait_ge(rows_ld, 16)
            v.wait_ge(setup, SETUP)
            v.wait_ge(sem("pool_setup"), 1)
            norm_stats(v, "an", 1, [x_site(0)])
            normed_x(v, 0, 0)
            for i in range(FIRST):
                if i == FIRST_X - 2:
                    v.wait_ge(x_ld[1], 16)
                dve_a(v, i, i % 2)
            with v.Fori(FIRST // 2, PAIRS // 2 - 1) as p:
                for j in range(2):
                    dve_a(v, p * 2 + j, j)
            for i in range(PAIRS - 2, LAST_A + 1):
                dve_a(v, i, i % 2)

            v.wait_ge(a_lgs, PAIRS)
            rev = CN[:, C_REV:C_REV + 8]
            G64 = GRAPHS

            def pick(logits, best, onehot):
                then(v.tensor_reduce(best, logits, AX.X, ALU.max))
                then(v.tensor_tensor(TMP[:, :, :], logits, bcast(best, 2, 8), ALU.is_equal))
                then(v.tensor_tensor(TMP[:, :, :], TMP[:, :, :], bcast(rev, 1, G64), ALU.mult))
                then(v.tensor_reduce(KEY[:, :], TMP[:, :, :], AX.X, ALU.max))
                then(v.tensor_tensor(onehot, bcast(rev, 1, G64), bcast(KEY[:, :], 2, 8), ALU.is_equal))

            pick(LG[:, :, :], BEST[:, 0, :], OH1[:, :, :])
            then(v.scalar_tensor_tensor(LG[:, :, :], OH1[:, :, :], MASKED, LG[:, :, :], ALU.mult, ALU.add))
            pick(LG[:, :, :], BEST[:, 1, :], OH2[:, :, :])
            v.tensor_tensor(OH12[:, :], OH1[:, :, :].rearrange("p a e -> p (a e)"),
                            OH2[:, :, :].rearrange("p a e -> p (a e)"), ALU.add).then_inc(r_oh, 1)
            v.tensor_tensor(WT[:, 0, :], BEST[:, 1, :], BEST[:, 0, :], ALU.subtract).then_inc(r_diff, 1)
            v.wait_ge(r_exp, 1)
            then(v.tensor_scalar(BEST[:, 0, :], WT[:, 1, :], 1.0, None, ALU.add))
            then(v.reciprocal(WT[:, 0, :], BEST[:, 0, :]))
            then(v.tensor_tensor(WT[:, 1, :], WT[:, 1, :], WT[:, 0, :], ALU.mult))
            v.wait_ge(r_cnt, 1)
            then(v.tensor_copy(LG[:, :, :].rearrange("p a e -> p (a e)"), PS[:, 4, :]))
            for e in range(EXPERTS):
                then(v.tensor_tensor_scan(TMP[:, :, e], LG[:, :, e], zeros[:, 0:G64], 0.0, ALU.add, ALU.add))
            then(v.tensor_copy(CNT[:, 0, :], TMP[:, G64 - 1, :]))
            then(v.tensor_tensor(LG[:, :, :], TMP[:, :, :], LG[:, :, :], ALU.subtract))
            then(v.tensor_tensor(LG[:, :, :], PS[:, 3, :].rearrange("p (a e) -> p a e", e=8), LG[:, :, :], ALU.add))
            then(v.tensor_tensor(TMP[:, :, :].rearrange("p a e -> p (a e)").rearrange("p (e a) -> p e a", e=8),
                                 bcast(CNT[:, 0, :], 2, 64), bcast(CN[:, C_THR:C_THR + 64], 1, 8), ALU.is_gt))
            then(v.tensor_reduce(CNT[:, 1, :], TMP[:, :, :].rearrange("p a e -> p (a e)").rearrange("p (e a) -> p e a", e=8),
                                 AX.X, ALU.add))
            then(v.tensor_tensor_scan(CNT[:, 2, :], CNT[:, 1, :], zeros[:, 0:8], 0.0, ALU.add, ALU.add))
            then(v.tensor_tensor(CNT[:, 3, :], CNT[:, 2, :], CNT[:, 1, :], ALU.subtract))
            then(v.tensor_scalar(CNT[:, 3, :], CNT[:, 3, :], float(TILE), None, ALU.mult))
            then(v.tensor_tensor(LG[:, :, :], LG[:, :, :], bcast(CNT[:, 3, :], 1, G64), ALU.add))
            for k, oh in enumerate((OH1, OH2)):
                then(v.tensor_tensor(TMP[:, :, :], LG[:, :, :], oh[:, :, :], ALU.mult))
                then(v.tensor_reduce(KEY[:, :], TMP[:, :, :], AX.X, ALU.add))
                v.tensor_copy(SL[:, :, k], KEY[:, :]).then_inc(r_slots, 1)
                v.wait_ge(r_slots, k + 1)
            big = WIDE[:, :].rearrange("p (t e) -> p t e", e=8)
            then(v.tensor_tensor(big, bcast(CNT[:, 2, :], 1, ROUTED_TILES),
                                 bcast(CN[:, C_TIX:C_TIX + ROUTED_TILES], 2, 8), ALU.is_le))
            then(v.tensor_reduce(EIDF[:, :], big, AX.X, ALU.add))
            v.tensor_scalar(EID[:, :], EIDF[:, :], float(EXPERTS - 1), None, ALU.min).then_inc(r_eid, 1)

            run_b(v, dve_b)

            combined_x(v, 0, 0, None, 0)
            norm_stats(v, "c1", 1, [x_site(0)])
            normed_z(v, 0, 0)
            for i in range(FIRST):
                dve_c(v, i, i % 2)
            with v.Fori(FIRST // 2, PAIRS // 2 - 1) as p:
                for j in range(2):
                    dve_c(v, p * 2 + j, j, p)
            for i in range(PAIRS - 2, LAST_C + 1):
                dve_c(v, i, i % 2)

            v.wait_ge(c_uw, PAIRS)
            v.tensor_scalar(WTOK[:, :], WTOK[:, :], row(ROW_BR)[:, 0:1], None, ALU.add).then_inc(c_uw, 1)
            v.wait_ge(d_wg, 1)
            then(v.tensor_copy(WK, WG))
            for r in range(8):
                then(v.max(TOP[:, :], WK))
                then(v.match_replace(WK, TOP[:, :], WK, TAKEN))
            then(v.tensor_scalar(SEL, WK, TAKEN / 3, None, ALU.is_lt))
            then(v.tensor_scalar(CAND, WG, TOP[:, 7:8], None, ALU.is_equal))
            then(v.tensor_tensor(CAND, CAND, SEL, ALU.mult))
            then(v.scalar_tensor_tensor(CAND, CN[0:GRAPHS, C_IOTA:C_IOTA + P], 1.0, CAND, ALU.add, ALU.mult))
            then(v.tensor_reduce(KMAX[:, :], CAND, AX.X, ALU.max))
            then(v.tensor_scalar(CAND, CAND, KMAX[:, 0:1], None, ALU.is_equal))
            then(v.tensor_tensor(SEL, SEL, CAND, ALU.subtract))
            then(v.tensor_tensor_scan(CAND, SEL, zeros[0:GRAPHS, 0:P], 0.0, ALU.add, ALU.add))
            then(v.scalar_tensor_tensor(CAND, SEL, 1000.0, CAND, ALU.mult, ALU.add))
            v.tensor_scalar(PLACE, CAND, 1001.0, None, ALU.subtract).then_inc(d_rank, 1)
            v.wait_ge(d_pt, 1)
            then(v.tensor_copy(POS[:, :], PS[:, 1, 0:GRAPHS]))
            one_hots(v, 0, 0)
            for t in range(FIRST):
                dve_d(v, t, t % 2)
            with v.Fori(FIRST // 2, MOD_TILES // 2 - 1) as p:
                for j in range(2):
                    dve_d(v, p * 2 + j, j, p)
            for t in range(MOD_TILES - 2, LAST_D + 1):
                dve_d(v, t, t % 2)


def kernel(x, adj, **p):
    import concourse.bacc as bacc
    from concourse.bass_utils import run_bass_kernel_spmd

    def a(name):
        return np.asarray(p[name])

    f32 = np.float32
    net_w1 = np.concatenate([a("L0_ffn_W1p"), a("L0_ffn_W1s")[None], a("L1_ffn_w1")[None]])
    net_w2 = np.concatenate([a("L0_ffn_W2p"), a("L0_ffn_W2s")[None], a("L1_ffn_w2")[None]])
    net_b1 = np.concatenate([a("L0_ffn_b1p"), a("L0_ffn_b1s")[None], a("L1_ffn_b1")[None]])
    net_b2 = np.concatenate([a("L0_ffn_b2p"), a("L0_ffn_b2s")[None], a("L1_ffn_b2")[None]])
    cols = np.concatenate([net_b1.reshape(-1, P), a("L0_gnn_bq")[None], a("L0_gnn_bk")[None],
                           a("L1_gnn_b1")[None]]).T
    rows = np.concatenate([np.stack([a("L0_gnn_bv"), a("L0_gnn_bo"), a("L1_gnn_ln1_g"), a("L1_gnn_ln1_b"),
                                     a("L1_gnn_ln2_g"), a("L1_gnn_ln2_b"), a("L1_gnn_b2"),
                                     a("L1_ffn_wr")[:, 0], np.repeat(a("L1_ffn_br"), P)]), net_b2])
    mats = np.concatenate([a("L0_gnn_wq").T, a("L0_gnn_wk").T, a("L0_gnn_wv").T, a("L0_gnn_wo").T,
                           a("L1_gnn_w_qkv"), a("L1_gnn_w1"), a("L1_gnn_w2"), a("L0_ffn_Wr")], axis=1)
    arrays = {"x": np.asarray(x), "adj": np.asarray(adj), "mats": mats, "cols": cols, "rows": rows,
              "w1": net_w1, "w2": net_w2, "consts": constants()}
    arrays = {k: np.ascontiguousarray(v) for k, v in arrays.items()}
    nc = bacc.Bacc("TRN2", target_bir_lowering=False, num_devices=1)
    aps = [nc.dram_tensor(k, v.shape, mybir.dt.from_np(v.dtype), kind="ExternalInput").ap() for k, v in arrays.items()]
    out = nc.dram_tensor("out", (GRAPHS, P, P), mybir.dt.float32, kind="ExternalOutput").ap()
    names = list(arrays)
    by = dict(zip(names, aps))
    build(nc, by["x"], by["adj"], by["mats"], by["cols"], by["rows"], by["w1"], by["w2"], by["consts"], out)
    r = run_bass_kernel_spmd(nc, [arrays], core_ids=[0])
    return r.results[0]["out"]
```

```python
from contextlib import ExitStack

import numpy as np

import concourse.bass as bass
from concourse import mybir

P = 128
GRAPHS, PAIRS = 64, 32
HIDDEN = 512
CHUNKS = HIDDEN // P
EXPERTS = 8
SHARED, MOD = 8, 9
NETS = 10
TILE = 2 * P
SHARED_TILES = GRAPHS * P // TILE
ROUTED_TILES = 2 * SHARED_TILES + EXPERTS
ALL_TILES = SHARED_TILES + ROUTED_TILES
ROUTED_ROWS = ROUTED_TILES * TILE
HEADS_A, HEADS_C = 4, 8
WIDTH_A, WIDTH_C = P // HEADS_A, P // HEADS_C
KEPT = 63
SLOTS = 64
MOD_TILES = GRAPHS // 4
EPS = 1e-5
MASKED = -1e30
TAKEN = -3e38
WSCALE = 64.0
FIRST = 8

COL_BQ, COL_BK, COL_B1C = NETS * CHUNKS, NETS * CHUNKS + 1, NETS * CHUNKS + 2
COLS = NETS * CHUNKS + 3
(ROW_BV, ROW_BO, ROW_G1, ROW_B1, ROW_G2, ROW_B2, ROW_FB, ROW_WR, ROW_BR) = range(9)
ROW_NETS = 9
ROWS = ROW_NETS + NETS
MAT_Q, MAT_K, MAT_V, MAT_O, MAT_QKV, MAT_F1, MAT_F2, MAT_R = 0, 128, 256, 384, 512, 896, 1024, 1152
MATS = 1160
C_ID, C_TRI, C_ONE, C_IOTA = 0, 128, 256, 384
C_H4, C_H8, C_REV, C_THR, C_TIX = 512, 516, 524, 532, 596
CONSTS = 596 + ROUTED_TILES


def constants():
    c = np.zeros((P, CONSTS), np.float32)
    k = np.arange(P)
    c[:, C_ID:C_ID + P] = np.eye(P)
    c[:, C_TRI:C_TRI + P] = k[:, None] < k[None, :]
    c[:, C_ONE:C_ONE + P] = 1.0
    c[:, C_IOTA:C_IOTA + P] = k
    c[:, C_H4:C_H4 + 4] = k[:, None] // WIDTH_A == np.arange(4)
    c[:, C_H8:C_H8 + 8] = k[:, None] // WIDTH_C == np.arange(8)
    c[:, C_REV:C_REV + 8] = np.arange(8, 0, -1)
    c[:, C_THR:C_THR + 64] = TILE * np.arange(64)
    c[:, C_TIX:C_TIX + ROUTED_TILES] = np.arange(ROUTED_TILES)
    return c


EXP_AND_LN = "natural_log_exp_and_others"


def build(nc, x, adj, mats, cols, rows, w1, w2, consts, out):
    F32, F16, BF16, I32 = mybir.dt.float32, mybir.dt.float16, mybir.dt.bfloat16, mybir.dt.int32
    ACT, ALU, AX = mybir.ActivationFunctionType, mybir.AluOpType, mybir.AxisListType
    ctx = ExitStack()
    with ctx:
        def sb(name, shape, dt=F32):
            return ctx.enter_context(nc.sbuf_tensor(name, shape, dt))

        sems = {}

        def sem(name):
            if name not in sems:
                sems[name] = ctx.enter_context(nc.semaphore(name))
            return sems[name]

        def two(name, shape, dt=F32):
            return [sb(f"{name}{j}", shape, dt) for j in range(2)]

        def after(eng, s, n):
            if isinstance(n, int) and n <= 0:
                return
            eng.wait_ge(s, n)

        sorted_rows = nc.dram_tensor("sorted_rows", [ROUTED_ROWS, 2 * P], F16, kind="Internal").ap()
        results = nc.dram_tensor("results", [ROUTED_ROWS, P], F32, kind="Internal").ap()

        X = sb("X", [P, PAIRS, 2, P])
        HL = sb("HL", [P, PAIRS, 2, 2, P], F16)
        WH = sb("WH", [P, NETS, 2, HIDDEN], F16)
        WL = sb("WL", [P, NETS, 2, HIDDEN], F16)
        MT = sb("MT", [P, MATS])
        CL = sb("CL", [P, COLS])
        RW = sb("RW", [P, ROWS, P])
        CN = sb("CN", [P, CONSTS])
        ADJ = sb("ADJ", [P, P], I32)
        ident16 = sb("ident16", [P, P], F16)
        identb = sb("identb", [P, P], BF16)
        mask0 = sb("mask0", [P, 4, P], BF16)
        mask1 = sb("mask1", [P, 4, P], BF16)
        has = sb("has", [P, 1])
        wscale = sb("wscale", [P, 1])
        zeros = sb("zeros", [P, 512])
        ADJF = sb("ADJF", [P, P])
        ADJN = sb("ADJN", [P, P])

        XN = two("XN", [P, 2, P])
        XNT = sb("XNT", [P, 2, P])
        QT = sb("QT", [P, 2, P])
        KBC = sb("KB", [P, 2, 1024])
        KB = [KBC[:, j, :] for j in range(2)]
        VA = two("VA", [P, 2, HEADS_A, WIDTH_A + 1])
        VC = two("VC", [P, 2, HEADS_C, WIDTH_C + 1])
        MX = sb("MX", [P, 8])
        PR = two("PR", [P, 8, P])
        PT = sb("PT", [P, 8, P])
        RS = sb("RS", [P, 8])
        ON = sb("ON", [P, 2, P])
        OT = sb("OT", [P, 2, P])
        HF = two("HF", [P, 2, P])
        HT = sb("HT", [P, 2, P])
        STATS, MV, ROOT = ([two(name + str(n), [P, 2] + w) for n in range(4)]
                           for name, w in (("STATS", [6]), ("MV", [2]), ("ROOT", [1])))
        epsc = sb("epsc", [P, 1])
        LG = sb("LG", [P, GRAPHS, EXPERTS])
        WT = sb("WT", [P, 2, GRAPHS])
        SL = sb("SL", [P, GRAPHS, 2], I32)
        EID = sb("EID", [P, ROUTED_TILES], I32)
        WTOK = sb("WTOK", [P, GRAPHS])
        POS = sb("POS", [P, GRAPHS])

        XS = two("XS", [P, 2, 2, P], F16)
        XTS = two("XTS", [P, 2, TILE], F16)
        RAW = two("RAW", [P, CHUNKS, TILE])
        HH = two("HH", [P, CHUNKS, TILE], F16)
        HLO = two("HLO", [P, CHUNKS, TILE], F16)
        YS = two("YS", [P, 2, P])
        SG = [t[:, :, :, :].rearrange("p g a d -> p g (a d)") for t in XS]
        ISG = two("ISG", [P, 4], I32)
        PS = ctx.enter_context(nc.psum_tensor("PS", [P, 8, 512], F32))

        PRF = [t[:, :, :].rearrange("p b m -> p (b m)") for t in PR]
        OH1 = PRF[0][:, 0:512].rearrange("p (a e) -> p a e", e=EXPERTS)
        TMP = PRF[0][:, 512:1024].rearrange("p (a e) -> p a e", e=EXPERTS)
        OH2 = PRF[1][:, 0:512].rearrange("p (a e) -> p a e", e=EXPERTS)
        OH12 = PRF[1][:, 512:1024]
        WIDE = KB[0][:, 0:ROUTED_TILES * EXPERTS]
        KEY = sb("KEY", [P, GRAPHS])
        BEST = sb("BEST", [P, 2, GRAPHS])
        CNT = sb("CNT", [P, 4, EXPERTS])
        EIDF = sb("EIDF", [P, ROUTED_TILES])

        ident = CN[:, C_ID:C_ID + P]

        def bcast(ap, axis, n):
            a = ap.unsqueeze(axis)
            shape = list(a.shape)
            shape[axis] = n
            return a.broadcast_to(shape)

        def row(r):
            return RW[:, r, :]

        x_ld = [sem("x_ld0"), sem("x_ld1")]
        const_ld, params_ld, rows_ld = sem("const_ld"), sem("params_ld"), sem("rows_ld")
        raw_ld = [sem("raw_ld0"), sem("raw_ld1")]
        zero_st = sem("zero_st")
        setup = sem("setup")
        pool_ready = sem("pool_ready")
        spare = sem("spare")
        out_st = [sem("out_st0"), sem("out_st1")]
        FIRST_X = 4
        SETUP = 7
        ZERO_ROWS = 4
        ZERO_STORES = ROUTED_ROWS // P // ZERO_ROWS
        CHUNK_STEPS = 2 * NETS

        def live(k, n=PAIRS):
            return not isinstance(k, int) or 0 <= k < n

        def at(stage, eng, i, j, lag, n=PAIRS):
            if live(i - lag, n):
                stage(eng, i - lag, (j + lag) % 2)

        def straight(eng, s, n):
            if isinstance(n, int):
                after(eng, s, n)

        def upto(n, last=PAIRS):
            return min(n, last) if isinstance(n, int) else n

        class Norm:

            def __init__(self, tag, place, src, before=0):
                self.table, self.src, self.before = place, src, before
                self.stats_done, self.aggr_done, self.ln_done, self.root_done = (
                    sem(tag + n) for n in ("_stats", "_aggr", "_ln", "_root"))

            def stats(self, v, k, j, src_ready=None):
                if src_ready is not None:
                    v.wait_ge(src_ready, k + 1).then_inc(spare, 1)
                for g in range(2):
                    ins = v.bn_stats(STATS[self.table][j][:, g, :], self.src(k, g))
                ins.then_inc(self.stats_done, 1)

            def aggregate(self, v, k, j, applied):
                after(v, applied, k - 1)
                v.wait_ge(self.stats_done, k + 1 + self.before).then_inc(spare, 1)
                for g in range(2):
                    ins = v.bn_aggr(MV[self.table][j][:, g, :], STATS[self.table][j][:, g, :])
                ins.then_inc(self.aggr_done, 1)

            def root(self, act, k, j):
                r = ROOT[self.table][j][:, :, 0]
                act.wait_ge(self.aggr_done, k + 1 + self.before)
                act.activation(r, MV[self.table][j][:, :, 1], ACT.Ln, bias=epsc[:, 0:1]).then_inc(self.ln_done, 1)
                act.wait_ge(self.ln_done, k + 1 + self.before)
                act.activation(r, r, ACT.Exp, scale=-0.5).then_inc(self.root_done, 1)

            def apply(self, v, k, j, dst, done, free=()):
                v.wait_ge(self.root_done, k + 1 + self.before)
                for s, m in free:
                    after(v, s, m)
                for g in range(2):
                    ins = v.tensor_scalar(dst(g), self.src(k, g), MV[self.table][j][:, g, 0:1],
                                          ROOT[self.table][j][:, g, :], ALU.subtract, ALU.mult)
                ins.then_inc(done, 1)

        a_xnT, a_T, a_qk, a_v, a_S, a_PT, a_O, a_OT, a_wo, a_h0T, a_lg = (sem("a_" + n) for n in
            "xnT T qk v S PT O OT wo h0T lg".split())
        a_q, a_k, a_exp, a_pt, a_OTs, a_h0Ts = (sem("a_" + n) for n in "q k exp pt OTs h0Ts".split())
        a_xn, a_vs, a_max, a_sub, a_r, a_On, a_x1, a_h0, a_lgs = (sem("a_" + n) for n in
            "xn vs max sub r On x1 h0 lgs".split())
        a_xb, a_hi, a_lo, prep_t, prep_hi, prep = (sem(n) for n in
            "a_xb a_hi a_lo prep_t prep_hi prep".split())
        norm_x = Norm("norm1", 0, lambda k, g: X[:, k, g, :])
        norm_h = Norm("norm2", 1, lambda k, g: X[:, k, g, :])
        LAST_A = PAIRS + 6

        def flat(t):
            return t.rearrange("p a b -> p (a b)")

        def transpose_x(pe, k, j):
            pe.wait_ge(a_xn, k + 1)
            straight(pe, a_xnT, k)
            after(pe, a_h0Ts, k - 4)
            for g in range(2):
                ins = pe.transpose(PS[:, 0, g * P:(g + 1) * P], XN[j][:, g, :], ident)
            ins.then_inc(a_T, 1)

        def queries_keys(pe, k, j):
            pe.wait_ge(a_xnT, k + 1)
            after(pe, a_k, k)
            pe.matmul(PS[:, 1, 0:256], MT[:, MAT_Q:MAT_Q + P], flat(XNT[:, :, :]), start=True, stop=True)
            pe.matmul(PS[:, 1, 256:512], MT[:, MAT_K:MAT_K + P], flat(XNT[:, :, :]), start=True, stop=True).then_inc(a_qk, 1)

        def values(pe, k, j):
            straight(pe, a_vs, k)
            after(pe, a_lgs, k - 3)
            for g in range(2):
                ins = pe.matmul(PS[:, 2, g * P:(g + 1) * P], XNT[:, g, :], MT[:, MAT_V:MAT_V + P],
                                start=True, stop=True)
            ins.then_inc(a_v, 1)

        def scores(pe, k, j):
            pe.wait_ge(a_k, k + 1)
            after(pe, a_sub, k)
            for g in range(2):
                pe.matmul(PS[:, 3 + g, :], QT[:, g, :], KB[j][:, g * 512:(g + 1) * 512], start=True, stop=False)
                ins = pe.matmul(PS[:, 3 + g, :], identb[:, :], mask0[:, :, :].rearrange("p h m -> p (h m)"),
                                start=False, stop=True)
            ins.then_inc(a_S, 1)

        def transpose_probs(pe, k, j):
            pe.wait_ge(a_exp, k + 1)
            after(pe, a_pt, k)
            for b in range(8):
                ins = pe.transpose(PS[:, 5 + b // 4, (b % 4) * P:(b % 4 + 1) * P], PR[j][:, b, :], ident)
            ins.then_inc(a_PT, 1)

        def probs_values(pe, k, j):
            pe.wait_ge(a_pt, k + 1)
            pe.wait_ge(a_vs, k + 1)
            after(pe, a_x1, k)
            for b in range(8):
                ins = pe.matmul(PS[:, 7, 33 * b:33 * b + 33], PT[:, b, :], VA[j][:, b // 4, b % 4, :], start=True, stop=True)
            ins.then_inc(a_O, 1)

        def transpose_attention(pe, k, j):
            pe.wait_ge(a_On, k + 1)
            for g in range(2):
                ins = pe.transpose(PS[:, 7, g * P:(g + 1) * P], ON[:, g, :], ident)
            ins.then_inc(a_OT, 1)

        def project(pe, k, j):
            pe.wait_ge(a_OTs, k + 1)
            for g in range(2):
                ins = pe.matmul(PS[:, 7, g * P:(g + 1) * P], OT[:, g, :], MT[:, MAT_O:MAT_O + P], start=True, stop=True)
            ins.then_inc(a_wo, 1)

        def transpose_h0(pe, k, j):
            pe.wait_ge(a_h0, k + 1)
            after(pe, a_xnT, upto(k + 5))
            straight(pe, a_h0Ts, k)
            for g in range(2):
                ins = pe.transpose(PS[:, 0, g * P:(g + 1) * P], HF[j][:, g, :], ident)
            ins.then_inc(a_h0T, 1)

        def router(pe, k, j):
            pe.wait_ge(a_h0Ts, k + 1)
            after(pe, a_vs, upto(k + 4))
            straight(pe, a_lgs, k)
            for g in range(2):
                ins = pe.matmul(PS[:, 2, 256 + 8 * g:264 + 8 * g], HT[:, g, :], MT[:, MAT_R:MAT_R + 8],
                                start=True, stop=True)
            ins.then_inc(a_lg, 1)

        def pe_a(pe, i, j):
            at(transpose_x, pe, i, j, 3)
            at(probs_values, pe, i, j, 6)
            at(values, pe, i, j, 4)
            at(scores, pe, i, j, 4)
            at(transpose_attention, pe, i, j, 6)
            at(transpose_h0, pe, i, j, 7)
            at(transpose_probs, pe, i, j, 5)
            at(queries_keys, pe, i, j, 3)
            at(project, pe, i, j, 6)
            at(router, pe, i, j, 7)

        def take_xT(act, k, j):
            act.wait_ge(a_T, k + 1)
            after(act, a_v, k)
            act.activation(flat(XNT[:, :, :]), PS[:, 0, 0:256], ACT.Copy).then_inc(a_xnT, 1)

        def take_queries(act, k, j):
            act.wait_ge(a_qk, k + 1)
            after(act, a_S, k)
            act.activation(flat(QT[:, :, :]), PS[:, 1, 0:256], ACT.Identity, bias=CL[:, COL_BQ:COL_BQ + 1]).then_inc(a_q, 1)

        def take_keys(act, k, j):
            act.wait_ge(a_q, k + 1)
            for h in range(HEADS_A):
                rows = slice(h * WIDTH_A, (h + 1) * WIDTH_A)
                ins = act.activation(KB[j][rows, :].rearrange("p (g h m) -> p g h m", g=2, h=HEADS_A)[:, :, h, :],
                                     PS[rows, 1, 256:512].rearrange("p (g m) -> p g m", g=2), ACT.Identity,
                                     bias=CL[rows, COL_BK:COL_BK + 1])
            ins.then_inc(a_k, 1)

        def exponent(act, k, j):
            act.wait_ge(a_sub, k + 1)
            act.activation(flat(PR[j][:, :, :]), flat(PR[j][:, :, :]), ACT.Exp, scale=float(WIDTH_A) ** -0.5).then_inc(a_exp, 1)

        def take_probs(act, k, j):
            act.wait_ge(a_PT, k + 1)
            after(act, a_O, k)
            act.activation(flat(PT[:, :, :]), flat(PS[:, 5:7, :]), ACT.Copy).then_inc(a_pt, 1)

        def take_attention(act, k, j):
            act.wait_ge(a_OT, k + 1)
            act.activation(flat(OT[:, :, :]), PS[:, 7, 0:256], ACT.Copy).then_inc(a_OTs, 1)

        def take_h0T(act, k, j):
            act.wait_ge(a_h0T, k + 1)
            act.activation(flat(HT[:, :, :]), PS[:, 0, 0:256], ACT.Copy).then_inc(a_h0Ts, 1)

        def root_x(act, k, j):
            norm_x.root(act, k, j)

        def root_h(act, k, j):
            norm_h.root(act, k, j)

        def act_a(act, i, j):
            at(take_keys, act, i, j, 4)
            at(take_xT, act, i, j, 3)
            at(root_h, act, i, j, 7)
            at(exponent, act, i, j, 5)
            at(root_x, act, i, j, 1)
            at(take_attention, act, i, j, 6)
            at(take_h0T, act, i, j, 7)
            at(take_probs, act, i, j, 5)
            at(take_queries, act, i, j, 3)

        def stats_x(v, k, j):
            norm_x.stats(v, k, j)

        def aggregate_x(v, k, j):
            norm_x.aggregate(v, k, j, a_xn)

        def normed_x(v, k, j):
            norm_x.apply(v, k, j, lambda g: XN[j][:, g, :], a_xn, [(a_T, k - 1)])

        def take_values(v, k, j):
            v.wait_ge(a_v, k + 1)
            after(v, a_O, k - 1)
            v.tensor_tensor(VA[j][:, :, :, 0:32], PS[:, 2, 0:256].rearrange("p (g h w) -> p g h w", g=2, w=32),
                            bcast(row(ROW_BV).rearrange("p (h w) -> p h w", w=32), 1, 2), ALU.add).then_inc(a_vs, 1)

        def less_maximum(v, k, j):
            s = PS[:, 3:5, :].rearrange("p g (h m) -> p (g h) m", h=4)
            v.wait_ge(a_S, k + 1)
            v.tensor_reduce(MX[:, :], s, AX.X, ALU.max).then_inc(a_max, 1)
            v.wait_ge(a_max, k + 1)
            after(v, a_PT, k - 1)
            v.tensor_tensor(PR[j][:, :, :], s, bcast(MX[:, :], 2, P), ALU.subtract).then_inc(a_sub, 1)

        def sums(v, k, j):
            v.wait_ge(a_O, k + 1)
            v.reciprocal(RS[:, :], PS[:, 7, 0:264].rearrange("p (b w) -> p b w", w=33)[:, :, 32]).then_inc(a_r, 1)

        def normalise(v, k, j):
            v.wait_ge(a_r, k + 1)
            v.scalar_tensor_tensor(ON[:, :, :].rearrange("p g (h w) -> p (g h) w", w=32),
                                   PS[:, 7, 0:264].rearrange("p (b w) -> p b w", w=33)[:, :, 0:32],
                                   has[:, 0:1], bcast(RS[:, :], 2, 32), ALU.mult, ALU.mult).then_inc(a_On, 1)

        def residual(v, k, j):
            v.wait_ge(a_wo, k + 1)
            v.wait_ge(a_xb, k + 1)
            v.tensor_tensor(X[:, k, :, :], PS[:, 7, 0:256].rearrange("p (g d) -> p g d", g=2), X[:, k, :, :],
                            ALU.add).then_inc(a_x1, 1)

        def stats_h(v, k, j):
            norm_h.stats(v, k, j, a_x1)

        def aggregate_h(v, k, j):
            norm_h.aggregate(v, k, j, a_h0)

        def normed_h(v, k, j):
            norm_h.apply(v, k, j, lambda g: HF[j][:, g, :], a_h0, [(a_h0T, k - 1), (a_lo, k - 1)])

        def take_logits(v, k, j):
            v.wait_ge(a_lg, k + 1)
            v.tensor_copy(LG[:, :, :].rearrange("p (q g) e -> p q (g e)", g=2)[:, k, :], PS[:, 2, 256:272]).then_inc(a_lgs, 1)

        def dve_a(v, i, j):
            at(normalise, v, i, j, 6)
            at(aggregate_x, v, i, j, 1)
            at(normed_h, v, i, j, 7)
            at(take_values, v, i, j, 4)
            at(less_maximum, v, i, j, 4)
            at(residual, v, i, j, 6)
            at(take_logits, v, i, j, 7)
            at(stats_h, v, i, j, 6)
            at(aggregate_h, v, i, j, 6)
            at(sums, v, i, j, 5)
            at(stats_x, v, i, j, 0)
            at(normed_x, v, i, j, 1)

        def add_bias(pool, k, j):
            pool.wait_ge(a_xn, k + 1)
            pool.tensor_tensor(X[:, k, :, :], X[:, k, :, :], bcast(row(ROW_BO), 1, 2), ALU.add).then_inc(a_xb, 1)

        def high_h0(pool, k, j):
            pool.wait_ge(a_h0, k + 1).then_inc(spare, 1)
            pool.tensor_copy(HL[:, k, :, 0, :], HF[j][:, :, :]).then_inc(a_hi, 1)

        def low_h0(pool, k, j):
            pool.wait_ge(a_hi, k + 1)
            pool.tensor_tensor(HL[:, k, :, 1, :], HF[j][:, :, :], HL[:, k, :, 0, :], ALU.subtract).then_inc(a_lo, 1)

        def split_weights(pool, i, j):
            e = i // 2 if isinstance(i, int) else chunk_net[0]
            raw = RAW[j][:, :, :].rearrange("p c t -> p (c t)")[:, 0:HIDDEN]
            tmp = RAW[j][:, :, :].rearrange("p c t -> p (c t)")[:, HIDDEN:2 * HIDDEN]
            pool.wait_ge(raw_ld[j], 16 * (e + 1))
            pool.tensor_tensor(tmp, raw, wscale[:, 0:1].broadcast_to([P, HIDDEN]), ALU.mult).then_inc(prep_t, 1)
            pool.wait_ge(prep_t, i + 1).then_inc(spare, 1)
            pool.tensor_copy(WH[:, e, j, :], tmp).then_inc(prep_hi, 1)
            pool.wait_ge(prep_hi, i + 1)
            pool.tensor_tensor(WL[:, e, j, :], tmp, WH[:, e, j, :], ALU.subtract).then_inc(prep, 1)

        def pool_a(pool, i, j, chunk):
            at(high_h0, pool, i, j, 7)
            at(add_bias, pool, i, j, 2)
            at(low_h0, pool, i, j, 7)
            if chunk:
                split_weights(pool, i, j)

        chunk_net = [None]

        class Net:
            def __init__(self, tag):
                (self.T, self.xT, self.h, self.g, self.hi, self.lo, self.y, self.ys) = (
                    sem(tag + n) for n in ("_T", "_xT", "_h", "_g", "_hi", "_lo", "_y", "_ys"))

        b, d = Net("b"), Net("d")

        def first_layer(pe, s, k, j, e):
            pe.wait_ge(s.xT, k + 1)
            for half in range(2):
                after(pe, s.g, 2 * k + half - 3)
                for c in (2 * half, 2 * half + 1):
                    dst = PS[:, 2 + 2 * j + half, (c % 2) * TILE:(c % 2 + 1) * TILE]
                    wh, wl = (w[:, e, 0, c * P:(c + 1) * P] for w in (WH, WL))
                    pe.matmul(dst, wh, XTS[j][:, 0, :], start=True, stop=False)
                    pe.matmul(dst, wh, XTS[j][:, 1, :], start=False, stop=False)
                    ins = pe.matmul(dst, wl, XTS[j][:, 0, :], start=False, stop=True)
                ins.then_inc(s.h, 1)

        def gelu(act, s, k, j, e, func):
            for half in range(2):
                act.wait_ge(s.h, 2 * k + half + 1)
                after(act, s.lo, 2 * k + half - 3)
                for c in (2 * half, 2 * half + 1):
                    ins = act.activation(RAW[j][:, c, :], PS[:, 2 + 2 * j + half, (c % 2) * TILE:(c % 2 + 1) * TILE],
                                         func, bias=CL[:, 0:NETS * CHUNKS].rearrange("p (e c) -> p e c", e=NETS)[:, e, c:c + 1],
                                         scale=1.0 / WSCALE)
                ins.then_inc(s.g, 1)

        def split(v, s, k, j):
            for half in range(2):
                cs = slice(2 * half, 2 * half + 2)
                v.wait_ge(s.g, 2 * k + half + 1)
                if half == 0:
                    after(v, s.y, k - 1)
                v.tensor_copy(HH[j][:, cs, :], RAW[j][:, cs, :]).then_inc(s.hi, 1)
                v.wait_ge(s.hi, 2 * k + half + 1)
                v.tensor_tensor(HLO[j][:, cs, :], RAW[j][:, cs, :], HH[j][:, cs, :], ALU.subtract).then_inc(s.lo, 1)

        def second_layer(pe, s, k, j, e, bank_free):
            pe.wait_ge(s.lo, 2 * k + 2)
            after(pe, *bank_free)
            for t in range(2):
                for c in range(CHUNKS):
                    hh, hl = (h[j][:, c, t * P:(t + 1) * P] for h in (HH, HLO))
                    wh, wl = (w[:, e, 1, c * P:(c + 1) * P] for w in (WH, WL))
                    dst = PS[:, 6 + j, t * P:(t + 1) * P]
                    pe.matmul(dst, hh, wh, start=c == 0, stop=False)
                    pe.matmul(dst, hh, wl, start=False, stop=False)
                    ins = pe.matmul(dst, hl, wh, start=False, stop=c == CHUNKS - 1)
            ins.then_inc(s.y, 1)

        xs_ld = [sem("xs_ld0"), sem("xs_ld1")]
        y_st = [sem("y_st0"), sem("y_st1")]
        sc_ready = sem("sc_ready")
        sc_done = [sem("sc_done0"), sem("sc_done1")]
        route = sem("route")
        r_slots, r_eid, r_cnt, r_diff, r_exp = (sem("r_" + n) for n in "slots eid cnt diff exp".split())
        r_oh = sem("r_oh")
        LAST_B = ALL_TILES + 1
        SPLIT_B = SHARED_TILES + 4

        def in_b(k):
            return not isinstance(k, int) or 0 <= k < ALL_TILES

        def is_shared(k, shared_loop):
            return k < SHARED_TILES if isinstance(k, int) else shared_loop

        def net_of(eng, k, shared_loop):
            if is_shared(k, shared_loop):
                return SHARED
            eng.wait_ge(r_eid, 1)
            return eng.value_load(EID[0:1, bass.ds(k - SHARED_TILES, 1)], min_val=0, max_val=EXPERTS - 1)

        def half_of(k, p, c):
            return k // 2 if isinstance(k, int) else p + c // 2

        def pe_b(pe, t, j, p, shared):
            if in_b(t):
                after(pe, b.xT, t - 1)
                if is_shared(t, shared):
                    src = HL[:, t, :, :, :]
                else:
                    src = XS[j]
                    pe.wait_ge(xs_ld[j], 16 * (half_of(t, p, j) + 1 - SHARED_TILES // 2))
                dst = PS[:, j, :].bitcast(F16)
                for hl in range(2):
                    for g in range(2):
                        ins = pe.transpose(dst[:, hl * TILE + g * P:hl * TILE + (g + 1) * P], src[:, g, hl, :], ident16[:, :])
                ins.then_inc(b.T, 1)
            k = t - 1
            if in_b(k):
                first_layer(pe, b, k, (j + 1) % 2, net_of(pe, k, shared))
            k = t - 2
            if in_b(k):
                second_layer(pe, b, k, j, net_of(pe, k, shared), (b.ys, k - 1))

        def act_b(act, t, j, p, shared):
            if in_b(t):
                act.wait_ge(b.T, t + 1)
                after(act, b.h, 2 * t - 2)
                act.activation(XTS[j][:, :, :].rearrange("p a b -> p (a b)"), PS[:, j, :].bitcast(F16)[:, 0:2 * TILE],
                               ACT.Copy).then_inc(b.xT, 1)
            k = t - 1
            if in_b(k):
                gelu(act, b, k, (j + 1) % 2, net_of(act, k, shared), ACT.Gelu)

        def dve_b(v, t, j, p, shared):
            k = t - 1
            if in_b(k):
                split(v, b, k, (j + 1) % 2)
            k = t - 2
            if in_b(k):
                e = net_of(v, k, shared)
                v.wait_ge(b.y, k + 1)
                if is_shared(k, shared):
                    v.scalar_tensor_tensor(X[:, k, :, :], PS[:, 6 + j, 0:256].rearrange("p (g d) -> p g d", g=2),
                                           1.0 / WSCALE, X[:, k, :, :], ALU.mult, ALU.add).then_inc(b.ys, 1)
                    return
                after(v, y_st[j], 16 * (half_of(k - 2, p, j - 4) + 1 - SHARED_TILES // 2))
                v.scalar_tensor_tensor(YS[j][:, :, :], PS[:, 6 + j, 0:256].rearrange("p (g d) -> p g d", g=2),
                                       1.0 / WSCALE, bcast(RW[:, ROW_NETS + e, :], 1, 2) if isinstance(e, int) else
                                       bcast(RW[:, ROW_NETS:ROWS, :][:, e, :], 1, 2), ALU.mult, ALU.add).then_inc(b.ys, 1)

        def sp_b(sp, t, j, p, shared):
            k = t + 1
            if in_b(k) and not is_shared(k, shared):
                jk = (j + 1) % 2
                if isinstance(k, int) and k == SHARED_TILES:
                    for s in sc_done:
                        sp.wait_ge(s, 64 * PAIRS // 2)
                if not isinstance(k, int) or k - 2 >= SHARED_TILES:
                    sp.wait_ge(b.T, k - 1)
                r = (k - SHARED_TILES) * TILE
                sp.dma_start(XS[jk][:, :, :, :].rearrange("p g a d -> p g (a d)"),
                             sorted_rows[bass.ds(r, TILE), :].rearrange("(g p) d -> p g d", p=P)).then_inc(xs_ld[jk], 16)
            k = t - 2
            if in_b(k) and not is_shared(k, shared):
                sp.wait_ge(b.ys, k + 1)
                sp.dma_start(results[bass.ds((k - SHARED_TILES) * TILE, TILE), :].rearrange("(g p) d -> p g d", p=P),
                             YS[j][:, :, :]).then_inc(y_st[j], 16)

        def run_b(eng, fn):
            for t in range(FIRST):
                fn(eng, t, t % 2, None, True)
            with eng.Fori(FIRST // 2, SHARED_TILES // 2 - 1) as p:
                for j in range(2):
                    fn(eng, p * 2 + j, j, p, True)
            for t in range(SHARED_TILES - 2, SPLIT_B):
                fn(eng, t, t % 2, None, True)
            with eng.Fori(SPLIT_B // 2, ALL_TILES // 2 - 1) as p:
                for j in range(2):
                    fn(eng, p * 2 + j, j, p, False)
            for t in range(ALL_TILES - 2, LAST_B + 1):
                fn(eng, t, t % 2, None, False)

        def both(name):
            return [sem(name + "0"), sem(name + "1")]

        c_T, c_aT, c_qk, c_v, c_w1, c_F = (sem("c_" + n) for n in "T aT qk v w1 F".split())
        c_zT, c_zk, c_aTs, c_q, c_k, c_relu = (sem("c_" + n) for n in "zT zk aTs q k relu".split())
        c_S, c_PT, c_O, c_exp, c_pt, c_max, c_sub, c_r, c_On = (both("c_" + n) for n in "S PT O exp pt max sub r On".split())
        c_x2b, c_x2, c_z, c_vs, c_s1, c_n1, c_s2, c_n2, c_x3, c_u, c_uw, c_xu = (
            sem("c_" + n) for n in "x2b x2 z vs s1 n1 s2 n2 x3 u uw xu".split())
        c_ag, c_a, c_ab, c_cg, c_c, c_hi, c_lo, c_um = (sem("c_" + n) for n in "ag a ab cg c hi lo um".split())
        g_idx = sem("g_idx")
        g_ld = both("g_ld")
        LAST_C = PAIRS + 8
        FIRST_C = 10
        GY = two("GY", [P, 4, P])
        S1 = [RAW[1][:, j, :].rearrange("p (g d) -> p g d", g=2) for j in range(2)]
        A1 = two("A1", [P, 2, P])
        AB = two("AB", [P, 2, P])
        S2 = [RAW[1][:, 2 + j, :].rearrange("p (g d) -> p g d", g=2) for j in range(2)]
        C2 = two("C2", [P, 2, P])
        PTC = [PT, RAW[0][:, :, :].rearrange("p c (a m) -> p (c a) m", a=2)]
        MXC = [MX, sb("MX1", [P, 8])]
        RSC = [RS, sb("RS1", [P, 8])]
        HR = sb("HR", [P, 2 * P])
        UM = YS[0]
        AT = HT
        Z = HL[:, :, :, :, :].rearrange("p k g a d -> p (k g a d)").bitcast(F32).rearrange("p (k g d) -> p k g d", g=2, d=P)

        norm_z = Norm("norm1", 0, lambda k, g: X[:, k, g, :], PAIRS)
        norm_u = Norm("norm2", 1, lambda k, g: X[:, k, g, :], PAIRS)
        norm_1 = [Norm("norm3", 2, lambda k, g, j=j: S1[j][:, g, :]) for j in range(2)]
        norm_2 = [Norm("norm4", 3, lambda k, g, j=j: S2[j][:, g, :]) for j in range(2)]

        def of_graph(stage, g):
            return lambda eng, k, j: stage(eng, k, j, g)

        def transpose_z(pe, k, j):
            pe.wait_ge(c_z, k + 1)
            straight(pe, c_zT, k)
            after(pe, c_relu, k - 3)
            for g in range(2):
                ins = pe.transpose(PS[:, 0, g * P:(g + 1) * P], XN[j][:, g, :], ident)
            ins.then_inc(c_T, 1)

        def queries_keys_c(pe, k, j):
            pe.wait_ge(c_zT, k + 1)
            after(pe, c_k, k)
            pe.matmul(PS[:, 1, 0:256], MT[:, MAT_QKV:MAT_QKV + P], flat(XNT[:, :, :]), start=True, stop=True)
            pe.matmul(PS[:, 1, 256:512], MT[:, MAT_QKV + P:MAT_QKV + 2 * P], flat(XNT[:, :, :]),
                      start=True, stop=True).then_inc(c_qk, 1)

        def values_c(pe, k, j):
            straight(pe, c_vs, k)
            after(pe, c_s2, k - 2)
            for g in range(2):
                ins = pe.matmul(PS[:, 2, g * P:(g + 1) * P], XNT[:, g, :], MT[:, MAT_QKV + 2 * P:MAT_QKV + 3 * P],
                                start=True, stop=True)
            ins.then_inc(c_v, 1)

        def scores_c(pe, k, j, g):
            if g == 0:
                pe.wait_ge(c_k, k + 1)
                after(pe, c_sub[1], k)
            else:
                pe.wait_ge(c_sub[0], k + 1)
            for h in range(2):
                pe.matmul(PS[:, 3 + h, :], QT[:, g, :], KB[g][:, h * 512:(h + 1) * 512], start=True, stop=False)
                ins = pe.matmul(PS[:, 3 + h, :], identb[:, :], mask1[:, :, :].rearrange("p h m -> p (h m)"),
                                start=False, stop=True)
            ins.then_inc(c_S[g], 1)

        def transpose_probs_c(pe, k, j, g):
            pe.wait_ge(c_exp[g], k + 1)
            after(pe, c_pt[1 - g], k + g)
            for h in range(8):
                ins = pe.transpose(PS[:, 5 + h // 4, (h % 4) * P:(h % 4 + 1) * P], PR[g][:, h, :], ident)
            ins.then_inc(c_PT[g], 1)

        def probs_values_c(pe, k, j, g):
            pe.wait_ge(c_pt[g], k + 1)
            if g == 0:
                pe.wait_ge(c_vs, k + 1)
            after(pe, c_On[1 - g], k + g)
            for h in range(8):
                ins = pe.matmul(PS[:, 7, 17 * h:17 * h + 17], PTC[g][:, h, :], VC[j][:, g, h, :], start=True, stop=True)
            ins.then_inc(c_O[g], 1)

        def transpose_a(pe, k, j):
            pe.wait_ge(c_a, k + 1)
            after(pe, c_zT, upto(k + 4))
            straight(pe, c_relu, k)
            for g in range(2):
                ins = pe.transpose(PS[:, 0, g * P:(g + 1) * P], A1[j][:, g, :], ident)
            ins.then_inc(c_aT, 1)

        def hidden_c(pe, k, j):
            pe.wait_ge(c_aTs, k + 1)
            pe.matmul(PS[:, 0, 0:256], MT[:, MAT_F1:MAT_F1 + P], flat(AT[:, :, :]), start=True, stop=True).then_inc(c_w1, 1)

        def network_out_c(pe, k, j):
            pe.wait_ge(c_relu, k + 1)
            after(pe, c_vs, upto(k + 3))
            straight(pe, c_s2, k)
            for g in range(2):
                ins = pe.matmul(PS[:, 2, g * P:(g + 1) * P], HR[:, g * P:(g + 1) * P], MT[:, MAT_F2:MAT_F2 + P],
                                start=True, stop=True)
            ins.then_inc(c_F, 1)

        def pe_c(pe, i, j):
            at(queries_keys_c, pe, i, j, 3)
            at(of_graph(probs_values_c, 1), pe, i, j, 5)
            at(hidden_c, pe, i, j, 6)
            at(of_graph(scores_c, 1), pe, i, j, 4)
            at(network_out_c, pe, i, j, 6)
            at(of_graph(transpose_probs_c, 0), pe, i, j, 4)
            at(transpose_z, pe, i, j, 2)
            at(values_c, pe, i, j, 3)
            at(of_graph(scores_c, 0), pe, i, j, 3)
            at(of_graph(probs_values_c, 0), pe, i, j, 4)
            at(of_graph(transpose_probs_c, 1), pe, i, j, 4)
            at(transpose_a, pe, i, j, 5)

        def take_zT(act, k, j):
            act.wait_ge(c_T, k + 1)
            after(act, c_v, k)
            act.activation(flat(XNT[:, :, :]), PS[:, 0, 0:256], ACT.Copy).then_inc(c_zT, 1)

        def keep_z(act, k, j):
            act.wait_ge(c_z, k + 1).then_inc(spare, 1)
            act.activation(Z[:, k, :, :], XN[j][:, :, :], ACT.Copy).then_inc(c_zk, 1)

        def take_queries_c(act, k, j):
            act.wait_ge(c_qk, k + 1)
            after(act, c_S[1], k)
            act.activation(flat(QT[:, :, :]), PS[:, 1, 0:256], ACT.Copy).then_inc(c_q, 1)

        def take_keys_c(act, k, j):
            act.wait_ge(c_q, k + 1)
            for h in range(HEADS_C):
                rows = slice(h // 2 * 32, h // 2 * 32 + 32)
                ins = act.activation(KBC[rows, :, :].rearrange("p g (h m) -> p g h m", h=HEADS_C)[:, :, h, :],
                                     PS[rows, 1, 256:512].rearrange("p (g m) -> p g m", g=2), ACT.Copy,
                                     scale=CN[rows, C_H8 + h:C_H8 + h + 1])
            ins.then_inc(c_k, 1)

        def take_values_c(act, k, j):
            act.wait_ge(c_v, k + 1)
            after(act, c_O[1], k - 1)
            act.activation(VC[j][:, :, :, 0:16], PS[:, 2, 0:256].rearrange("p (g h w) -> p g h w", g=2, w=16),
                           ACT.Copy).then_inc(c_vs, 1)

        def exponent_c(act, k, j, g):
            act.wait_ge(c_sub[g], k + 1)
            act.activation(flat(PR[g][:, :, :]), flat(PR[g][:, :, :]), ACT.Exp, scale=float(WIDTH_C) ** -0.5).then_inc(c_exp[g], 1)

        def take_probs_c(act, k, j, g):
            act.wait_ge(c_PT[g], k + 1)
            after(act, c_O[g], k)
            act.activation(flat(PTC[g][:, :, :]), flat(PS[:, 5:7, :]), ACT.Copy).then_inc(c_pt[g], 1)

        def take_aT(act, k, j):
            act.wait_ge(c_aT, k + 1)
            act.activation(flat(AT[:, :, :]), PS[:, 0, 0:256], ACT.Copy).then_inc(c_aTs, 1)

        def relu_c(act, k, j):
            act.wait_ge(c_w1, k + 1)
            act.activation(HR[:, :], PS[:, 0, 0:256], ACT.Relu, bias=CL[:, COL_B1C:COL_B1C + 1]).then_inc(c_relu, 1)

        def root_z(act, k, j):
            norm_z.root(act, k, j)

        def root_u(act, k, j):
            norm_u.root(act, k, j)

        def root_1(act, k, j):
            norm_1[j].root(act, k, j)

        def root_2(act, k, j):
            norm_2[j].root(act, k, j)

        def act_c(act, i, j):
            at(take_aT, act, i, j, 6)
            at(relu_c, act, i, j, 6)
            at(root_z, act, i, j, 1)
            at(of_graph(exponent_c, 0), act, i, j, 4)
            at(root_u, act, i, j, 7)
            at(take_queries_c, act, i, j, 3)
            at(take_keys_c, act, i, j, 3)
            at(take_zT, act, i, j, 2)
            at(keep_z, act, i, j, 2)
            at(of_graph(take_probs_c, 0), act, i, j, 4)
            at(root_1, act, i, j, 5)
            at(of_graph(exponent_c, 1), act, i, j, 4)
            at(root_2, act, i, j, 6)
            at(of_graph(take_probs_c, 1), act, i, j, 4)
            at(take_values_c, act, i, j, 3)

        def expert_added(v, k, j, choice, before, done):
            for g in range(2):
                w = WT[:, choice, :].rearrange("p (q g) -> p q g", g=2)[:, k, g:g + 1]
                ins = v.scalar_tensor_tensor(X[:, k, g, :], GY[j][:, 2 * g + choice, :], w, X[:, k, g, :],
                                             ALU.mult, ALU.add)
            ins.then_inc(done, 1)

        def first_expert(v, k, j):
            v.wait_ge(g_ld[j], 32 * (k - j) + 64)
            expert_added(v, k, j, 0, None, c_x2b)

        def second_expert(v, k, j):
            v.wait_ge(c_x2b, k + 1)
            expert_added(v, k, j, 1, c_x2b, c_x2)

        def stats_z(v, k, j):
            norm_z.stats(v, k, j, c_x2)

        def aggregate_z(v, k, j):
            norm_z.aggregate(v, k, j, c_z)

        def normed_z(v, k, j):
            norm_z.apply(v, k, j, lambda g: XN[j][:, g, :], c_z, [(c_T, k - 1), (c_zk, k - 1)])

        def maximum_c(v, k, j, g):
            v.wait_ge(c_S[g], k + 1)
            v.tensor_reduce(MXC[g][:, :], PS[:, 3:5, :].rearrange("p g (h m) -> p (g h) m", h=4), AX.X,
                            ALU.max).then_inc(c_max[g], 1)

        def less_maximum_c(v, k, j, g):
            v.wait_ge(c_max[g], k + 1)
            after(v, c_PT[g], k)
            v.tensor_tensor(PR[g][:, :, :], PS[:, 3:5, :].rearrange("p g (h m) -> p (g h) m", h=4),
                            bcast(MXC[g][:, :], 2, P), ALU.subtract).then_inc(c_sub[g], 1)

        def sums_c(v, k, j, g):
            v.wait_ge(c_O[g], k + 1)
            v.reciprocal(RSC[g][:, :], PS[:, 7, 0:136].rearrange("p (h w) -> p h w", w=17)[:, :, 16]).then_inc(c_r[g], 1)

        def normalise_c(v, k, j, g):
            v.wait_ge(c_r[g], k + 1)
            v.tensor_tensor(ON[:, g, :].rearrange("p (h w) -> p h w", w=16),
                            PS[:, 7, 0:136].rearrange("p (h w) -> p h w", w=17)[:, :, 0:16],
                            bcast(RSC[g][:, :], 2, 16), ALU.mult).then_inc(c_On[g], 1)

        def attention_residual(v, k, j):
            v.wait_ge(c_On[1], k + 1)
            v.wait_ge(c_zk, k + 1)
            v.tensor_tensor(S1[j][:, :, :], Z[:, k, :, :], ON[:, :, :], ALU.add).then_inc(c_s1, 1)

        def stats_1(v, k, j):
            norm_1[j].stats(v, k, j, c_s1)

        def aggregate_1(v, k, j):
            norm_1[j].aggregate(v, k, j, c_n1)

        def normed_1(v, k, j):
            norm_1[j].apply(v, k, j, lambda g: A1[j][:, g, :], c_n1, [(c_aT, k - 1), (c_ab, k - 1)])

        def network_residual(v, k, j):
            v.wait_ge(c_F, k + 1)
            v.wait_ge(c_ab, k + 1)
            v.tensor_tensor(S2[j][:, :, :], PS[:, 2, 0:256].rearrange("p (g d) -> p g d", g=2), AB[j][:, :, :],
                            ALU.add).then_inc(c_s2, 1)

        def stats_2(v, k, j):
            norm_2[j].stats(v, k, j, c_s2)

        def aggregate_2(v, k, j):
            norm_2[j].aggregate(v, k, j, c_n2)

        def normed_2(v, k, j):
            norm_2[j].apply(v, k, j, lambda g: C2[j][:, g, :], c_n2, [(c_x3, k - 1)])

        def layer_added(v, k, j):
            v.wait_ge(c_c, k + 1)
            v.tensor_tensor(X[:, k, :, :], X[:, k, :, :], C2[j][:, :, :], ALU.add).then_inc(c_x3, 1)

        def stats_u(v, k, j):
            norm_u.stats(v, k, j, c_x3)

        def aggregate_u(v, k, j):
            norm_u.aggregate(v, k, j, c_u)

        def normed_u(v, k, j):
            norm_u.apply(v, k, j, lambda g: HF[j][:, g, :], c_u, [(c_lo, k - 1), (c_um, k - 1)])

        def u_added(v, k, j):
            v.wait_ge(c_u, k + 1)
            v.tensor_tensor(X[:, k, :, :], X[:, k, :, :], HF[j][:, :, :], ALU.add).then_inc(c_xu, 1)

        def token_weights(v, k, j):
            v.wait_ge(c_um, k + 1)
            v.tensor_reduce(WTOK[:, :].rearrange("p (q g) -> p q g", g=2)[:, k, :], UM[:, :, :], AX.X,
                            ALU.add).then_inc(c_uw, 1)

        def dve_c(v, i, j):
            at(of_graph(normalise_c, 0), v, i, j, 5)
            at(of_graph(less_maximum_c, 0), v, i, j, 4)
            at(token_weights, v, i, j, 9)
            at(of_graph(sums_c, 1), v, i, j, 5)
            at(layer_added, v, i, j, 7)
            at(of_graph(normalise_c, 1), v, i, j, 5)
            at(stats_u, v, i, j, 7)
            at(attention_residual, v, i, j, 5)
            at(aggregate_u, v, i, j, 7)
            at(normed_z, v, i, j, 1)
            at(stats_1, v, i, j, 5)
            at(of_graph(maximum_c, 1), v, i, j, 4)
            at(network_residual, v, i, j, 6)
            at(of_graph(less_maximum_c, 1), v, i, j, 4)
            at(first_expert, v, i, j, 0)
            at(aggregate_1, v, i, j, 5)
            at(stats_2, v, i, j, 6)
            at(second_expert, v, i, j, 0)
            at(normed_u, v, i, j, 7)
            at(normed_1, v, i, j, 5)
            at(stats_z, v, i, j, 0)
            at(aggregate_2, v, i, j, 6)
            at(of_graph(maximum_c, 0), v, i, j, 3)
            at(normed_2, v, i, j, 6)
            at(of_graph(sums_c, 0), v, i, j, 4)
            at(aggregate_z, v, i, j, 0)
            at(u_added, v, i, j, 7)

        def gather(pool, k, j):
            if not isinstance(k, int) or k > 1:
                pool.wait_ge(c_x2, k - 1).then_inc(spare, 1)
            pool.tensor_copy(ISG[j][:, :], SL[:, :, :].rearrange("p (q g) k -> p q (g k)", g=2)[:, k, :]).then_inc(g_idx, 1)
            pool.wait_ge(g_idx, k + 1).then_inc(spare, 1)
            for q in range(4):
                pool.indirect_dma_start(out=GY[j][:, q, :], out_offset=None, in_=results[:, :],
                                        in_offset=bass.IndirectOffsetOnAxis(ap=ISG[j][:, q:q + 1], axis=0)).then_inc(g_ld[j], 16)

        def affine(pool, t, k, ready, half, done, gain, bias):
            pool.wait_ge(ready, k + 1)
            pool.tensor_tensor(t[:, :, :], t[:, :, :], bcast(row(gain), 1, 2), ALU.mult).then_inc(half, 1)
            pool.wait_ge(half, k + 1)
            pool.tensor_tensor(t[:, :, :], t[:, :, :], bcast(row(bias), 1, 2), ALU.add).then_inc(done, 1)

        def affine_1(pool, k, j):
            affine(pool, A1[j], k, c_n1, c_ag, c_a, ROW_G1, ROW_B1)

        def affine_2(pool, k, j):
            affine(pool, C2[j], k, c_n2, c_cg, c_c, ROW_G2, ROW_B2)

        def with_output_bias(pool, k, j):
            pool.wait_ge(c_a, k + 1)
            after(pool, c_s2, k - 1)
            pool.tensor_tensor(AB[j][:, :, :], A1[j][:, :, :], bcast(row(ROW_FB), 1, 2), ALU.add).then_inc(c_ab, 1)

        def weighted_u(pool, k, j):
            pool.wait_ge(c_u, k + 1)
            after(pool, c_uw, k)
            pool.tensor_tensor(UM[:, :, :], HF[j][:, :, :], bcast(row(ROW_WR), 1, 2), ALU.mult).then_inc(c_um, 1)

        def high_u(pool, k, j):
            pool.wait_ge(c_u, k + 1).then_inc(spare, 1)
            pool.tensor_copy(HL[:, k, :, 0, :], HF[j][:, :, :]).then_inc(c_hi, 1)

        def low_u(pool, k, j):
            pool.wait_ge(c_hi, k + 1)
            pool.tensor_tensor(HL[:, k, :, 1, :], HF[j][:, :, :], HL[:, k, :, 0, :], ALU.subtract).then_inc(c_lo, 1)

        def pool_c(pool, i, j):
            at(gather, pool, i, j, 0)
            at(weighted_u, pool, i, j, 8)
            at(low_u, pool, i, j, 8)
            at(high_u, pool, i, j, 7)
            at(affine_1, pool, i, j, 5)
            at(affine_2, pool, i, j, 6)
            at(with_output_bias, pool, i, j, 5)

        d_rank, d_oh, d_OT, d_OTs, d_yh, d_yf, d_yl, d_Z, d_o, d_wt, d_wg, d_pt = (
            sem("d_" + n) for n in "rank oh OT OTs yh yf yl Z o wt wg pt".split())
        LAST_D = MOD_TILES + 2
        PR16 = [t.bitcast(F16) for t in PRF]
        OH = [t[:, 0:512].rearrange("p (g s) -> p g s", g=4) for t in PR16]
        OHT = [t[:, 512:1024].rearrange("p (g s) -> p g s", g=4) for t in PR16]
        YH = [t[:, 1024:1280].rearrange("p (g d) -> p g d", g=2) for t in PR16]
        YL = [t[:, 1280:1536].rearrange("p (g d) -> p g d", g=2) for t in PR16]
        OUT = GY
        YF = A1
        IOTAM = sb("IOTAM", [P, P])
        WG, WK, SEL, CAND, PLACE = (KB[0][0:GRAPHS, n * P:(n + 1) * P] for n in range(5))
        TOP = sb("TOP", [GRAPHS, 8])
        KMAX = sb("KMAX", [GRAPHS, 1])

        def in_d(k):
            return not isinstance(k, int) or 0 <= k < MOD_TILES

        def u_parts(t, g, hl):
            return HL[:, :, :, :, :].rearrange("p (t q) g a d -> p t (q g) a d", q=2)[:, t, g, hl, :]

        def pe_d(pe, t, j):
            if in_d(t):
                if isinstance(t, int) and t == 0:
                    pe.wait_ge(c_lo, PAIRS)
                pe.wait_ge(d_oh, t + 1)
                after(pe, d_OTs, t - 1)
                for hl in range(2):
                    for g in range(4):
                        o = g % 2 * SLOTS
                        ins = pe.matmul(PS[:, j, hl * TILE + g * SLOTS:hl * TILE + (g + 1) * SLOTS], u_parts(t, g, hl),
                                        OH[j][:, g, o:o + SLOTS], start=True, stop=True)
                ins.then_inc(d.T, 1)
            k, jj = t - 1, (j + 1) % 2
            if in_d(k):
                first_layer(pe, d, k, jj, MOD)
                dst = PS[:, jj, :].bitcast(F16)
                for g in range(4):
                    ins = pe.transpose(dst[:, g * P:(g + 1) * P], OH[jj][:, g, :], ident16[:, :])
                ins.then_inc(d_OT, 1)
            k = t - 2
            if in_d(k):
                second_layer(pe, d, k, j, MOD, (d_o, k - 1))
            k = t - 3
            if in_d(k):
                pe.wait_ge(d_yl, k + 1)
                pe.wait_ge(d_OTs, k + 1)
                for g in range(4):
                    dst = PS[:, 6 + jj, g * P:(g + 1) * P]
                    pe.matmul(dst, OHT[jj][:, g, :], YH[jj][:, g // 2, :], start=True, stop=False)
                    ins = pe.matmul(dst, OHT[jj][:, g, :], YL[jj][:, g // 2, :], start=False, stop=True)
                ins.then_inc(d_Z, 1)

        def act_d(act, t, j):
            jj = (j + 1) % 2
            if in_d(t):
                act.wait_ge(d.T, t + 1)
                after(act, d.h, 2 * t - 2)
                act.activation(flat(XTS[j][:, :, :]), PS[:, j, :], ACT.Copy).then_inc(d.xT, 1)
            k = t - 1
            if in_d(k):
                gelu(act, d, k, jj, MOD, ACT.Gelu_apprx_tanh)
                act.wait_ge(d_OT, k + 1)
                after(act, d_Z, k - 1)
                act.activation(flat(OHT[jj][:, :, :]), PS[:, jj, :].bitcast(F16)[:, 0:512], ACT.Copy).then_inc(d_OTs, 1)

        def one_hots(v, t, j):
            after(v, d_OT, t - 1)
            for g in range(4):
                col = POS[:, :].rearrange("p (t g) -> p t g", g=4)[:, t, g:g + 1]
                table = IOTAM[:, :] if g % 2 else CN[:, C_IOTA:C_IOTA + P]
                ins = v.tensor_scalar(OH[j][:, g, :], table, col, None, ALU.is_equal)
            ins.then_inc(d_oh, 1)

        def dve_d(v, t, j, p=None):
            jj = (j + 1) % 2
            if in_d(t + 1):
                one_hots(v, t + 1, jj)
            k = t - 1
            if in_d(k):
                split(v, d, k, jj)
            k = t - 2
            if in_d(k):
                v.wait_ge(d.y, k + 1)
                v.scalar_tensor_tensor(YF[j][:, :, :], PS[:, 6 + j, 0:256].rearrange("p (g d) -> p g d", g=2),
                                       1.0 / WSCALE, bcast(row(ROW_NETS + MOD), 1, 2), ALU.mult, ALU.add).then_inc(d_yf, 1)
                v.wait_ge(d_yf, k + 1)
                after(v, d_Z, k - 1)
                v.tensor_copy(YH[j][:, :, :], YF[j][:, :, :]).then_inc(d_yh, 1)
                v.wait_ge(d_yh, k + 1)
                v.tensor_tensor(YL[j][:, :, :], YF[j][:, :, :], YH[j][:, :, :], ALU.subtract).then_inc(d_yl, 1)
            k = t - 3
            if in_d(k):
                v.wait_ge(d_Z, k + 1)
                after(v, out_st[jj], 16 * half_of(k - 2, p, j - 5) + 16)
                for g in range(4):
                    w = WTOK[:, :].rearrange("p (t g) -> p t g", g=4)[:, k, g:g + 1]
                    xk = X[:, :, :, :].rearrange("p (t q) g d -> p t (q g) d", q=2)[:, k, g, :]
                    ins = v.scalar_tensor_tensor(OUT[jj][:, g, :], PS[:, 6 + jj, g * P:(g + 1) * P], w, xk,
                                                 ALU.mult, ALU.add)
                ins.then_inc(d_o, 1)

        def sp_d(sp, t, j, p=None):
            k, jj = t - 3, (j + 1) % 2
            if in_d(k):
                sp.wait_ge(d_o, k + 1)
                sp.dma_start(out[bass.ds(4 * k, 4), :, :].rearrange("g p d -> p g d"), OUT[jj][:, :, :]).then_inc(out_st[jj], 16)

        def run(eng, fn, last, end, done=0, start=FIRST):
            for i in range(done, start):
                fn(eng, i, i % 2)
            with eng.Fori(start // 2, end // 2) as p:
                for j in range(2):
                    fn(eng, p * 2 + j, j)
            for i in range(end, last + 1):
                fn(eng, i, i % 2)

        def run_p(eng, fn, last, end, start=FIRST):
            for i in range(start):
                fn(eng, i, i % 2, None)
            with eng.Fori(start // 2, end // 2) as p:
                for j in range(2):
                    fn(eng, p * 2 + j, j, p)
            for i in range(end, last + 1):
                fn(eng, i, i % 2, None)

        block = ctx.enter_context(nc.Block())

        @block.sync
        def _(sp):
            sp.dma_start(CN[:, :], consts).then_inc(const_ld, 16)
            sp.dma_start(ADJ[:, :], adj).then_inc(const_ld, 16)
            xv = x.rearrange("(q g) p d -> p q g d", g=2)
            sp.dma_start(X[:, 0:FIRST_X, :, :], xv[:, 0:FIRST_X, :, :]).then_inc(x_ld[0], 16)
            sp.dma_start(MT[:, :], mats).then_inc(params_ld, 16)
            sp.dma_start(CL[:, :], cols).then_inc(params_ld, 16)
            sp.dma_start(RW[:, :, :].rearrange("p r d -> p (r d)"),
                         rows.rearrange("(a r) d -> a (r d)", a=1).broadcast_to([P, ROWS * P])).then_inc(rows_ld, 16)
            sp.dma_start(X[:, FIRST_X:PAIRS, :, :], xv[:, FIRST_X:PAIRS, :, :]).then_inc(x_ld[1], 16)

            def raw_load(i, e, k):
                after(sp, prep, i - 1)
                dst = RAW[k][:, :, :].rearrange("p c t -> p (c t)")[:, 0:HIDDEN]
                if k == 0:
                    sp.dma_start(dst, w1[e, :, :]).then_inc(raw_ld[k], 16)
                else:
                    sp.dma_start(dst.rearrange("p (c d) -> p c d", c=CHUNKS),
                                 w2[e, :, :].rearrange("(c p) d -> p c d", p=P)).then_inc(raw_ld[k], 16)

            raw_load(0, 0, 0)
            raw_load(1, 0, 1)
            with sp.Fori(1, NETS) as e:
                for k in range(2):
                    raw_load(e * 2 + k, e, k)
            sp.wait_ge(setup, 1)
            with sp.Fori(0, ZERO_STORES) as q:
                sp.dma_start(sorted_rows[bass.ds(q * (ZERO_ROWS * P), ZERO_ROWS * P), :].rearrange("(p a) d -> p (a d)", p=P),
                             zeros[:, :].bitcast(F16)).then_inc(zero_st, 16)
            run_b(sp, sp_b)
            for j in range(2):
                sp.wait_ge(y_st[j], 16 * ROUTED_TILES // 2)
            run_p(sp, sp_d, LAST_D, MOD_TILES)
            for j in range(2):
                sp.wait_ge(out_st[j], 16 * MOD_TILES // 2)

        @block.gpsimd
        def _(pool):
            pool.memset(wscale[:, :], WSCALE)
            pool.memset(epsc[:, :], EPS)
            for j in range(2):
                pool.memset(KB[j][:, :], 0.0)
                pool.memset(VA[j][:, :, :, WIDTH_A:WIDTH_A + 1], 1.0)
                ins = pool.memset(VC[j][:, :, :, WIDTH_C:WIDTH_C + 1], 1.0)
            ins.then_inc(pool_ready, 1)
            pool.wait_ge(pool_ready, 1)
            pool.wait_ge(const_ld, 32)
            pool.wait_ge(rows_ld, 16)
            for i in range(FIRST):
                pool_a(pool, i, i % 2, True)
            with pool.Fori(FIRST // 2, NETS) as p:
                for j in range(2):
                    chunk_net[0] = p
                    pool_a(pool, p * 2 + j, j, True)
            with pool.Fori(NETS, PAIRS // 2) as p:
                for j in range(2):
                    pool_a(pool, p * 2 + j, j, False)
            for i in range(PAIRS, LAST_A + 1):
                pool_a(pool, i, i % 2, False)

            pool.wait_ge(r_slots, 2)
            pool.wait_ge(zero_st, 16 * ZERO_STORES)
            pool.wait_ge(a_lo, PAIRS)

            def scatter(q, j, p):
                if p is not None:
                    pool.wait_ge(sc_done[j], 64 * p).then_inc(spare, 1)
                pool.tensor_copy(SG[j][:, :, :].bitcast(I32), HL[:, q, :, :, :].rearrange("p g a d -> p g (a d)").bitcast(I32)
                                 ).then_inc(sc_ready, 1)
                pool.tensor_copy(ISG[j][:, :], SL[:, :, :].rearrange("p (q g) k -> p q (g k)", g=2)[:, q, :]).then_inc(sc_ready, 1)
                pool.wait_ge(sc_ready, q * 2 + 2).then_inc(spare, 1)
                for n in range(4):
                    pool.indirect_dma_start(out=sorted_rows[:, :],
                                            out_offset=bass.IndirectOffsetOnAxis(ap=ISG[j][:, n:n + 1], axis=0),
                                            in_=SG[j][:, n // 2, :], in_offset=None).then_inc(sc_done[j], 16)

            for q in range(2):
                scatter(q, q, None)
            with pool.Fori(1, PAIRS // 2) as p:
                for j in range(2):
                    scatter(p * 2 + j, j, p)

            pool.wait_ge(b.ys, SHARED_TILES)
            pool.tensor_tensor(X[:, :, :, :].rearrange("p k g d -> p (k g) d"), X[:, :, :, :].rearrange("p k g d -> p (k g) d"),
                               bcast(row(ROW_NETS + SHARED), 1, GRAPHS), ALU.add).then_inc(pool_ready, 1)
            pool.wait_ge(r_eid, 1)
            pool.memset(KBC[:, :, :], 0.0).then_inc(pool_ready, 1)
            for j in range(2):
                pool.wait_ge(sc_done[j], 64 * PAIRS // 2)
            for j in range(2):
                pool.wait_ge(y_st[j], 16 * ROUTED_TILES // 2)
            run(pool, pool_c, LAST_C, PAIRS, start=FIRST_C)

        @block.scalar
        def _(act):
            act.wait_ge(params_ld, 32)
            act.wait_ge(pool_ready, 1)
            act.preload_act_table_set(EXP_AND_LN)
            run(act, act_a, LAST_A, PAIRS)
            act.wait_ge(r_diff, 1)
            act.activation(WT[:, 1, :], WT[:, 0, :], ACT.Exp).then_inc(r_exp, 1)
            run_b(act, act_b)
            act.preload_act_table_set(EXP_AND_LN)
            act.wait_ge(pool_ready, 3)
            run(act, act_c, LAST_C, PAIRS, start=FIRST_C)
            act.wait_ge(d_wt, 1)
            act.activation(WG, PS[0:GRAPHS, 0, 0:P], ACT.Copy).then_inc(d_wg, 1)
            run(act, act_d, LAST_D, MOD_TILES)

        @block.tensor
        def _(pe):
            pe.wait_ge(const_ld, 32)
            pe.wait_ge(params_ld, 32)
            pe.wait_ge(setup, SETUP)
            run(pe, pe_a, LAST_A, PAIRS)
            pe.wait_ge(r_oh, 1)
            oh = OH12[:, :]
            pe.matmul(PS[:, 3, :], CN[:, C_TRI:C_TRI + P], oh, start=True, stop=True)
            pe.matmul(PS[:, 4, :], CN[:, C_ONE:C_ONE + P], oh, start=True, stop=True).then_inc(r_cnt, 1)
            pe.wait_ge(prep, CHUNK_STEPS)
            pe.wait_ge(a_lo, PAIRS)
            pe.wait_ge(a_h0Ts, PAIRS)
            pe.wait_ge(a_lgs, PAIRS)
            pe.wait_ge(a_x1, PAIRS)
            pe.wait_ge(r_slots, 1)
            run_b(pe, pe_b)
            pe.wait_ge(b.ys, ALL_TILES)
            run(pe, pe_c, LAST_C, PAIRS, start=FIRST_C)
            pe.wait_ge(c_uw, PAIRS + 1)
            pe.wait_ge(c_s2, PAIRS)
            pe.transpose(PS[0:GRAPHS, 0, 0:P], WTOK[:, :], ident).then_inc(d_wt, 1)
            pe.wait_ge(d_rank, 1)
            pe.transpose(PS[:, 1, 0:GRAPHS], PLACE, CN[0:GRAPHS, C_ID:C_ID + GRAPHS]).then_inc(d_pt, 1)
            run(pe, pe_d, LAST_D, MOD_TILES)

        @block.vector
        def _(v):
            one = [0]

            def then(ins):
                one[0] += 1
                ins.then_inc(route, 1)
                v.wait_ge(route, one[0])

            v.memset(zeros[:, :], 0.0).then_inc(setup, 1)
            v.wait_ge(const_ld, 32)
            v.tensor_copy(ident16[:, :], ident).then_inc(setup, 1)
            v.tensor_copy(identb[:, :], ident).then_inc(setup, 1)
            then(v.tensor_copy(ADJF[:, :], ADJ[:, :]))
            v.tensor_scalar(mask0[:, :, :], bcast(ADJF[:, :], 1, 4), 0.0, MASKED, ALU.is_equal, ALU.mult).then_inc(setup, 1)
            v.tensor_scalar(mask1[:, :, :], bcast(ADJF[:, :], 1, 4), 0.0, MASKED, ALU.is_le, ALU.mult).then_inc(setup, 1)
            v.tensor_scalar(IOTAM[:, :], CN[:, C_IOTA:C_IOTA + P], float(SLOTS), None, ALU.subtract).then_inc(setup, 1)
            then(v.tensor_scalar(ADJN[:, :], ADJF[:, :], 0.0, None, ALU.not_equal))
            v.tensor_reduce(has[:, :], ADJN[:, :], AX.X, ALU.max).then_inc(setup, 1)
            v.wait_ge(x_ld[0], 16)
            v.wait_ge(rows_ld, 16)
            v.wait_ge(setup, SETUP)
            v.wait_ge(pool_ready, 1)
            for i in range(FIRST):
                if i == FIRST_X:
                    v.wait_ge(x_ld[1], 16)
                dve_a(v, i, i % 2)
            run(v, dve_a, LAST_A, PAIRS, done=FIRST)

            v.wait_ge(a_lgs, PAIRS)
            rev = CN[:, C_REV:C_REV + 8]
            G64 = GRAPHS

            def pick(logits, best, onehot):
                then(v.tensor_reduce(best, logits, AX.X, ALU.max))
                then(v.tensor_tensor(TMP[:, :, :], logits, bcast(best, 2, 8), ALU.is_equal))
                then(v.tensor_tensor(TMP[:, :, :], TMP[:, :, :], bcast(rev, 1, G64), ALU.mult))
                then(v.tensor_reduce(KEY[:, :], TMP[:, :, :], AX.X, ALU.max))
                then(v.tensor_tensor(onehot, bcast(rev, 1, G64), bcast(KEY[:, :], 2, 8), ALU.is_equal))

            pick(LG[:, :, :], BEST[:, 0, :], OH1[:, :, :])
            then(v.scalar_tensor_tensor(LG[:, :, :], OH1[:, :, :], MASKED, LG[:, :, :], ALU.mult, ALU.add))
            pick(LG[:, :, :], BEST[:, 1, :], OH2[:, :, :])
            v.tensor_tensor(OH12[:, :], OH1[:, :, :].rearrange("p a e -> p (a e)"),
                            OH2[:, :, :].rearrange("p a e -> p (a e)"), ALU.add).then_inc(r_oh, 1)
            v.tensor_tensor(WT[:, 0, :], BEST[:, 1, :], BEST[:, 0, :], ALU.subtract).then_inc(r_diff, 1)
            v.wait_ge(r_exp, 1)
            then(v.tensor_scalar(BEST[:, 0, :], WT[:, 1, :], 1.0, None, ALU.add))
            then(v.reciprocal(WT[:, 0, :], BEST[:, 0, :]))
            then(v.tensor_tensor(WT[:, 1, :], WT[:, 1, :], WT[:, 0, :], ALU.mult))
            v.wait_ge(r_cnt, 1)
            then(v.tensor_copy(LG[:, :, :].rearrange("p a e -> p (a e)"), PS[:, 4, :]))
            for e in range(EXPERTS):
                then(v.tensor_tensor_scan(TMP[:, :, e], LG[:, :, e], zeros[:, 0:G64], 0.0, ALU.add, ALU.add))
            then(v.tensor_copy(CNT[:, 0, :], TMP[:, G64 - 1, :]))
            then(v.tensor_tensor(LG[:, :, :], TMP[:, :, :], LG[:, :, :], ALU.subtract))
            then(v.tensor_tensor(LG[:, :, :], PS[:, 3, :].rearrange("p (a e) -> p a e", e=8), LG[:, :, :], ALU.add))
            then(v.tensor_tensor(TMP[:, :, :].rearrange("p a e -> p (a e)").rearrange("p (e a) -> p e a", e=8),
                                 bcast(CNT[:, 0, :], 2, 64), bcast(CN[:, C_THR:C_THR + 64], 1, 8), ALU.is_gt))
            then(v.tensor_reduce(CNT[:, 1, :], TMP[:, :, :].rearrange("p a e -> p (a e)").rearrange("p (e a) -> p e a", e=8),
                                 AX.X, ALU.add))
            then(v.tensor_tensor_scan(CNT[:, 2, :], CNT[:, 1, :], zeros[:, 0:8], 0.0, ALU.add, ALU.add))
            then(v.tensor_tensor(CNT[:, 3, :], CNT[:, 2, :], CNT[:, 1, :], ALU.subtract))
            then(v.tensor_scalar(CNT[:, 3, :], CNT[:, 3, :], float(TILE), None, ALU.mult))
            then(v.tensor_tensor(LG[:, :, :], LG[:, :, :], bcast(CNT[:, 3, :], 1, G64), ALU.add))
            for k, oh in enumerate((OH1, OH2)):
                then(v.tensor_tensor(TMP[:, :, :], LG[:, :, :], oh[:, :, :], ALU.mult))
                then(v.tensor_reduce(KEY[:, :], TMP[:, :, :], AX.X, ALU.add))
                v.tensor_copy(SL[:, :, k], KEY[:, :]).then_inc(r_slots, 1)
                v.wait_ge(r_slots, k + 1)
            big = WIDE[:, :].rearrange("p (t e) -> p t e", e=8)
            then(v.tensor_tensor(big, bcast(CNT[:, 2, :], 1, ROUTED_TILES),
                                 bcast(CN[:, C_TIX:C_TIX + ROUTED_TILES], 2, 8), ALU.is_le))
            then(v.tensor_reduce(EIDF[:, :], big, AX.X, ALU.add))
            v.tensor_scalar(EID[:, :], EIDF[:, :], float(EXPERTS - 1), None, ALU.min).then_inc(r_eid, 1)

            run_b(v, dve_b)

            v.wait_ge(pool_ready, 2)
            run(v, dve_c, LAST_C, PAIRS, start=FIRST_C)

            v.wait_ge(c_uw, PAIRS)
            v.tensor_scalar(WTOK[:, :], WTOK[:, :], row(ROW_BR)[:, 0:1], None, ALU.add).then_inc(c_uw, 1)
            v.wait_ge(d_wg, 1)
            then(v.tensor_copy(WK, WG))
            for r in range(8):
                then(v.max(TOP[:, :], WK))
                then(v.match_replace(WK, TOP[:, :], WK, TAKEN))
            then(v.tensor_scalar(SEL, WK, TAKEN / 3, None, ALU.is_lt))
            then(v.tensor_scalar(CAND, WG, TOP[:, 7:8], None, ALU.is_equal))
            then(v.tensor_tensor(CAND, CAND, SEL, ALU.mult))
            then(v.scalar_tensor_tensor(CAND, CN[0:GRAPHS, C_IOTA:C_IOTA + P], 1.0, CAND, ALU.add, ALU.mult))
            then(v.tensor_reduce(KMAX[:, :], CAND, AX.X, ALU.max))
            then(v.tensor_scalar(CAND, CAND, KMAX[:, 0:1], None, ALU.is_equal))
            then(v.tensor_tensor(SEL, SEL, CAND, ALU.subtract))
            then(v.tensor_tensor_scan(CAND, SEL, zeros[0:GRAPHS, 0:P], 0.0, ALU.add, ALU.add))
            then(v.scalar_tensor_tensor(CAND, SEL, 1000.0, CAND, ALU.mult, ALU.add))
            v.tensor_scalar(PLACE, CAND, 1001.0, None, ALU.subtract).then_inc(d_rank, 1)
            v.wait_ge(d_pt, 1)
            then(v.tensor_copy(POS[:, :], PS[:, 1, 0:GRAPHS]))
            one_hots(v, 0, 0)
            for t in range(FIRST):
                dve_d(v, t, t % 2)
            with v.Fori(FIRST // 2, MOD_TILES // 2 - 1) as p:
                for j in range(2):
                    dve_d(v, p * 2 + j, j, p)
            for t in range(MOD_TILES - 2, LAST_D + 1):
                dve_d(v, t, t % 2)


def kernel(x, adj, **p):
    import concourse.bacc as bacc
    from concourse.bass_utils import run_bass_kernel_spmd

    def a(name):
        return np.asarray(p[name])

    f32 = np.float32
    net_w1 = np.concatenate([a("L0_ffn_W1p"), a("L0_ffn_W1s")[None], a("L1_ffn_w1")[None]])
    net_w2 = np.concatenate([a("L0_ffn_W2p"), a("L0_ffn_W2s")[None], a("L1_ffn_w2")[None]])
    net_b1 = np.concatenate([a("L0_ffn_b1p"), a("L0_ffn_b1s")[None], a("L1_ffn_b1")[None]])
    net_b2 = np.concatenate([a("L0_ffn_b2p"), a("L0_ffn_b2s")[None], a("L1_ffn_b2")[None]])
    cols = np.concatenate([net_b1.reshape(-1, P), a("L0_gnn_bq")[None], a("L0_gnn_bk")[None],
                           a("L1_gnn_b1")[None]]).T
    rows = np.concatenate([np.stack([a("L0_gnn_bv"), a("L0_gnn_bo"), a("L1_gnn_ln1_g"), a("L1_gnn_ln1_b"),
                                     a("L1_gnn_ln2_g"), a("L1_gnn_ln2_b"), a("L1_gnn_b2"),
                                     a("L1_ffn_wr")[:, 0], np.repeat(a("L1_ffn_br"), P)]), net_b2])
    mats = np.concatenate([a("L0_gnn_wq").T, a("L0_gnn_wk").T, a("L0_gnn_wv").T, a("L0_gnn_wo").T,
                           a("L1_gnn_w_qkv"), a("L1_gnn_w1"), a("L1_gnn_w2"), a("L0_ffn_Wr")], axis=1)
    arrays = {"x": np.asarray(x), "adj": np.asarray(adj), "mats": mats, "cols": cols, "rows": rows,
              "w1": net_w1, "w2": net_w2, "consts": constants()}
    arrays = {k: np.ascontiguousarray(v) for k, v in arrays.items()}
    nc = bacc.Bacc("TRN2", target_bir_lowering=False, num_devices=1)
    aps = [nc.dram_tensor(k, v.shape, mybir.dt.from_np(v.dtype), kind="ExternalInput").ap() for k, v in arrays.items()]
    out = nc.dram_tensor("out", (GRAPHS, P, P), mybir.dt.float32, kind="ExternalOutput").ap()
    names = list(arrays)
    by = dict(zip(names, aps))
    build(nc, by["x"], by["adj"], by["mats"], by["cols"], by["rows"], by["w1"], by["w2"], by["consts"], out)
    r = run_bass_kernel_spmd(nc, [arrays], core_ids=[0])
    return r.results[0]["out"]
```

```python
from contextlib import ExitStack

import numpy as np

import concourse.bass as bass
from concourse import mybir

P = 128
GRAPHS, PAIRS = 64, 32
HIDDEN = 512
CHUNKS = HIDDEN // P
EXPERTS = 8
SHARED, MOD = 8, 9
NETS = 10
TILE = 2 * P
SHARED_TILES = GRAPHS * P // TILE
ROUTED_TILES = 2 * SHARED_TILES + EXPERTS
ALL_TILES = SHARED_TILES + ROUTED_TILES
ROUTED_ROWS = ROUTED_TILES * TILE
HEADS_A, HEADS_C = 4, 8
WIDTH_A, WIDTH_C = P // HEADS_A, P // HEADS_C
KEPT = 63
SLOTS = 64
MOD_TILES = GRAPHS // 4
EPS = 1e-5
MASKED = -1e30
TAKEN = -3e38
WSCALE = 64.0
FIRST = 8

COL_BQ, COL_BK, COL_B1C = NETS * CHUNKS, NETS * CHUNKS + 1, NETS * CHUNKS + 2
COLS = NETS * CHUNKS + 3
(ROW_BV, ROW_BO, ROW_G1, ROW_B1, ROW_G2, ROW_B2, ROW_FB, ROW_WR, ROW_BR) = range(9)
ROW_NETS = 9
ROWS = ROW_NETS + NETS
MAT_Q, MAT_K, MAT_V, MAT_O, MAT_QKV, MAT_F1, MAT_F2, MAT_R = 0, 128, 256, 384, 512, 896, 1024, 1152
MATS = 1160
C_ID, C_TRI, C_ONE, C_IOTA = 0, 128, 256, 384
C_H4, C_H8, C_REV, C_THR, C_TIX = 512, 516, 524, 532, 596
CONSTS = 596 + ROUTED_TILES


def constants():
    c = np.zeros((P, CONSTS), np.float32)
    k = np.arange(P)
    c[:, C_ID:C_ID + P] = np.eye(P)
    c[:, C_TRI:C_TRI + P] = k[:, None] < k[None, :]
    c[:, C_ONE:C_ONE + P] = 1.0
    c[:, C_IOTA:C_IOTA + P] = k
    c[:, C_H4:C_H4 + 4] = k[:, None] // WIDTH_A == np.arange(4)
    c[:, C_H8:C_H8 + 8] = k[:, None] // WIDTH_C == np.arange(8)
    c[:, C_REV:C_REV + 8] = np.arange(8, 0, -1)
    c[:, C_THR:C_THR + 64] = TILE * np.arange(64)
    c[:, C_TIX:C_TIX + ROUTED_TILES] = np.arange(ROUTED_TILES)
    return c


EXP_AND_LN = "natural_log_exp_and_others"


def build(nc, x, adj, mats, cols, rows, w1, w2, consts, out):
    F32, F16, BF16, I32 = mybir.dt.float32, mybir.dt.float16, mybir.dt.bfloat16, mybir.dt.int32
    ACT, ALU, AX = mybir.ActivationFunctionType, mybir.AluOpType, mybir.AxisListType
    ctx = ExitStack()
    with ctx:
        def sb(name, shape, dt=F32):
            return ctx.enter_context(nc.sbuf_tensor(name, shape, dt))

        sems = {}

        def sem(name):
            if name not in sems:
                sems[name] = ctx.enter_context(nc.semaphore(name))
            return sems[name]

        def two(name, shape, dt=F32):
            return [sb(f"{name}{j}", shape, dt) for j in range(2)]

        def after(eng, s, n):
            if isinstance(n, int) and n <= 0:
                return
            eng.wait_ge(s, n)

        sorted_rows = nc.dram_tensor("sorted_rows", [ROUTED_ROWS, 2 * P], F16, kind="Internal").ap()
        results = nc.dram_tensor("results", [ROUTED_ROWS, P], F32, kind="Internal").ap()

        X = sb("X", [P, PAIRS, 2, P])
        HL = sb("HL", [P, PAIRS, 2, 2, P], F16)
        WH = sb("WH", [P, NETS, 2, HIDDEN], F16)
        WL = sb("WL", [P, NETS, 2, HIDDEN], F16)
        MT = sb("MT", [P, MATS])
        CL = sb("CL", [P, COLS])
        RW = sb("RW", [P, ROWS, P])
        CN = sb("CN", [P, CONSTS])
        ADJ = sb("ADJ", [P, P], I32)
        ident16 = sb("ident16", [P, P], F16)
        identb = sb("identb", [P, P], BF16)
        mask0 = sb("mask0", [P, 4, P], BF16)
        mask1 = sb("mask1", [P, 4, P], BF16)
        has = sb("has", [P, 1])
        wscale = sb("wscale", [P, 1])
        zeros = sb("zeros", [P, 512])
        ADJF = sb("ADJF", [P, P])
        ADJN = sb("ADJN", [P, P])

        XN = two("XN", [P, 2, P])
        XNT = sb("XNT", [P, 2, P])
        QT = sb("QT", [P, 2, P])
        KBC = sb("KB", [P, 2, 1024])
        KB = [KBC[:, j, :] for j in range(2)]
        VA = two("VA", [P, 2, HEADS_A, WIDTH_A + 1])
        VC = two("VC", [P, 2, HEADS_C, WIDTH_C + 1])
        MX = sb("MX", [P, 8])
        PR = two("PR", [P, 8, P])
        PT = sb("PT", [P, 8, P])
        RS = sb("RS", [P, 8])
        ON = sb("ON", [P, 2, P])
        OT = sb("OT", [P, 2, P])
        HF = two("HF", [P, 2, P])
        HT = sb("HT", [P, 2, P])
        STATS, MV, ROOT = ([two(name + str(n), [P, 2] + w) for n in range(4)]
                           for name, w in (("STATS", [6]), ("MV", [2]), ("ROOT", [1])))
        epsc = sb("epsc", [P, 1])
        LG = sb("LG", [P, GRAPHS, EXPERTS])
        WT = sb("WT", [P, 2, GRAPHS])
        SL = sb("SL", [P, GRAPHS, 2], I32)
        EID = sb("EID", [P, ROUTED_TILES], I32)
        WTOK = sb("WTOK", [P, GRAPHS])
        POS = sb("POS", [P, GRAPHS])

        XS = two("XS", [P, 2, 2, P], F16)
        XTS = two("XTS", [P, 2, TILE], F16)
        RAW = two("RAW", [P, CHUNKS, TILE])
        HH = two("HH", [P, CHUNKS, TILE], F16)
        HLO = two("HLO", [P, CHUNKS, TILE], F16)
        YS = two("YS", [P, 2, P])
        SG = [t[:, :, :, :].rearrange("p g a d -> p g (a d)") for t in XS]
        ISG = two("ISG", [P, 4], I32)
        PS = ctx.enter_context(nc.psum_tensor("PS", [P, 8, 512], F32))

        PRF = [t[:, :, :].rearrange("p b m -> p (b m)") for t in PR]
        OH1 = PRF[0][:, 0:512].rearrange("p (a e) -> p a e", e=EXPERTS)
        TMP = PRF[0][:, 512:1024].rearrange("p (a e) -> p a e", e=EXPERTS)
        OH2 = PRF[1][:, 0:512].rearrange("p (a e) -> p a e", e=EXPERTS)
        OH12 = PRF[1][:, 512:1024]
        WIDE = PT[:, :, :].rearrange("p b m -> p (b m)")[:, 0:ROUTED_TILES * EXPERTS]
        KEY = sb("KEY", [P, GRAPHS])
        BEST = sb("BEST", [P, 2, GRAPHS])
        CNT = sb("CNT", [P, 4, EXPERTS])
        EIDF = sb("EIDF", [P, ROUTED_TILES])

        ident = CN[:, C_ID:C_ID + P]

        def bcast(ap, axis, n):
            a = ap.unsqueeze(axis)
            shape = list(a.shape)
            shape[axis] = n
            return a.broadcast_to(shape)

        def row(r):
            return RW[:, r, :]

        x_ld = [sem("x_ld0"), sem("x_ld1")]
        const_ld, params_ld, rows_ld = sem("const_ld"), sem("params_ld"), sem("rows_ld")
        raw_ld = [sem("raw_ld0"), sem("raw_ld1")]
        zero_st = sem("zero_st")
        setup = sem("setup")
        pool_ready = sem("pool_ready")
        spare = sem("spare")
        out_st = [sem("out_st0"), sem("out_st1")]
        FIRST_X = 4
        SETUP = 8
        ZERO_ROWS = 4
        ZERO_STORES = ROUTED_ROWS // P // ZERO_ROWS
        CHUNK_STEPS = 2 * NETS

        def live(k, n=PAIRS):
            return not isinstance(k, int) or 0 <= k < n

        def at(stage, eng, i, j, lag, n=PAIRS):
            if live(i - lag, n):
                stage(eng, i - lag, (j + lag) % 2)

        def straight(eng, s, n):
            if isinstance(n, int):
                after(eng, s, n)

        def upto(n, last=PAIRS):
            return min(n, last) if isinstance(n, int) else n

        class Norm:

            def __init__(self, tag, place, src, before=0):
                self.table, self.src, self.before = place, src, before
                self.stats_done, self.aggr_done, self.ln_done, self.root_done = (
                    sem(tag + n) for n in ("_stats", "_aggr", "_ln", "_root"))

            def stats(self, v, k, j, src_ready=None):
                if src_ready is not None:
                    v.wait_ge(src_ready, k + 1).then_inc(spare, 1)
                for g in range(2):
                    ins = v.bn_stats(STATS[self.table][j][:, g, :], self.src(k, g))
                ins.then_inc(self.stats_done, 1)

            def aggregate(self, v, k, j, applied):
                after(v, applied, k - 1)
                v.wait_ge(self.stats_done, k + 1 + self.before).then_inc(spare, 1)
                for g in range(2):
                    ins = v.bn_aggr(MV[self.table][j][:, g, :], STATS[self.table][j][:, g, :])
                ins.then_inc(self.aggr_done, 1)

            def root(self, act, k, j):
                r = ROOT[self.table][j][:, :, 0]
                act.wait_ge(self.aggr_done, k + 1 + self.before)
                act.activation(r, MV[self.table][j][:, :, 1], ACT.Ln, bias=epsc[:, 0:1]).then_inc(self.ln_done, 1)
                act.wait_ge(self.ln_done, k + 1 + self.before)
                act.activation(r, r, ACT.Exp, scale=-0.5).then_inc(self.root_done, 1)

            def apply(self, v, k, j, dst, done, free=()):
                v.wait_ge(self.root_done, k + 1 + self.before)
                for s, m in free:
                    after(v, s, m)
                for g in range(2):
                    ins = v.tensor_scalar(dst(g), self.src(k, g), MV[self.table][j][:, g, 0:1],
                                          ROOT[self.table][j][:, g, :], ALU.subtract, ALU.mult)
                ins.then_inc(done, 1)

        a_xnT, a_T, a_qk, a_v, a_S, a_PT, a_O, a_OT, a_wo, a_h0T, a_lg = (sem("a_" + n) for n in
            "xnT T qk v S PT O OT wo h0T lg".split())
        a_q, a_k, a_exp, a_pt, a_OTs, a_h0Ts = (sem("a_" + n) for n in "q k exp pt OTs h0Ts".split())
        a_xn, a_vs, a_max, a_sub, a_r, a_On, a_x1, a_h0, a_lgs = (sem("a_" + n) for n in
            "xn vs max sub r On x1 h0 lgs".split())
        a_xb, a_hi, a_lo, prep_t, prep_hi, prep = (sem(n) for n in
            "a_xb a_hi a_lo prep_t prep_hi prep".split())
        norm_x = Norm("norm1", 0, lambda k, g: X[:, k, g, :])
        norm_h = Norm("norm2", 1, lambda k, g: X[:, k, g, :])
        LAST_A = PAIRS + 6

        def flat(t):
            return t.rearrange("p a b -> p (a b)")

        def transpose_x(pe, k, j):
            pe.wait_ge(a_xn, k + 1)
            straight(pe, a_xnT, k)
            after(pe, a_h0Ts, k - 4)
            for g in range(2):
                ins = pe.transpose(PS[:, 0, g * P:(g + 1) * P], XN[j][:, g, :], ident)
            ins.then_inc(a_T, 1)

        def queries_keys(pe, k, j):
            pe.wait_ge(a_xnT, k + 1)
            after(pe, a_k, k)
            pe.matmul(PS[:, 1, 0:256], MT[:, MAT_Q:MAT_Q + P], flat(XNT[:, :, :]), start=True, stop=True)
            pe.matmul(PS[:, 1, 256:512], MT[:, MAT_K:MAT_K + P], flat(XNT[:, :, :]), start=True, stop=True).then_inc(a_qk, 1)

        def values(pe, k, j):
            straight(pe, a_vs, k)
            after(pe, a_lgs, k - 3)
            for g in range(2):
                ins = pe.matmul(PS[:, 2, g * P:(g + 1) * P], XNT[:, g, :], MT[:, MAT_V:MAT_V + P],
                                start=True, stop=True)
            ins.then_inc(a_v, 1)

        def scores(pe, k, j):
            pe.wait_ge(a_k, k + 1)
            after(pe, a_sub, k)
            for g in range(2):
                pe.matmul(PS[:, 3 + g, :], QT[:, g, :], KB[j][:, g * 512:(g + 1) * 512], start=True, stop=False)
                ins = pe.matmul(PS[:, 3 + g, :], identb[:, :], mask0[:, :, :].rearrange("p h m -> p (h m)"),
                                start=False, stop=True)
            ins.then_inc(a_S, 1)

        def transpose_probs(pe, k, j):
            pe.wait_ge(a_exp, k + 1)
            after(pe, a_pt, k)
            for b in range(8):
                ins = pe.transpose(PS[:, 5 + b // 4, (b % 4) * P:(b % 4 + 1) * P], PR[j][:, b, :], ident)
            ins.then_inc(a_PT, 1)

        def probs_values(pe, k, j):
            pe.wait_ge(a_pt, k + 1)
            pe.wait_ge(a_vs, k + 1)
            after(pe, a_x1, k)
            for b in range(8):
                ins = pe.matmul(PS[:, 7, 33 * b:33 * b + 33], PT[:, b, :], VA[j][:, b // 4, b % 4, :], start=True, stop=True)
            ins.then_inc(a_O, 1)

        def transpose_attention(pe, k, j):
            pe.wait_ge(a_On, k + 1)
            for g in range(2):
                ins = pe.transpose(PS[:, 7, g * P:(g + 1) * P], ON[:, g, :], ident)
            ins.then_inc(a_OT, 1)

        def project(pe, k, j):
            pe.wait_ge(a_OTs, k + 1)
            for g in range(2):
                ins = pe.matmul(PS[:, 7, g * P:(g + 1) * P], OT[:, g, :], MT[:, MAT_O:MAT_O + P], start=True, stop=True)
            ins.then_inc(a_wo, 1)

        def transpose_h0(pe, k, j):
            pe.wait_ge(a_h0, k + 1)
            after(pe, a_xnT, upto(k + 5))
            straight(pe, a_h0Ts, k)
            for g in range(2):
                ins = pe.transpose(PS[:, 0, g * P:(g + 1) * P], HF[j][:, g, :], ident)
            ins.then_inc(a_h0T, 1)

        def router(pe, k, j):
            pe.wait_ge(a_h0Ts, k + 1)
            after(pe, a_vs, upto(k + 4))
            straight(pe, a_lgs, k)
            for g in range(2):
                ins = pe.matmul(PS[:, 2, 256 + 8 * g:264 + 8 * g], HT[:, g, :], MT[:, MAT_R:MAT_R + 8],
                                start=True, stop=True)
            ins.then_inc(a_lg, 1)

        def pe_a(pe, i, j):
            at(transpose_x, pe, i, j, 3)
            at(probs_values, pe, i, j, 6)
            at(values, pe, i, j, 4)
            at(scores, pe, i, j, 4)
            at(transpose_attention, pe, i, j, 6)
            at(transpose_h0, pe, i, j, 7)
            at(transpose_probs, pe, i, j, 5)
            at(queries_keys, pe, i, j, 3)
            at(project, pe, i, j, 6)
            at(router, pe, i, j, 7)

        def take_xT(act, k, j):
            act.wait_ge(a_T, k + 1)
            after(act, a_v, k)
            act.activation(flat(XNT[:, :, :]), PS[:, 0, 0:256], ACT.Copy).then_inc(a_xnT, 1)

        def take_queries(act, k, j):
            act.wait_ge(a_qk, k + 1)
            after(act, a_S, k)
            act.activation(flat(QT[:, :, :]), PS[:, 1, 0:256], ACT.Identity, bias=CL[:, COL_BQ:COL_BQ + 1]).then_inc(a_q, 1)

        def take_keys(act, k, j):
            act.wait_ge(a_q, k + 1)
            for h in range(HEADS_A):
                rows = slice(h * WIDTH_A, (h + 1) * WIDTH_A)
                ins = act.activation(KB[j][rows, :].rearrange("p (g h m) -> p g h m", g=2, h=HEADS_A)[:, :, h, :],
                                     PS[rows, 1, 256:512].rearrange("p (g m) -> p g m", g=2), ACT.Identity,
                                     bias=CL[rows, COL_BK:COL_BK + 1])
            ins.then_inc(a_k, 1)

        def exponent(act, k, j):
            act.wait_ge(a_sub, k + 1)
            act.activation(flat(PR[j][:, :, :]), flat(PR[j][:, :, :]), ACT.Exp, scale=float(WIDTH_A) ** -0.5).then_inc(a_exp, 1)

        def take_probs(act, k, j):
            act.wait_ge(a_PT, k + 1)
            after(act, a_O, k)
            act.activation(flat(PT[:, :, :]), flat(PS[:, 5:7, :]), ACT.Copy).then_inc(a_pt, 1)

        def take_attention(act, k, j):
            act.wait_ge(a_OT, k + 1)
            act.activation(flat(OT[:, :, :]), PS[:, 7, 0:256], ACT.Copy).then_inc(a_OTs, 1)

        def take_h0T(act, k, j):
            act.wait_ge(a_h0T, k + 1)
            act.activation(flat(HT[:, :, :]), PS[:, 0, 0:256], ACT.Copy).then_inc(a_h0Ts, 1)

        def root_x(act, k, j):
            norm_x.root(act, k, j)

        def root_h(act, k, j):
            norm_h.root(act, k, j)

        def act_a(act, i, j):
            at(take_keys, act, i, j, 4)
            at(take_xT, act, i, j, 3)
            at(root_h, act, i, j, 7)
            at(exponent, act, i, j, 5)
            at(root_x, act, i, j, 1)
            at(take_attention, act, i, j, 6)
            at(take_h0T, act, i, j, 7)
            at(take_probs, act, i, j, 5)
            at(take_queries, act, i, j, 3)

        def stats_x(v, k, j):
            norm_x.stats(v, k, j)

        def aggregate_x(v, k, j):
            norm_x.aggregate(v, k, j, a_xn)

        def normed_x(v, k, j):
            norm_x.apply(v, k, j, lambda g: XN[j][:, g, :], a_xn, [(a_T, k - 1)])

        def take_values(v, k, j):
            v.wait_ge(a_v, k + 1)
            after(v, a_O, k - 1)
            v.tensor_tensor(VA[j][:, :, :, 0:32], PS[:, 2, 0:256].rearrange("p (g h w) -> p g h w", g=2, w=32),
                            bcast(row(ROW_BV).rearrange("p (h w) -> p h w", w=32), 1, 2), ALU.add).then_inc(a_vs, 1)

        def less_maximum(v, k, j):
            s = PS[:, 3:5, :].rearrange("p g (h m) -> p (g h) m", h=4)
            v.wait_ge(a_S, k + 1)
            v.tensor_reduce(MX[:, :], s, AX.X, ALU.max).then_inc(a_max, 1)
            v.wait_ge(a_max, k + 1)
            after(v, a_PT, k - 1)
            v.tensor_tensor(PR[j][:, :, :], s, bcast(MX[:, :], 2, P), ALU.subtract).then_inc(a_sub, 1)

        def sums(v, k, j):
            v.wait_ge(a_O, k + 1)
            v.reciprocal(RS[:, :], PS[:, 7, 0:264].rearrange("p (b w) -> p b w", w=33)[:, :, 32]).then_inc(a_r, 1)

        def normalise(v, k, j):
            v.wait_ge(a_r, k + 1)
            v.scalar_tensor_tensor(ON[:, :, :].rearrange("p g (h w) -> p (g h) w", w=32),
                                   PS[:, 7, 0:264].rearrange("p (b w) -> p b w", w=33)[:, :, 0:32],
                                   has[:, 0:1], bcast(RS[:, :], 2, 32), ALU.mult, ALU.mult).then_inc(a_On, 1)

        def residual(v, k, j):
            v.wait_ge(a_wo, k + 1)
            v.wait_ge(a_xb, k + 1)
            v.tensor_tensor(X[:, k, :, :], PS[:, 7, 0:256].rearrange("p (g d) -> p g d", g=2), X[:, k, :, :],
                            ALU.add).then_inc(a_x1, 1)

        def stats_h(v, k, j):
            norm_h.stats(v, k, j, a_x1)

        def aggregate_h(v, k, j):
            norm_h.aggregate(v, k, j, a_h0)

        def normed_h(v, k, j):
            norm_h.apply(v, k, j, lambda g: HF[j][:, g, :], a_h0, [(a_h0T, k - 1), (a_lo, k - 1)])

        def take_logits(v, k, j):
            v.wait_ge(a_lg, k + 1)
            v.tensor_copy(LG[:, :, :].rearrange("p (q g) e -> p q (g e)", g=2)[:, k, :], PS[:, 2, 256:272]).then_inc(a_lgs, 1)

        def dve_a(v, i, j):
            at(normalise, v, i, j, 6)
            at(aggregate_x, v, i, j, 1)
            at(normed_h, v, i, j, 7)
            at(take_values, v, i, j, 4)
            at(less_maximum, v, i, j, 4)
            at(residual, v, i, j, 6)
            at(take_logits, v, i, j, 7)
            at(stats_h, v, i, j, 6)
            at(aggregate_h, v, i, j, 6)
            at(sums, v, i, j, 5)
            at(stats_x, v, i, j, 0)
            at(normed_x, v, i, j, 1)

        def add_bias(pool, k, j):
            pool.wait_ge(a_xn, k + 1)
            pool.tensor_tensor(X[:, k, :, :], X[:, k, :, :], bcast(row(ROW_BO), 1, 2), ALU.add).then_inc(a_xb, 1)

        def high_h0(pool, k, j):
            pool.wait_ge(a_h0, k + 1).then_inc(spare, 1)
            pool.tensor_copy(HL[:, k, :, 0, :], HF[j][:, :, :]).then_inc(a_hi, 1)

        def low_h0(pool, k, j):
            pool.wait_ge(a_hi, k + 1)
            pool.tensor_tensor(HL[:, k, :, 1, :], HF[j][:, :, :], HL[:, k, :, 0, :], ALU.subtract).then_inc(a_lo, 1)

        def split_weights(pool, i, j):
            e = i // 2 if isinstance(i, int) else chunk_net[0]
            raw = RAW[j][:, :, :].rearrange("p c t -> p (c t)")[:, 0:HIDDEN]
            tmp = RAW[j][:, :, :].rearrange("p c t -> p (c t)")[:, HIDDEN:2 * HIDDEN]
            pool.wait_ge(raw_ld[j], 16 * (e + 1))
            pool.tensor_tensor(tmp, raw, wscale[:, 0:1].broadcast_to([P, HIDDEN]), ALU.mult).then_inc(prep_t, 1)
            pool.wait_ge(prep_t, i + 1).then_inc(spare, 1)
            pool.tensor_copy(WH[:, e, j, :], tmp).then_inc(prep_hi, 1)
            pool.wait_ge(prep_hi, i + 1)
            pool.tensor_tensor(WL[:, e, j, :], tmp, WH[:, e, j, :], ALU.subtract).then_inc(prep, 1)

        def pool_a(pool, i, j, chunk):
            at(high_h0, pool, i, j, 7)
            at(add_bias, pool, i, j, 2)
            at(low_h0, pool, i, j, 7)
            if chunk:
                split_weights(pool, i, j)

        chunk_net = [None]

        class Net:
            def __init__(self, tag):
                (self.T, self.xT, self.h, self.g, self.hi, self.lo, self.y, self.ys) = (
                    sem(tag + n) for n in ("_T", "_xT", "_h", "_g", "_hi", "_lo", "_y", "_ys"))

        b, d = Net("b"), Net("d")

        def net_weights(e):
            return [(WH[:, e, layer, :], WL[:, e, layer, :]) for layer in range(2)]

        def first_layer(pe, s, k, j, w1):
            pe.wait_ge(s.xT, k + 1)
            for half in range(2):
                after(pe, s.g, 2 * k + half - 3)
                for c in (2 * half, 2 * half + 1):
                    dst = PS[:, 2 + 2 * j + half, (c % 2) * TILE:(c % 2 + 1) * TILE]
                    wh, wl = (w[:, c * P:(c + 1) * P] for w in w1)
                    pe.matmul(dst, wh, XTS[j][:, 0, :], start=True, stop=False)
                    pe.matmul(dst, wh, XTS[j][:, 1, :], start=False, stop=False)
                    ins = pe.matmul(dst, wl, XTS[j][:, 0, :], start=False, stop=True)
                ins.then_inc(s.h, 1)

        def gelu(act, s, k, j, bias, func):
            for half in range(2):
                act.wait_ge(s.h, 2 * k + half + 1)
                after(act, s.lo, 2 * k + half - 3)
                for c in (2 * half, 2 * half + 1):
                    ins = act.activation(RAW[j][:, c, :], PS[:, 2 + 2 * j + half, (c % 2) * TILE:(c % 2 + 1) * TILE],
                                         func, bias=bias[:, c:c + 1],
                                         scale=1.0 / WSCALE)
                ins.then_inc(s.g, 1)

        def split(v, s, k, j):
            for half in range(2):
                cs = slice(2 * half, 2 * half + 2)
                v.wait_ge(s.g, 2 * k + half + 1)
                if half == 0:
                    after(v, s.y, k - 1)
                v.tensor_copy(HH[j][:, cs, :], RAW[j][:, cs, :]).then_inc(s.hi, 1)
                v.wait_ge(s.hi, 2 * k + half + 1)
                v.tensor_tensor(HLO[j][:, cs, :], RAW[j][:, cs, :], HH[j][:, cs, :], ALU.subtract).then_inc(s.lo, 1)

        def second_layer(pe, s, k, j, w2, bank_free):
            pe.wait_ge(s.lo, 2 * k + 2)
            after(pe, *bank_free)
            for t in range(2):
                for c in range(CHUNKS):
                    hh, hl = (h[j][:, c, t * P:(t + 1) * P] for h in (HH, HLO))
                    wh, wl = (w[:, c * P:(c + 1) * P] for w in w2)
                    dst = PS[:, 6 + j, t * P:(t + 1) * P]
                    pe.matmul(dst, hh, wh, start=c == 0, stop=False)
                    pe.matmul(dst, hh, wl, start=False, stop=False)
                    ins = pe.matmul(dst, hl, wh, start=False, stop=c == CHUNKS - 1)
            ins.then_inc(s.y, 1)

        xs_ld = [sem("xs_ld0"), sem("xs_ld1")]
        y_st = [sem("y_st0"), sem("y_st1")]
        sc_ready = sem("sc_ready")
        sc_done = [sem("sc_done0"), sem("sc_done1")]
        route = sem("route")
        r_slots, r_eid, r_cnt, r_diff, r_exp = (sem("r_" + n) for n in "slots eid cnt diff exp".split())
        r_oh = sem("r_oh")
        LAST_B = ALL_TILES + 1
        SPLIT_B = SHARED_TILES + 4

        def in_b(k):
            return not isinstance(k, int) or 0 <= k < ALL_TILES

        def is_shared(k, shared_loop):
            return k < SHARED_TILES if isinstance(k, int) else shared_loop

        b1_in, w2_in = sem("b1_in"), sem("w2_in")
        W2T = [t.bitcast(F16).rearrange("p (a w) -> p a w", a=4)[:, 0:2, :] for t in PRF]
        B1T = two("B1T", [P, CHUNKS])
        B2T = [t[:, 0, :] for t in XN]

        def net_of(eng, n):
            return eng.value_load(EID[0:1, bass.ds(n, 1)], min_val=0, max_val=EXPERTS - 1)

        def pool_b(pool, n, j):
            e, k = net_of(pool, n), n + SHARED_TILES
            first = isinstance(n, int) and n < 2
            if not first:
                pool.wait_ge(b.g, 2 * k - 2).then_inc(spare, 1)
            pool.tensor_copy(B1T[j][:, :], CL[:, 0:NETS * CHUNKS].rearrange("p (e c) -> p e c", e=NETS)[:, e, :]
                             ).then_inc(b1_in, 1)
            if not first:
                pool.wait_ge(b.y, k - 1).then_inc(spare, 1)
            pool.tensor_copy(W2T[j][:, 0, :].bitcast(I32), WH[:, e, 1, :].bitcast(I32))
            pool.tensor_copy(W2T[j][:, 1, :].bitcast(I32), WL[:, e, 1, :].bitcast(I32))
            if not first:
                pool.wait_ge(b.ys, k - 1).then_inc(spare, 1)
            pool.tensor_copy(B2T[j], RW[:, ROW_NETS:ROWS, :][:, e, :]).then_inc(w2_in, 1)

        def pe_b(pe, t, j, shared):
            e = SHARED
            if in_b(t - 1) and not is_shared(t - 1, shared):
                pe.wait_ge(r_eid, 1)
                e = net_of(pe, t - 1 - SHARED_TILES)
            if in_b(t):
                after(pe, b.xT, t - 1)
                if is_shared(t, shared):
                    src = HL[:, t, :, :, :]
                else:
                    src = XS[j]
                    pe.wait_ge(xs_ld[j], 8 * (t - j - SHARED_TILES) + 16)
                dst = PS[:, j, :].bitcast(F16)
                for hl in range(2):
                    for g in range(2):
                        ins = pe.transpose(dst[:, hl * TILE + g * P:hl * TILE + (g + 1) * P], src[:, g, hl, :], ident16[:, :])
                ins.then_inc(b.T, 1)
            k = t - 1
            if in_b(k):
                first_layer(pe, b, k, (j + 1) % 2, net_weights(e)[0])
            k = t - 2
            if in_b(k):
                if not is_shared(k, shared):
                    pe.wait_ge(w2_in, k - SHARED_TILES + 1)
                    w2 = W2T[j][:, 0, :], W2T[j][:, 1, :]
                else:
                    w2 = net_weights(SHARED)[1]
                second_layer(pe, b, k, j, w2, (b.ys, k - 1))

        def act_b(act, t, j, shared):
            if in_b(t):
                act.wait_ge(b.T, t + 1)
                after(act, b.h, 2 * t - 2)
                act.activation(XTS[j][:, :, :].rearrange("p a b -> p (a b)"), PS[:, j, :].bitcast(F16)[:, 0:2 * TILE],
                               ACT.Copy).then_inc(b.xT, 1)
            k = t - 1
            if in_b(k):
                if is_shared(k, shared):
                    bias = CL[:, SHARED * CHUNKS:(SHARED + 1) * CHUNKS]
                else:
                    bias = B1T[(j + 1) % 2]
                    act.wait_ge(b1_in, k - SHARED_TILES + 1)
                gelu(act, b, k, (j + 1) % 2, bias, ACT.Gelu)

        def stage_rows(v, q, j):
            after(v, sc_done[j], 32 * (q - j))
            v.tensor_copy(SG[j][:, :, :], HL[:, q, :, :, :].rearrange("p g a d -> p g (a d)"))
            v.tensor_copy(ISG[j][:, :], SL[:, :, :].rearrange("p (q g) k -> p q (g k)", g=2)[:, q, :]).then_inc(sc_ready, 1)

        def dve_b(v, t, j, shared):
            if is_shared(t, shared) and not (isinstance(t, int) and t < 2):
                stage_rows(v, t, j)
            k = t - 1
            if in_b(k):
                split(v, b, k, (j + 1) % 2)
            k = t - 2
            if in_b(k):
                v.wait_ge(b.y, k + 1)
                if is_shared(k, shared):
                    v.scalar_tensor_tensor(X[:, k, :, :], PS[:, 6 + j, 0:256].rearrange("p (g d) -> p g d", g=2),
                                           1.0 / WSCALE, X[:, k, :, :], ALU.mult, ALU.add).then_inc(b.ys, 1)
                    return
                v.wait_ge(w2_in, k - SHARED_TILES + 1)
                after(v, y_st[j], 8 * (k - 2 - j - SHARED_TILES) + 16)
                v.scalar_tensor_tensor(YS[j][:, :, :], PS[:, 6 + j, 0:256].rearrange("p (g d) -> p g d", g=2),
                                       1.0 / WSCALE, bcast(B2T[j], 1, 2), ALU.mult, ALU.add).then_inc(b.ys, 1)

        def sp_b(sp, t, j, shared):
            k = t + 2
            if in_b(k) and not is_shared(k, shared):
                if isinstance(k, int) and k == SHARED_TILES:
                    for s in sc_done:
                        sp.wait_ge(s, 64 * PAIRS // 2)
                if not isinstance(k, int) or k - 2 >= SHARED_TILES:
                    sp.wait_ge(b.T, k - 1)
                r = (k - SHARED_TILES) * TILE
                sp.dma_start(XS[j][:, :, :, :].rearrange("p g a d -> p g (a d)"),
                             sorted_rows[bass.ds(r, TILE), :].rearrange("(g p) d -> p g d", p=P)).then_inc(xs_ld[j], 16)
            k = t - 2
            if in_b(k) and not is_shared(k, shared):
                sp.wait_ge(b.ys, k + 1)
                sp.dma_start(results[bass.ds((k - SHARED_TILES) * TILE, TILE), :].rearrange("(g p) d -> p g d", p=P),
                             YS[j][:, :, :]).then_inc(y_st[j], 16)

        def run_b(eng, fn):
            for t in range(FIRST):
                fn(eng, t, t % 2, True)
            with eng.Fori(FIRST // 2, SHARED_TILES // 2 - 1) as p:
                for j in range(2):
                    fn(eng, p * 2 + j, j, True)
            for t in range(SHARED_TILES - 2, SPLIT_B):
                fn(eng, t, t % 2, True)
            with eng.Fori(SPLIT_B // 4, ALL_TILES // 4 - 1) as p:
                for j in range(4):
                    fn(eng, p * 4 + j, j % 2, False)
            for t in range(ALL_TILES - 4, LAST_B + 1):
                fn(eng, t, t % 2, False)

        def both(name):
            return [sem(name + "0"), sem(name + "1")]

        c_T, c_aT, c_qk, c_v, c_w1, c_F = (sem("c_" + n) for n in "T aT qk v w1 F".split())
        c_zT, c_zk, c_aTs, c_q, c_k, c_relu = (sem("c_" + n) for n in "zT zk aTs q k relu".split())
        c_S, c_PT, c_O, c_exp, c_pt, c_max, c_sub, c_r, c_On = (both("c_" + n) for n in "S PT O exp pt max sub r On".split())
        c_x2b, c_x2, c_z, c_vs, c_s1, c_n1, c_s2, c_n2, c_x3, c_u, c_uw, c_xu = (
            sem("c_" + n) for n in "x2b x2 z vs s1 n1 s2 n2 x3 u uw xu".split())
        c_ag, c_a, c_ab, c_cg, c_c, c_hi, c_lo, c_um = (sem("c_" + n) for n in "ag a ab cg c hi lo um".split())
        g_idx, c_xb = sem("g_idx"), sem("c_xb")
        g_ld = both("g_ld")
        LAST_C = PAIRS + 8
        FIRST_C = 10
        GY = two("GY", [P, 4, P])
        S1 = [RAW[1][:, j, :].rearrange("p (g d) -> p g d", g=2) for j in range(2)]
        A1 = two("A1", [P, 2, P])
        AB = two("AB", [P, 2, P])
        S2 = [RAW[1][:, 2 + j, :].rearrange("p (g d) -> p g d", g=2) for j in range(2)]
        C2 = two("C2", [P, 2, P])
        PTC = [PT, RAW[0][:, :, :].rearrange("p c (a m) -> p (c a) m", a=2)]
        MXC = [MX, sb("MX1", [P, 8])]
        RSC = [RS, sb("RS1", [P, 8])]
        HR = sb("HR", [P, 2 * P])
        UM = YS[0]
        AT = HT
        Z = HL[:, :, :, :, :].rearrange("p k g a d -> p (k g a d)").bitcast(F32).rearrange("p (k g d) -> p k g d", g=2, d=P)

        norm_z = Norm("norm1", 0, lambda k, g: X[:, k, g, :], PAIRS)
        norm_u = Norm("norm2", 1, lambda k, g: X[:, k, g, :], PAIRS)
        norm_1 = [Norm("norm3", 2, lambda k, g, j=j: S1[j][:, g, :]) for j in range(2)]
        norm_2 = [Norm("norm4", 3, lambda k, g, j=j: S2[j][:, g, :]) for j in range(2)]

        def of_graph(stage, g):
            return lambda eng, k, j: stage(eng, k, j, g)

        def transpose_z(pe, k, j):
            pe.wait_ge(c_z, k + 1)
            straight(pe, c_zT, k)
            after(pe, c_relu, k - 3)
            for g in range(2):
                ins = pe.transpose(PS[:, 0, g * P:(g + 1) * P], XN[j][:, g, :], ident)
            ins.then_inc(c_T, 1)

        def queries_keys_c(pe, k, j):
            pe.wait_ge(c_zT, k + 1)
            after(pe, c_k, k)
            pe.matmul(PS[:, 1, 0:256], MT[:, MAT_QKV:MAT_QKV + P], flat(XNT[:, :, :]), start=True, stop=True)
            pe.matmul(PS[:, 1, 256:512], MT[:, MAT_QKV + P:MAT_QKV + 2 * P], flat(XNT[:, :, :]),
                      start=True, stop=True).then_inc(c_qk, 1)

        def values_c(pe, k, j):
            straight(pe, c_vs, k)
            after(pe, c_s2, k - 2)
            for g in range(2):
                ins = pe.matmul(PS[:, 2, g * P:(g + 1) * P], XNT[:, g, :], MT[:, MAT_QKV + 2 * P:MAT_QKV + 3 * P],
                                start=True, stop=True)
            ins.then_inc(c_v, 1)

        def scores_c(pe, k, j, g):
            if g == 0:
                pe.wait_ge(c_k, k + 1)
                after(pe, c_sub[1], k)
            else:
                pe.wait_ge(c_sub[0], k + 1)
            for h in range(2):
                pe.matmul(PS[:, 3 + h, :], QT[:, g, :], KB[g][:, h * 512:(h + 1) * 512], start=True, stop=False)
                ins = pe.matmul(PS[:, 3 + h, :], identb[:, :], mask1[:, :, :].rearrange("p h m -> p (h m)"),
                                start=False, stop=True)
            ins.then_inc(c_S[g], 1)

        def transpose_probs_c(pe, k, j, g):
            pe.wait_ge(c_exp[g], k + 1)
            after(pe, c_pt[1 - g], k + g)
            for h in range(8):
                ins = pe.transpose(PS[:, 5 + h // 4, (h % 4) * P:(h % 4 + 1) * P], PR[g][:, h, :], ident)
            ins.then_inc(c_PT[g], 1)

        def probs_values_c(pe, k, j, g):
            pe.wait_ge(c_pt[g], k + 1)
            if g == 0:
                pe.wait_ge(c_vs, k + 1)
            after(pe, c_On[1 - g], k + g)
            for h in range(8):
                ins = pe.matmul(PS[:, 7, 17 * h:17 * h + 17], PTC[g][:, h, :], VC[j][:, g, h, :], start=True, stop=True)
            ins.then_inc(c_O[g], 1)

        def transpose_a(pe, k, j):
            pe.wait_ge(c_a, k + 1)
            after(pe, c_zT, upto(k + 4))
            straight(pe, c_relu, k)
            for g in range(2):
                ins = pe.transpose(PS[:, 0, g * P:(g + 1) * P], A1[j][:, g, :], ident)
            ins.then_inc(c_aT, 1)

        def hidden_c(pe, k, j):
            pe.wait_ge(c_aTs, k + 1)
            pe.matmul(PS[:, 0, 0:256], MT[:, MAT_F1:MAT_F1 + P], flat(AT[:, :, :]), start=True, stop=True).then_inc(c_w1, 1)

        def network_out_c(pe, k, j):
            pe.wait_ge(c_relu, k + 1)
            after(pe, c_vs, upto(k + 3))
            straight(pe, c_s2, k)
            for g in range(2):
                ins = pe.matmul(PS[:, 2, g * P:(g + 1) * P], HR[:, g * P:(g + 1) * P], MT[:, MAT_F2:MAT_F2 + P],
                                start=True, stop=True)
            ins.then_inc(c_F, 1)

        def pe_c(pe, i, j):
            at(queries_keys_c, pe, i, j, 3)
            at(of_graph(probs_values_c, 1), pe, i, j, 5)
            at(hidden_c, pe, i, j, 6)
            at(of_graph(scores_c, 1), pe, i, j, 4)
            at(network_out_c, pe, i, j, 6)
            at(of_graph(transpose_probs_c, 0), pe, i, j, 4)
            at(transpose_z, pe, i, j, 2)
            at(values_c, pe, i, j, 3)
            at(of_graph(scores_c, 0), pe, i, j, 3)
            at(of_graph(probs_values_c, 0), pe, i, j, 4)
            at(of_graph(transpose_probs_c, 1), pe, i, j, 4)
            at(transpose_a, pe, i, j, 5)

        def take_zT(act, k, j):
            act.wait_ge(c_T, k + 1)
            after(act, c_v, k)
            act.activation(flat(XNT[:, :, :]), PS[:, 0, 0:256], ACT.Copy).then_inc(c_zT, 1)

        def keep_z(act, k, j):
            act.wait_ge(c_z, k + 1).then_inc(spare, 1)
            act.activation(Z[:, k, :, :], XN[j][:, :, :], ACT.Copy).then_inc(c_zk, 1)

        def take_queries_c(act, k, j):
            act.wait_ge(c_qk, k + 1)
            after(act, c_S[1], k)
            act.activation(flat(QT[:, :, :]), PS[:, 1, 0:256], ACT.Copy).then_inc(c_q, 1)

        def take_keys_c(act, k, j):
            act.wait_ge(c_q, k + 1)
            for h in range(HEADS_C):
                rows = slice(h // 2 * 32, h // 2 * 32 + 32)
                ins = act.activation(KBC[rows, :, :].rearrange("p g (h m) -> p g h m", h=HEADS_C)[:, :, h, :],
                                     PS[rows, 1, 256:512].rearrange("p (g m) -> p g m", g=2), ACT.Copy,
                                     scale=CN[rows, C_H8 + h:C_H8 + h + 1])
            ins.then_inc(c_k, 1)

        def take_values_c(act, k, j):
            act.wait_ge(c_v, k + 1)
            after(act, c_O[1], k - 1)
            act.activation(VC[j][:, :, :, 0:16], PS[:, 2, 0:256].rearrange("p (g h w) -> p g h w", g=2, w=16),
                           ACT.Copy).then_inc(c_vs, 1)

        def exponent_c(act, k, j, g):
            act.wait_ge(c_sub[g], k + 1)
            act.activation(flat(PR[g][:, :, :]), flat(PR[g][:, :, :]), ACT.Exp, scale=float(WIDTH_C) ** -0.5).then_inc(c_exp[g], 1)

        def take_probs_c(act, k, j, g):
            act.wait_ge(c_PT[g], k + 1)
            after(act, c_O[g], k)
            act.activation(flat(PTC[g][:, :, :]), flat(PS[:, 5:7, :]), ACT.Copy).then_inc(c_pt[g], 1)

        def take_aT(act, k, j):
            act.wait_ge(c_aT, k + 1)
            act.activation(flat(AT[:, :, :]), PS[:, 0, 0:256], ACT.Copy).then_inc(c_aTs, 1)

        def relu_c(act, k, j):
            act.wait_ge(c_w1, k + 1)
            act.activation(HR[:, :], PS[:, 0, 0:256], ACT.Relu, bias=CL[:, COL_B1C:COL_B1C + 1]).then_inc(c_relu, 1)

        def root_z(act, k, j):
            norm_z.root(act, k, j)

        def root_u(act, k, j):
            norm_u.root(act, k, j)

        def root_1(act, k, j):
            norm_1[j].root(act, k, j)

        def root_2(act, k, j):
            norm_2[j].root(act, k, j)

        def act_c(act, i, j):
            at(take_aT, act, i, j, 6)
            at(relu_c, act, i, j, 6)
            at(root_z, act, i, j, 1)
            at(of_graph(exponent_c, 0), act, i, j, 4)
            at(root_u, act, i, j, 7)
            at(take_queries_c, act, i, j, 3)
            at(take_keys_c, act, i, j, 3)
            at(take_zT, act, i, j, 2)
            at(keep_z, act, i, j, 2)
            at(of_graph(take_probs_c, 0), act, i, j, 4)
            at(root_1, act, i, j, 5)
            at(of_graph(exponent_c, 1), act, i, j, 4)
            at(root_2, act, i, j, 6)
            at(of_graph(take_probs_c, 1), act, i, j, 4)
            at(take_values_c, act, i, j, 3)

        def expert_added(v, k, j, choice, before, done):
            for g in range(2):
                w = WT[:, choice, :].rearrange("p (q g) -> p q g", g=2)[:, k, g:g + 1]
                ins = v.scalar_tensor_tensor(X[:, k, g, :], GY[j][:, 2 * g + choice, :], w, X[:, k, g, :],
                                             ALU.mult, ALU.add)
            ins.then_inc(done, 1)

        def first_expert(v, k, j):
            v.wait_ge(c_xb, k + 1)
            v.wait_ge(g_ld[j], 32 * (k - j) + 64)
            expert_added(v, k, j, 0, None, c_x2b)

        def second_expert(v, k, j):
            v.wait_ge(c_x2b, k + 1)
            expert_added(v, k, j, 1, c_x2b, c_x2)

        def stats_z(v, k, j):
            norm_z.stats(v, k, j, c_x2)

        def aggregate_z(v, k, j):
            norm_z.aggregate(v, k, j, c_z)

        def normed_z(v, k, j):
            norm_z.apply(v, k, j, lambda g: XN[j][:, g, :], c_z, [(c_T, k - 1), (c_zk, k - 1)])

        def maximum_c(v, k, j, g):
            v.wait_ge(c_S[g], k + 1)
            v.tensor_reduce(MXC[g][:, :], PS[:, 3:5, :].rearrange("p g (h m) -> p (g h) m", h=4), AX.X,
                            ALU.max).then_inc(c_max[g], 1)

        def less_maximum_c(v, k, j, g):
            v.wait_ge(c_max[g], k + 1)
            after(v, c_PT[g], k)
            v.tensor_tensor(PR[g][:, :, :], PS[:, 3:5, :].rearrange("p g (h m) -> p (g h) m", h=4),
                            bcast(MXC[g][:, :], 2, P), ALU.subtract).then_inc(c_sub[g], 1)

        def sums_c(v, k, j, g):
            v.wait_ge(c_O[g], k + 1)
            v.reciprocal(RSC[g][:, :], PS[:, 7, 0:136].rearrange("p (h w) -> p h w", w=17)[:, :, 16]).then_inc(c_r[g], 1)

        def normalise_c(v, k, j, g):
            v.wait_ge(c_r[g], k + 1)
            v.tensor_tensor(ON[:, g, :].rearrange("p (h w) -> p h w", w=16),
                            PS[:, 7, 0:136].rearrange("p (h w) -> p h w", w=17)[:, :, 0:16],
                            bcast(RSC[g][:, :], 2, 16), ALU.mult).then_inc(c_On[g], 1)

        def attention_residual(v, k, j):
            v.wait_ge(c_On[1], k + 1)
            v.wait_ge(c_zk, k + 1)
            v.tensor_tensor(S1[j][:, :, :], Z[:, k, :, :], ON[:, :, :], ALU.add).then_inc(c_s1, 1)

        def stats_1(v, k, j):
            norm_1[j].stats(v, k, j, c_s1)

        def aggregate_1(v, k, j):
            norm_1[j].aggregate(v, k, j, c_n1)

        def normed_1(v, k, j):
            norm_1[j].apply(v, k, j, lambda g: A1[j][:, g, :], c_n1, [(c_aT, k - 1), (c_ab, k - 1)])

        def network_residual(v, k, j):
            v.wait_ge(c_F, k + 1)
            v.wait_ge(c_ab, k + 1)
            v.tensor_tensor(S2[j][:, :, :], PS[:, 2, 0:256].rearrange("p (g d) -> p g d", g=2), AB[j][:, :, :],
                            ALU.add).then_inc(c_s2, 1)

        def stats_2(v, k, j):
            norm_2[j].stats(v, k, j, c_s2)

        def aggregate_2(v, k, j):
            norm_2[j].aggregate(v, k, j, c_n2)

        def normed_2(v, k, j):
            norm_2[j].apply(v, k, j, lambda g: C2[j][:, g, :], c_n2, [(c_x3, k - 1)])

        def layer_added(v, k, j):
            v.wait_ge(c_c, k + 1)
            v.tensor_tensor(X[:, k, :, :], X[:, k, :, :], C2[j][:, :, :], ALU.add).then_inc(c_x3, 1)

        def stats_u(v, k, j):
            norm_u.stats(v, k, j, c_x3)

        def aggregate_u(v, k, j):
            norm_u.aggregate(v, k, j, c_u)

        def normed_u(v, k, j):
            norm_u.apply(v, k, j, lambda g: HF[j][:, g, :], c_u, [(c_lo, k - 1), (c_um, k - 1)])

        def u_added(v, k, j):
            v.wait_ge(c_u, k + 1)
            v.tensor_tensor(X[:, k, :, :], X[:, k, :, :], HF[j][:, :, :], ALU.add).then_inc(c_xu, 1)

        def token_weights(v, k, j):
            v.wait_ge(c_um, k + 1)
            v.tensor_reduce(WTOK[:, :].rearrange("p (q g) -> p q g", g=2)[:, k, :], UM[:, :, :], AX.X,
                            ALU.add).then_inc(c_uw, 1)

        def dve_c(v, i, j):
            at(of_graph(normalise_c, 0), v, i, j, 5)
            at(of_graph(less_maximum_c, 0), v, i, j, 4)
            at(token_weights, v, i, j, 9)
            at(of_graph(sums_c, 1), v, i, j, 5)
            at(layer_added, v, i, j, 7)
            at(of_graph(normalise_c, 1), v, i, j, 5)
            at(stats_u, v, i, j, 7)
            at(attention_residual, v, i, j, 5)
            at(aggregate_u, v, i, j, 7)
            at(normed_z, v, i, j, 1)
            at(stats_1, v, i, j, 5)
            at(of_graph(maximum_c, 1), v, i, j, 4)
            at(network_residual, v, i, j, 6)
            at(of_graph(less_maximum_c, 1), v, i, j, 4)
            at(first_expert, v, i, j, 0)
            at(aggregate_1, v, i, j, 5)
            at(stats_2, v, i, j, 6)
            at(second_expert, v, i, j, 0)
            at(normed_u, v, i, j, 7)
            at(normed_1, v, i, j, 5)
            at(stats_z, v, i, j, 0)
            at(aggregate_2, v, i, j, 6)
            at(of_graph(maximum_c, 0), v, i, j, 3)
            at(normed_2, v, i, j, 6)
            at(of_graph(sums_c, 0), v, i, j, 4)
            at(aggregate_z, v, i, j, 0)
            at(u_added, v, i, j, 7)

        def shared_bias(pool, k, j):
            if isinstance(k, int) and k == 0:
                pool.wait_ge(b.ys, SHARED_TILES)
            pool.tensor_tensor(X[:, k, :, :], X[:, k, :, :], bcast(row(ROW_NETS + SHARED), 1, 2), ALU.add).then_inc(c_xb, 1)

        def gather(pool, k, j):
            if not isinstance(k, int) or k > 1:
                pool.wait_ge(c_x2, k - 1).then_inc(spare, 1)
            pool.tensor_copy(ISG[j][:, :], SL[:, :, :].rearrange("p (q g) k -> p q (g k)", g=2)[:, k, :]).then_inc(g_idx, 1)
            pool.wait_ge(g_idx, k + 1).then_inc(spare, 1)
            for q in range(4):
                pool.indirect_dma_start(out=GY[j][:, q, :], out_offset=None, in_=results[:, :],
                                        in_offset=bass.IndirectOffsetOnAxis(ap=ISG[j][:, q:q + 1], axis=0)).then_inc(g_ld[j], 16)

        def affine(pool, t, k, ready, half, done, gain, bias):
            pool.wait_ge(ready, k + 1)
            pool.tensor_tensor(t[:, :, :], t[:, :, :], bcast(row(gain), 1, 2), ALU.mult).then_inc(half, 1)
            pool.wait_ge(half, k + 1)
            pool.tensor_tensor(t[:, :, :], t[:, :, :], bcast(row(bias), 1, 2), ALU.add).then_inc(done, 1)

        def affine_1(pool, k, j):
            affine(pool, A1[j], k, c_n1, c_ag, c_a, ROW_G1, ROW_B1)

        def affine_2(pool, k, j):
            affine(pool, C2[j], k, c_n2, c_cg, c_c, ROW_G2, ROW_B2)

        def with_output_bias(pool, k, j):
            pool.wait_ge(c_a, k + 1)
            after(pool, c_s2, k - 1)
            pool.tensor_tensor(AB[j][:, :, :], A1[j][:, :, :], bcast(row(ROW_FB), 1, 2), ALU.add).then_inc(c_ab, 1)

        def weighted_u(pool, k, j):
            pool.wait_ge(c_u, k + 1)
            after(pool, c_uw, k)
            pool.tensor_tensor(UM[:, :, :], HF[j][:, :, :], bcast(row(ROW_WR), 1, 2), ALU.mult).then_inc(c_um, 1)

        def high_u(pool, k, j):
            pool.wait_ge(c_u, k + 1).then_inc(spare, 1)
            pool.tensor_copy(HL[:, k, :, 0, :], HF[j][:, :, :]).then_inc(c_hi, 1)

        def low_u(pool, k, j):
            pool.wait_ge(c_hi, k + 1)
            pool.tensor_tensor(HL[:, k, :, 1, :], HF[j][:, :, :], HL[:, k, :, 0, :], ALU.subtract).then_inc(c_lo, 1)

        def pool_c(pool, i, j):
            at(shared_bias, pool, i, j, 0)
            at(gather, pool, i, j, 0)
            at(weighted_u, pool, i, j, 8)
            at(low_u, pool, i, j, 8)
            at(high_u, pool, i, j, 7)
            at(affine_1, pool, i, j, 5)
            at(affine_2, pool, i, j, 6)
            at(with_output_bias, pool, i, j, 5)

        d_oh, d_OT, d_OTs, d_yh, d_yf, d_yl, d_Z, d_o = (sem("d_" + n) for n in "oh OT OTs yh yf yl Z o".split())
        d_setup = sem("d_setup")
        PR16 = [t.bitcast(F16) for t in PRF]
        OH = [PR16[m % 2][:, o:o + 512].rearrange("p (g s) -> p g s", g=4) for m, o in enumerate((0, 0, 1536, 1536))]
        OHT = [t[:, 512:1024].rearrange("p (g s) -> p g s", g=4) for t in PR16]
        YH = [t[:, 1024:1280].rearrange("p (g d) -> p g d", g=2) for t in PR16]
        YL = [t[:, 1280:1536].rearrange("p (g d) -> p g d", g=2) for t in PR16]
        OUT = GY
        YF = A1
        IOTAS = sb("IOTAS", [P, 2, 2, P])
        WG, WK, SEL, CAND, PLACE = (KB[0][0:GRAPHS, n * P:(n + 1) * P] for n in range(5))
        TOP = sb("TOP", [GRAPHS, 8])
        KMAX = sb("KMAX", [GRAPHS, 1])

        def in_d(k):
            return not isinstance(k, int) or 0 <= k < MOD_TILES

        def u_parts(t, g, hl):
            return HL[:, :, :, :, :].rearrange("p (t q) g a d -> p t (q g) a d", q=2)[:, t, g, hl, :]

        def pe_d(pe, t, m):
            j = m % 2
            if in_d(t):
                if isinstance(t, int) and t == 0:
                    pe.wait_ge(c_lo, PAIRS)
                pe.wait_ge(d_oh, t + 1)
                after(pe, d_OTs, t - 1)
                for hl in range(2):
                    for g in range(4):
                        o = g % 2 * SLOTS
                        ins = pe.matmul(PS[:, j, hl * TILE + g * SLOTS:hl * TILE + (g + 1) * SLOTS], u_parts(t, g, hl),
                                        OH[m][:, g, o:o + SLOTS], start=True, stop=True)
                ins.then_inc(d.T, 1)
            k, jj = t - 1, (j + 1) % 2
            if in_d(k):
                first_layer(pe, d, k, jj, net_weights(MOD)[0])
                dst = PS[:, jj, :].bitcast(F16)
                for g in range(4):
                    ins = pe.transpose(dst[:, g * P:(g + 1) * P], OH[(m + 3) % 4][:, g, :], ident16[:, :])
                ins.then_inc(d_OT, 1)
            k = t - 3
            if in_d(k):
                pe.wait_ge(d_yl, k + 1)
                pe.wait_ge(d_OTs, k + 1)
                for g in range(4):
                    dst = PS[:, 6 + jj, g * P:(g + 1) * P]
                    pe.matmul(dst, OHT[jj][:, g, :], YH[jj][:, g // 2, :], start=True, stop=False)
                    ins = pe.matmul(dst, OHT[jj][:, g, :], YL[jj][:, g // 2, :], start=False, stop=True)
                ins.then_inc(d_Z, 1)
            k = t - 2
            if in_d(k):
                second_layer(pe, d, k, j, net_weights(MOD)[1], (d_o, k - 1))

        def act_d(act, t, m):
            j, jj = m % 2, (m + 1) % 2
            if in_d(t):
                act.wait_ge(d.T, t + 1)
                after(act, d.h, 2 * t - 2)
                act.activation(flat(XTS[j][:, :, :]), PS[:, j, :], ACT.Copy).then_inc(d.xT, 1)
            k = t - 1
            if in_d(k):
                gelu(act, d, k, jj, CL[:, MOD * CHUNKS:(MOD + 1) * CHUNKS], ACT.Gelu_apprx_tanh)
                act.wait_ge(d_OT, k + 1)
                after(act, d_Z, k - 1)
                act.activation(flat(OHT[jj][:, :, :]), PS[:, jj, :].bitcast(F16)[:, 0:512], ACT.Copy).then_inc(d_OTs, 1)

        def one_hots(v, t, m):
            after(v, d_OT, t - 3)
            places = bcast(POS[:, :].rearrange("p (t g) -> p t g", g=4)[:, t, :], 2, P)
            v.tensor_tensor(OH[m], IOTAS[:, :, :, :].rearrange("p h a m -> p (h a) m"), places,
                            ALU.is_equal).then_inc(d_oh, 1)

        def high_y(pool, k, j):
            pool.wait_ge(d_yf, k + 1).then_inc(spare, 1)
            if not isinstance(k, int) or k > 1:
                pool.wait_ge(d_Z, k - 1).then_inc(spare, 1)
            pool.tensor_copy(YH[j][:, :, :], YF[j][:, :, :]).then_inc(d_yh, 1)

        def low_y(pool, k, j):
            pool.wait_ge(d_yh, k + 1)
            pool.tensor_tensor(YL[j][:, :, :], YF[j][:, :, :], YH[j][:, :, :], ALU.subtract).then_inc(d_yl, 1)

        def pool_d(pool, t, m):
            j = m % 2
            at(high_y, pool, t, j, 2, MOD_TILES)
            at(low_y, pool, t, j, 2, MOD_TILES)

        def dve_d(v, s, m):
            j, jj = m % 2, (m + 1) % 2
            k = s - 6
            if in_d(k):
                v.wait_ge(d_Z, k + 1)
                after(v, out_st[j], 8 * (k - 2 - j) + 16)
                for g in range(4):
                    w = WTOK[:, :].rearrange("p (t g) -> p t g", g=4)[:, k, g:g + 1]
                    xk = X[:, :, :, :].rearrange("p (t q) g d -> p t (q g) d", q=2)[:, k, g, :]
                    ins = v.scalar_tensor_tensor(OUT[j][:, g, :], PS[:, 6 + j, g * P:(g + 1) * P], w, xk,
                                                 ALU.mult, ALU.add)
                ins.then_inc(d_o, 1)
            if in_d(s):
                one_hots(v, s, m)
            k = s - 3
            if in_d(k):
                split(v, d, k, jj)
            k = s - 4
            if in_d(k):
                v.wait_ge(d.y, k + 1)
                after(v, d_yl, k - 1)
                v.scalar_tensor_tensor(YF[j][:, :, :], PS[:, 6 + j, 0:256].rearrange("p (g d) -> p g d", g=2),
                                       1.0 / WSCALE, bcast(row(ROW_NETS + MOD), 1, 2), ALU.mult, ALU.add).then_inc(d_yf, 1)

        def sp_d(sp, t, m):
            k, j = t - 4, m % 2
            if in_d(k):
                sp.wait_ge(d_o, k + 1)
                sp.dma_start(out[bass.ds(4 * k, 4), :, :].rearrange("g p d -> p g d"), OUT[j][:, :, :]).then_inc(out_st[j], 16)

        def run(eng, fn, last, end, done=0, start=FIRST):
            for i in range(done, start):
                fn(eng, i, i % 2)
            with eng.Fori(start // 2, end // 2) as p:
                for j in range(2):
                    fn(eng, p * 2 + j, j)
            for i in range(end, last + 1):
                fn(eng, i, i % 2)

        def run_d(eng, fn, last):
            for t in range(FIRST):
                fn(eng, t, t % 4)
            with eng.Fori(FIRST // 4, MOD_TILES // 4) as p:
                for m in range(4):
                    fn(eng, p * 4 + m, m)
            for t in range(MOD_TILES, last + 1):
                fn(eng, t, t % 4)

        block = ctx.enter_context(nc.Block())

        @block.sync
        def _(sp):
            sp.dma_start(CN[:, :], consts).then_inc(const_ld, 16)
            sp.dma_start(ADJ[:, :], adj).then_inc(const_ld, 16)
            xv = x.rearrange("(q g) p d -> p q g d", g=2)
            sp.dma_start(X[:, 0:FIRST_X, :, :], xv[:, 0:FIRST_X, :, :]).then_inc(x_ld[0], 16)
            sp.dma_start(MT[:, :], mats).then_inc(params_ld, 16)
            sp.dma_start(CL[:, :], cols).then_inc(params_ld, 16)
            sp.dma_start(RW[:, :, :].rearrange("p r d -> p (r d)"),
                         rows.rearrange("(a r) d -> a (r d)", a=1).broadcast_to([P, ROWS * P])).then_inc(rows_ld, 16)
            sp.dma_start(X[:, FIRST_X:PAIRS, :, :], xv[:, FIRST_X:PAIRS, :, :]).then_inc(x_ld[1], 16)

            def raw_load(i, e, k):
                after(sp, prep, i - 1)
                dst = RAW[k][:, :, :].rearrange("p c t -> p (c t)")[:, 0:HIDDEN]
                if k == 0:
                    sp.dma_start(dst, w1[e, :, :]).then_inc(raw_ld[k], 16)
                else:
                    sp.dma_start(dst.rearrange("p (c d) -> p c d", c=CHUNKS),
                                 w2[e, :, :].rearrange("(c p) d -> p c d", p=P)).then_inc(raw_ld[k], 16)

            raw_load(0, 0, 0)
            raw_load(1, 0, 1)
            with sp.Fori(1, NETS) as e:
                for k in range(2):
                    raw_load(e * 2 + k, e, k)
            sp.wait_ge(setup, 1)
            with sp.Fori(0, ZERO_STORES) as q:
                sp.dma_start(sorted_rows[bass.ds(q * (ZERO_ROWS * P), ZERO_ROWS * P), :].rearrange("(p a) d -> p (a d)", p=P),
                             zeros[:, :].bitcast(F16)).then_inc(zero_st, 16)
            run_b(sp, sp_b)
            for j in range(2):
                sp.wait_ge(y_st[j], 16 * ROUTED_TILES // 2)
            run_d(sp, sp_d, MOD_TILES + 3)
            for j in range(2):
                sp.wait_ge(out_st[j], 16 * MOD_TILES // 2)

        @block.gpsimd
        def _(pool):
            pool.memset(wscale[:, :], WSCALE)
            pool.memset(epsc[:, :], EPS)
            for j in range(2):
                pool.memset(KB[j][:, :], 0.0)
                pool.memset(VA[j][:, :, :, WIDTH_A:WIDTH_A + 1], 1.0)
                ins = pool.memset(VC[j][:, :, :, WIDTH_C:WIDTH_C + 1], 1.0)
            ins.then_inc(pool_ready, 1)
            pool.wait_ge(pool_ready, 1)
            pool.wait_ge(const_ld, 32)
            pool.wait_ge(rows_ld, 16)
            for i in range(FIRST):
                pool_a(pool, i, i % 2, True)
            with pool.Fori(FIRST // 2, NETS) as p:
                for j in range(2):
                    chunk_net[0] = p
                    pool_a(pool, p * 2 + j, j, True)
            with pool.Fori(NETS, PAIRS // 2) as p:
                for j in range(2):
                    pool_a(pool, p * 2 + j, j, False)
            for i in range(PAIRS, LAST_A + 1):
                pool_a(pool, i, i % 2, False)

            pool.wait_ge(zero_st, 16 * ZERO_STORES)
            pool.wait_ge(a_lo, PAIRS)

            def scatter(pool, q, j):
                pool.wait_ge(sc_ready, q + 1).then_inc(spare, 1)
                for n in range(4):
                    pool.indirect_dma_start(out=sorted_rows[:, :],
                                            out_offset=bass.IndirectOffsetOnAxis(ap=ISG[j][:, n:n + 1], axis=0),
                                            in_=SG[j][:, n // 2, :], in_offset=None).then_inc(sc_done[j], 16)

            pool.wait_ge(a_S, PAIRS)
            pool.memset(KBC[:, :, :], 0.0).then_inc(pool_ready, 1)
            run(pool, scatter, PAIRS - 1, PAIRS, start=0)
            pool.wait_ge(r_eid, 1)
            run(pool, pool_b, ROUTED_TILES - 1, ROUTED_TILES, start=2)
            for j in range(2):
                pool.wait_ge(y_st[j], 16 * ROUTED_TILES // 2)
            run(pool, pool_c, LAST_C, PAIRS, start=FIRST_C)
            run_d(pool, pool_d, MOD_TILES + 1)

        @block.scalar
        def _(act):
            act.wait_ge(params_ld, 32)
            act.wait_ge(pool_ready, 1)
            act.preload_act_table_set(EXP_AND_LN)
            run(act, act_a, LAST_A, PAIRS)
            act.wait_ge(r_diff, 1)
            act.activation(WT[:, 1, :], WT[:, 0, :], ACT.Exp).then_inc(r_exp, 1)
            run_b(act, act_b)
            act.preload_act_table_set(EXP_AND_LN)
            act.wait_ge(pool_ready, 2)
            run(act, act_c, LAST_C, PAIRS, start=FIRST_C)
            act.wait_ge(d_setup, 1)
            act.activation(WG, PS[0:GRAPHS, 0, 0:P], ACT.Copy).then_inc(d_setup, 1)
            run_d(act, act_d, MOD_TILES)

        @block.tensor
        def _(pe):
            pe.wait_ge(const_ld, 32)
            pe.wait_ge(params_ld, 32)
            pe.wait_ge(setup, SETUP)
            run(pe, pe_a, LAST_A, PAIRS)
            pe.wait_ge(r_oh, 1)
            oh = OH12[:, :]
            pe.matmul(PS[:, 4, :], CN[:, C_ONE:C_ONE + P], oh, start=True, stop=True).then_inc(r_cnt, 1)
            pe.matmul(PS[:, 3, :], CN[:, C_TRI:C_TRI + P], oh, start=True, stop=True).then_inc(r_cnt, 1)
            pe.wait_ge(prep, CHUNK_STEPS)
            pe.wait_ge(a_lo, PAIRS)
            pe.wait_ge(a_h0Ts, PAIRS)
            pe.wait_ge(a_lgs, PAIRS)
            pe.wait_ge(a_x1, PAIRS)
            pe.wait_ge(r_slots, 1)
            run_b(pe, pe_b)
            pe.wait_ge(b.ys, ALL_TILES)
            run(pe, pe_c, LAST_C, PAIRS, start=FIRST_C)
            pe.wait_ge(c_uw, PAIRS + 1)
            pe.wait_ge(c_s2, PAIRS)
            pe.transpose(PS[0:GRAPHS, 0, 0:P], WTOK[:, :], ident).then_inc(d_setup, 1)
            pe.wait_ge(d_setup, 3)
            pe.transpose(PS[:, 1, 0:GRAPHS], PLACE, CN[0:GRAPHS, C_ID:C_ID + GRAPHS]).then_inc(d_setup, 1)
            run_d(pe, pe_d, MOD_TILES + 2)

        @block.vector
        def _(v):
            one = [0]

            def then(ins):
                one[0] += 1
                ins.then_inc(route, 1)
                v.wait_ge(route, one[0])

            v.memset(zeros[:, :], 0.0).then_inc(setup, 1)
            v.wait_ge(const_ld, 32)
            v.tensor_copy(ident16[:, :], ident).then_inc(setup, 1)
            v.tensor_copy(identb[:, :], ident).then_inc(setup, 1)
            then(v.tensor_copy(ADJF[:, :], ADJ[:, :]))
            v.tensor_scalar(mask0[:, :, :], bcast(ADJF[:, :], 1, 4), 0.0, MASKED, ALU.is_equal, ALU.mult).then_inc(setup, 1)
            v.tensor_scalar(mask1[:, :, :], bcast(ADJF[:, :], 1, 4), 0.0, MASKED, ALU.is_le, ALU.mult).then_inc(setup, 1)
            v.tensor_copy(IOTAS[:, :, 0, :], bcast(CN[:, C_IOTA:C_IOTA + P], 1, 2)).then_inc(setup, 1)
            v.tensor_scalar(IOTAS[:, :, 1, :], bcast(CN[:, C_IOTA:C_IOTA + P], 1, 2), float(SLOTS), None, ALU.subtract).then_inc(setup, 1)
            then(v.tensor_scalar(ADJN[:, :], ADJF[:, :], 0.0, None, ALU.not_equal))
            v.tensor_reduce(has[:, :], ADJN[:, :], AX.X, ALU.max).then_inc(setup, 1)
            v.wait_ge(x_ld[0], 16)
            v.wait_ge(rows_ld, 16)
            v.wait_ge(setup, SETUP)
            v.wait_ge(pool_ready, 1)
            for i in range(FIRST):
                if i == FIRST_X:
                    v.wait_ge(x_ld[1], 16)
                dve_a(v, i, i % 2)
            run(v, dve_a, LAST_A, PAIRS, done=FIRST)

            v.wait_ge(a_lgs, PAIRS)
            rev = CN[:, C_REV:C_REV + 8]
            G64 = GRAPHS

            def pick(logits, best, onehot):
                then(v.tensor_reduce(best, logits, AX.X, ALU.max))
                then(v.tensor_tensor(TMP[:, :, :], logits, bcast(best, 2, 8), ALU.is_equal))
                then(v.tensor_tensor(TMP[:, :, :], TMP[:, :, :], bcast(rev, 1, G64), ALU.mult))
                then(v.tensor_reduce(KEY[:, :], TMP[:, :, :], AX.X, ALU.max))
                then(v.tensor_tensor(onehot, bcast(rev, 1, G64), bcast(KEY[:, :], 2, 8), ALU.is_equal))

            pick(LG[:, :, :], BEST[:, 0, :], OH1[:, :, :])
            then(v.scalar_tensor_tensor(LG[:, :, :], OH1[:, :, :], MASKED, LG[:, :, :], ALU.mult, ALU.add))
            pick(LG[:, :, :], BEST[:, 1, :], OH2[:, :, :])
            v.tensor_tensor(OH12[:, :], OH1[:, :, :].rearrange("p a e -> p (a e)"),
                            OH2[:, :, :].rearrange("p a e -> p (a e)"), ALU.add).then_inc(r_oh, 1)
            v.tensor_tensor(WT[:, 0, :], BEST[:, 1, :], BEST[:, 0, :], ALU.subtract).then_inc(r_diff, 1)
            v.wait_ge(r_exp, 1)
            then(v.tensor_scalar(BEST[:, 0, :], WT[:, 1, :], 1.0, None, ALU.add))
            then(v.reciprocal(WT[:, 0, :], BEST[:, 0, :]))
            then(v.tensor_tensor(WT[:, 1, :], WT[:, 1, :], WT[:, 0, :], ALU.mult))
            v.wait_ge(r_cnt, 1)
            then(v.tensor_copy(LG[:, :, :].rearrange("p a e -> p (a e)"), PS[:, 4, :]))
            for e in range(EXPERTS):
                then(v.tensor_tensor_scan(TMP[:, :, e], LG[:, :, e], zeros[:, 0:G64], 0.0, ALU.add, ALU.add))
            then(v.tensor_copy(CNT[:, 0, :], TMP[:, G64 - 1, :]))
            then(v.tensor_tensor(LG[:, :, :], TMP[:, :, :], LG[:, :, :], ALU.subtract))
            v.wait_ge(r_cnt, 2)
            then(v.tensor_tensor(LG[:, :, :], PS[:, 3, :].rearrange("p (a e) -> p a e", e=8), LG[:, :, :], ALU.add))
            then(v.tensor_tensor(TMP[:, :, :].rearrange("p a e -> p (a e)").rearrange("p (e a) -> p e a", e=8),
                                 bcast(CNT[:, 0, :], 2, 64), bcast(CN[:, C_THR:C_THR + 64], 1, 8), ALU.is_gt))
            then(v.tensor_reduce(CNT[:, 1, :], TMP[:, :, :].rearrange("p a e -> p (a e)").rearrange("p (e a) -> p e a", e=8),
                                 AX.X, ALU.add))
            then(v.tensor_tensor_scan(CNT[:, 2, :], CNT[:, 1, :], zeros[:, 0:8], 0.0, ALU.add, ALU.add))
            then(v.tensor_tensor(CNT[:, 3, :], CNT[:, 2, :], CNT[:, 1, :], ALU.subtract))
            then(v.tensor_scalar(CNT[:, 3, :], CNT[:, 3, :], float(TILE), None, ALU.mult))
            then(v.tensor_tensor(LG[:, :, :], LG[:, :, :], bcast(CNT[:, 3, :], 1, G64), ALU.add))
            for k, oh in enumerate((OH1, OH2)):
                then(v.tensor_tensor(TMP[:, :, :], LG[:, :, :], oh[:, :, :], ALU.mult))
                then(v.tensor_reduce(KEY[:, :], TMP[:, :, :], AX.X, ALU.add))
                v.tensor_copy(SL[:, :, k], KEY[:, :]).then_inc(r_slots, 1)
                v.wait_ge(r_slots, k + 1)
            v.wait_ge(a_lo, PAIRS)
            for q in range(2):
                stage_rows(v, q, q)
            big = WIDE[:, :].rearrange("p (t e) -> p t e", e=8)
            then(v.tensor_tensor(big, bcast(CNT[:, 2, :], 1, ROUTED_TILES),
                                 bcast(CN[:, C_TIX:C_TIX + ROUTED_TILES], 2, 8), ALU.is_le))
            then(v.tensor_reduce(EIDF[:, :], big, AX.X, ALU.add))
            v.tensor_scalar(EID[:, :], EIDF[:, :], float(EXPERTS - 1), None, ALU.min).then_inc(r_eid, 1)
            run_b(v, dve_b)

            run(v, dve_c, LAST_C, PAIRS, start=FIRST_C)

            v.wait_ge(c_uw, PAIRS)
            v.tensor_scalar(WTOK[:, :], WTOK[:, :], row(ROW_BR)[:, 0:1], None, ALU.add).then_inc(c_uw, 1)
            v.wait_ge(d_setup, 2)
            then(v.tensor_copy(WK, WG))
            for r in range(8):
                then(v.max(TOP[:, :], WK))
                then(v.match_replace(WK, TOP[:, :], WK, TAKEN))
            then(v.tensor_scalar(SEL, WK, TAKEN / 3, None, ALU.is_lt))
            then(v.tensor_scalar(CAND, WG, TOP[:, 7:8], None, ALU.is_equal))
            then(v.tensor_tensor(CAND, CAND, SEL, ALU.mult))
            then(v.scalar_tensor_tensor(CAND, CN[0:GRAPHS, C_IOTA:C_IOTA + P], 1.0, CAND, ALU.add, ALU.mult))
            then(v.tensor_reduce(KMAX[:, :], CAND, AX.X, ALU.max))
            then(v.tensor_scalar(CAND, CAND, KMAX[:, 0:1], None, ALU.is_equal))
            then(v.tensor_tensor(SEL, SEL, CAND, ALU.subtract))
            then(v.tensor_tensor_scan(CAND, SEL, zeros[0:GRAPHS, 0:P], 0.0, ALU.add, ALU.add))
            then(v.scalar_tensor_tensor(CAND, SEL, 1000.0, CAND, ALU.mult, ALU.add))
            v.tensor_scalar(PLACE, CAND, 1001.0, None, ALU.subtract).then_inc(d_setup, 1)
            v.wait_ge(d_setup, 4)
            then(v.tensor_copy(POS[:, :], PS[:, 1, 0:GRAPHS]))
            run_d(v, dve_d, MOD_TILES + 5)


def kernel(x, adj, **p):
    import concourse.bacc as bacc
    from concourse.bass_utils import run_bass_kernel_spmd

    def a(name):
        return np.asarray(p[name])

    f32 = np.float32
    net_w1 = np.concatenate([a("L0_ffn_W1p"), a("L0_ffn_W1s")[None], a("L1_ffn_w1")[None]])
    net_w2 = np.concatenate([a("L0_ffn_W2p"), a("L0_ffn_W2s")[None], a("L1_ffn_w2")[None]])
    net_b1 = np.concatenate([a("L0_ffn_b1p"), a("L0_ffn_b1s")[None], a("L1_ffn_b1")[None]])
    net_b2 = np.concatenate([a("L0_ffn_b2p"), a("L0_ffn_b2s")[None], a("L1_ffn_b2")[None]])
    cols = np.concatenate([net_b1.reshape(-1, P), a("L0_gnn_bq")[None], a("L0_gnn_bk")[None],
                           a("L1_gnn_b1")[None]]).T
    rows = np.concatenate([np.stack([a("L0_gnn_bv"), a("L0_gnn_bo"), a("L1_gnn_ln1_g"), a("L1_gnn_ln1_b"),
                                     a("L1_gnn_ln2_g"), a("L1_gnn_ln2_b"), a("L1_gnn_b2"),
                                     a("L1_ffn_wr")[:, 0], np.repeat(a("L1_ffn_br"), P)]), net_b2])
    mats = np.concatenate([a("L0_gnn_wq").T, a("L0_gnn_wk").T, a("L0_gnn_wv").T, a("L0_gnn_wo").T,
                           a("L1_gnn_w_qkv"), a("L1_gnn_w1"), a("L1_gnn_w2"), a("L0_ffn_Wr")], axis=1)
    arrays = {"x": np.asarray(x), "adj": np.asarray(adj), "mats": mats, "cols": cols, "rows": rows,
              "w1": net_w1, "w2": net_w2, "consts": constants()}
    arrays = {k: np.ascontiguousarray(v) for k, v in arrays.items()}
    nc = bacc.Bacc("TRN2", target_bir_lowering=False, num_devices=1)
    aps = [nc.dram_tensor(k, v.shape, mybir.dt.from_np(v.dtype), kind="ExternalInput").ap() for k, v in arrays.items()]
    out = nc.dram_tensor("out", (GRAPHS, P, P), mybir.dt.float32, kind="ExternalOutput").ap()
    names = list(arrays)
    by = dict(zip(names, aps))
    build(nc, by["x"], by["adj"], by["mats"], by["cols"], by["rows"], by["w1"], by["w2"], by["consts"], out)
    r = run_bass_kernel_spmd(nc, [arrays], core_ids=[0])
    return r.results[0]["out"]
```
